# Optimizing a Trainium2 kernel written in Bass

```python
import numpy as np
import jax
import jax.numpy as jnp

def _softmax(x, axis=-1):
    return jax.nn.softmax(x, axis=axis)

def _gelu(x):
    return jax.nn.gelu(x, approximate=True)

def _silu(x):
    return jax.nn.silu(x)

def _sigmoid(x):
    return jax.nn.sigmoid(x)

def _layernorm(x, axis=-1, eps=1e-05):
    m = jnp.mean(x, axis=axis, keepdims=True)
    v = jnp.var(x, axis=axis, keepdims=True)
    return (x - m) / jnp.sqrt(v + eps)

def _scatter_add(tgt, idx, src, axis=0):
    return tgt.at[idx].add(src)

def _segment_sum(src, seg, n):
    return jax.ops.segment_sum(src, seg, n)
kernel_name = 'mk_decoder_postln_d2_seqx_r8_95f4d5'

def setup_inputs(seed: int=0):
    np.random.seed(seed)
    _w = jnp.asarray

    def _rec_inputs():
        import jax
        import jax.numpy as jnp
        _rk = jax.random.key(seed)
        x = -0.0002928 + 1 * jax.random.normal(jax.random.fold_in(_rk, 1), (8, 256, 128), jnp.float32)
        _lenS = 256 - jax.random.randint(jax.random.fold_in(_rk, 7), (8,), 0, max(1, 256 // 4) + 1, jnp.int32)
        _lenS2 = 256 - jax.random.randint(jax.random.fold_in(_rk, 8), (8,), 0, max(1, 256 // 4) + 1, jnp.int32)
        _ctx_1024P = jax.random.normal(jax.random.fold_in(_rk, 11), (8, 16, 128), jnp.float32)
        _ctx_1024c = jax.random.dirichlet(jax.random.fold_in(_rk, 511), 0.3 * jnp.ones((16,), jnp.float32), (8, 256))
        _ctx_1024t = jnp.einsum('bsk,bkd->bsd', _ctx_1024c, _ctx_1024P)
        _ctx_1024t = _ctx_1024t * jax.lax.rsqrt(jnp.mean(jnp.square(_ctx_1024t)) + 1e-12) * 0.953939
        ctx_1024 = -1.39393e-06 + 0.999914 * (_ctx_1024t + 0.3 * jax.random.normal(jax.random.fold_in(_rk, 611), (8, 256, 128), jnp.float32))
        return (x, ctx_1024)
    x, ctx_1024 = _rec_inputs()

    def _L0_attn_setup():
        import jax, jax.numpy as jnp
        import numpy as np
        D_MODEL = 128
        EXPAND = 2
        HEADDIM = 64
        D_STATE = 128
        D_CONV = 4
        D_INNER = EXPAND * D_MODEL
        NHEADS = D_INNER // HEADDIM
        CONV_DIM = D_INNER + 2 * D_STATE
        EPS = 1e-05

        def _causal_depthwise_conv(u, w, b):
            B, L, C = u.shape
            up = jnp.pad(u, ((0, 0), (D_CONV - 1, 0), (0, 0)))
            y = b
            for k in range(D_CONV):
                y = y + up[:, k:k + L, :] * w[:, k]
            return y

        def _rms(v):
            return v * jax.lax.rsqrt(jnp.mean(v * v, axis=-1, keepdims=True) + EPS)
        key = jax.random.key(seed)
        ks = jax.random.split(key, 8)
        d_in_proj = 2 * D_INNER + 2 * D_STATE + NHEADS
        x = jax.random.normal(ks[0], (2, 256, D_MODEL), jnp.float32)
        W_in = jax.random.normal(ks[1], (D_MODEL, d_in_proj), jnp.float32) * D_MODEL ** (-0.5)
        conv_w = jax.random.normal(ks[2], (CONV_DIM, D_CONV), jnp.float32) * 0.2
        conv_b = jnp.zeros((CONV_DIM,), jnp.float32)
        dt = jnp.exp(jax.random.uniform(ks[3], (NHEADS,), jnp.float32, minval=np.log(0.001), maxval=np.log(0.1)))
        dt_bias = dt + jnp.log(-jnp.expm1(-dt))
        A_log = jnp.log(jax.random.uniform(ks[4], (NHEADS,), jnp.float32, minval=1.0, maxval=16.0))
        D = jnp.ones((NHEADS,), jnp.float32)
        norm_w = jnp.ones((D_INNER,), jnp.float32)
        W_out = jax.random.normal(ks[5], (D_INNER, D_MODEL), jnp.float32) * D_INNER ** (-0.5)
        return dict(x=x, W_in=W_in, conv_w=conv_w, conv_b=conv_b, dt_bias=dt_bias, A_log=A_log, D=D, norm_w=norm_w, W_out=W_out)
    _L0_attn_all = _L0_attn_setup()
    _L0_attn_in = {k: v for k, v in _L0_attn_all.items() if k in ('W_in', 'conv_w', 'conv_b', 'dt_bias', 'A_log', 'D', 'norm_w', 'W_out')}
    del _L0_attn_all

    def _L0_xattn_setup():
        import jax, jax.numpy as jnp
        import numpy as np
        B, S, DIM, NH = (2, 256, 128, 8)
        DH = DIM // NH
        GATE_SOFT_CAP = 15.0
        BACKEND_EPS = 5e-05
        NORM_EPS = 1e-06

        def _mlstm_parallel(q, k, v, i_pre, f_pre):
            log_fg = jax.nn.log_sigmoid(f_pre)
            lf_cs = jnp.cumsum(log_fg, axis=-1)
            lf = jnp.concatenate([jnp.zeros_like(lf_cs[..., :1]), lf_cs], axis=-1)
            log_d = lf[..., 1:, None] - lf[..., None, 1:] + i_pre[..., None, :]
            t_idx = jnp.arange(q.shape[2])
            mask = t_idx[:, None] >= t_idx[None, :]
            log_d = jnp.where(mask, log_d, -jnp.inf)
            m = jnp.max(log_d, axis=-1, keepdims=True)
            d_mat = jnp.exp(log_d - m)
            scores = jnp.einsum('bhtd,bhsd->bhts', q, k) * (1.0 / np.sqrt(DH))
            s_mat = scores * d_mat
            denom = jnp.maximum(jnp.abs(jnp.sum(s_mat, axis=-1, keepdims=True)), jnp.exp(-m)) + BACKEND_EPS
            return jnp.einsum('bhts,bhsd->bhtd', s_mat, v) / denom
        key = jax.random.key(seed)
        kq, kk, kv, kw = jax.random.split(key, 4)
        q = jax.random.normal(kq, (B, S, DIM), dtype=jnp.float32)
        k = jax.random.normal(kk, (B, S, DIM), dtype=jnp.float32)
        v = jax.random.normal(kv, (B, S, DIM), dtype=jnp.float32)
        ifgate_w = 0.02 * jax.random.normal(kw, (2 * NH, 3 * DIM), dtype=jnp.float32)
        ifgate_b = jnp.concatenate([jnp.full((NH,), -10.0, dtype=jnp.float32), jnp.linspace(3.0, 6.0, NH, dtype=jnp.float32)])
        outnorm_w = jnp.zeros((DIM,), dtype=jnp.float32)
        return {'q': q, 'k': k, 'v': v, 'ifgate_w': ifgate_w, 'ifgate_b': ifgate_b, 'outnorm_w': outnorm_w}
    _L0_xattn_all = _L0_xattn_setup()
    _L0_xattn_in = {k: v for k, v in _L0_xattn_all.items() if k in ('ifgate_w', 'ifgate_b', 'outnorm_w')}
    del _L0_xattn_all

    def _L0_ffn_setup():
        import jax, jax.numpy as jnp
        import numpy as np
        LORA_DIM = 16
        LORA_TOKEN_INDEX = 1
        B, S, D, H = (4, 256, 128, 512)
        key = jax.random.key(seed)
        ks = jax.random.split(key, 6)
        x = jax.random.normal(ks[0], (B, S, D), dtype=jnp.float32)
        W1 = jax.random.normal(ks[1], (H, D), dtype=jnp.float32) * 0.02
        b1 = jnp.zeros((H,), dtype=jnp.float32)
        W2 = jax.random.normal(ks[2], (D, H), dtype=jnp.float32) * 0.02
        b2 = jnp.zeros((D,), dtype=jnp.float32)
        scale = jnp.asarray(0.001, dtype=jnp.float32)
        return {'x': x, 'W1': W1, 'b1': b1, 'W2': W2, 'b2': b2, 'scale': scale}
    _L0_ffn_all = _L0_ffn_setup()
    _L0_ffn_in = {k: v for k, v in _L0_ffn_all.items() if k in ('W1', 'b1', 'W2', 'b2', 'scale')}
    del _L0_ffn_all

    def _L1_attn_setup():
        import jax, jax.numpy as jnp
        import numpy as np
        import math
        D_MODEL = 128
        N_HEADS = 16
        EPS_GN = 1e-05

        def channel_group_norm(x, gamma, beta, num_groups, eps=EPS_GN):
            B, T, D = x.shape
            g = num_groups
            xt = x.transpose(0, 2, 1).reshape(B, g, D // g, T)
            mu = xt.mean(axis=(2, 3), keepdims=True)
            var = xt.var(axis=(2, 3), keepdims=True)
            xn = ((xt - mu) / jnp.sqrt(var + eps)).reshape(B, D, T)
            xn = xn * gamma[None, :, None] + beta[None, :, None]
            return xn.transpose(0, 2, 1)

        def l2_normalize(x, eps=1e-12):
            n = jnp.linalg.norm(x, axis=-1, keepdims=True)
            return x / jnp.maximum(n, eps)

        def decay_gammas(num_heads, dtype=jnp.float32):
            return 1.0 - jnp.exp(jnp.linspace(math.log(1.0 / 32.0), math.log(1.0 / 512.0), num_heads)).astype(dtype)
        key = jax.random.key(seed)
        ks = jax.random.split(key, 16)
        B, T, D = (4, 128, D_MODEL)
        s = 1.0 / math.sqrt(D)
        inp = {'x': jax.random.normal(ks[0], (B, T, D), jnp.float32), 'norm_g': jnp.ones((D,), jnp.float32), 'norm_b': jnp.zeros((D,), jnp.float32), 'qw': jax.random.normal(ks[1], (D, D), jnp.float32) * s, 'kw': jax.random.normal(ks[2], (D, D), jnp.float32) * s, 'vw': jax.random.normal(ks[3], (D, D), jnp.float32) * s, 'ow': jax.random.normal(ks[4], (D, D), jnp.float32) * s, 'ob': jnp.zeros((D,), jnp.float32), 'ffn_norm_g': jnp.ones((D,), jnp.float32), 'ffn_norm_b': jnp.zeros((D,), jnp.float32), 'w1': jax.random.normal(ks[5], (2 * D, D), jnp.float32) * s, 'b1': jnp.zeros((2 * D,), jnp.float32), 'w2': jax.random.normal(ks[6], (D, 2 * D), jnp.float32) * (1.0 / math.sqrt(2 * D)), 'b2': jnp.zeros((D,), jnp.float32)}
        return inp
    _L1_attn_all = _L1_attn_setup()
    _L1_attn_in = {k: v for k, v in _L1_attn_all.items() if k in ('norm_g', 'norm_b', 'qw', 'kw', 'vw', 'ow', 'ob', 'ffn_norm_g', 'ffn_norm_b', 'w1', 'b1', 'w2', 'b2')}
    del _L1_attn_all

    def _L1_xattn_setup():
        import jax, jax.numpy as jnp
        import numpy as np
        FEATURE_DIM = 128
        NUM_HEADS = 16
        HEAD_DIM = FEATURE_DIM // NUM_HEADS
        key = jax.random.key(seed)
        ks = jax.random.split(key, 11)
        B, SQ, SKV, D = (4, 128, 256, FEATURE_DIM)
        s = 1.0 / np.sqrt(D)
        return {'query': jax.random.normal(ks[0], (B, SQ, D), jnp.float32), 'key': jax.random.normal(ks[1], (B, SKV, D), jnp.float32), 'value': jax.random.normal(ks[2], (B, SKV, D), jnp.float32), 'wq': jax.random.normal(ks[3], (D, D), jnp.float32) * s, 'bq': jnp.zeros((D,), jnp.float32), 'wk': jax.random.normal(ks[4], (D, D), jnp.float32) * s, 'bk': jnp.zeros((D,), jnp.float32), 'wv': jax.random.normal(ks[5], (D, D), jnp.float32) * s, 'bv': jnp.zeros((D,), jnp.float32), 'wo': jax.random.normal(ks[6], (D, D), jnp.float32) * s, 'bo': jnp.zeros((D,), jnp.float32)}
    _L1_xattn_all = _L1_xattn_setup()
    _L1_xattn_in = {k: v for k, v in _L1_xattn_all.items() if k in ('wq', 'bq', 'wk', 'bk', 'wv', 'bv', 'wo', 'bo')}
    del _L1_xattn_all

    def _L1_ffn_setup():
        import jax, jax.numpy as jnp
        import numpy as np
        D_MODEL = 128
        N_EXPERTS = 8
        TOP_K = 2
        LN_EPS = 1e-05
        key = jax.random.key(seed)
        ks = jax.random.split(key, 8)
        B, S, d, E = (2, 256, D_MODEL, N_EXPERTS)
        f = 2 * d
        s_in = 0.02
        return {'x': jax.random.normal(ks[0], (B, S, d), jnp.float32), 'Wg': jax.random.normal(ks[1], (d, E), jnp.float32) * s_in, 'bg': jnp.zeros((E,), jnp.float32), 'W1': jax.random.normal(ks[2], (E, d, f), jnp.float32) * s_in, 'b1': jnp.zeros((E, f), jnp.float32), 'W2': jax.random.normal(ks[3], (E, f, d), jnp.float32) * s_in, 'b2': jnp.zeros((E, d), jnp.float32), 'gamma': jnp.ones((d,), jnp.float32), 'beta': jnp.zeros((d,), jnp.float32)}
    _L1_ffn_all = _L1_ffn_setup()
    _L1_ffn_in = {k: v for k, v in _L1_ffn_all.items() if k in ('Wg', 'bg', 'W1', 'b1', 'W2', 'b2', 'gamma', 'beta')}
    del _L1_ffn_all
    return {'x': x, 'ctx_1024': ctx_1024, 'L0_attn_W_in': _L0_attn_in['W_in'], 'L0_attn_conv_w': _L0_attn_in['conv_w'], 'L0_attn_conv_b': _L0_attn_in['conv_b'], 'L0_attn_dt_bias': _L0_attn_in['dt_bias'], 'L0_attn_A_log': _L0_attn_in['A_log'], 'L0_attn_D': _L0_attn_in['D'], 'L0_attn_norm_w': _L0_attn_in['norm_w'], 'L0_attn_W_out': _L0_attn_in['W_out'], 'L0_xattn_ifgate_w': _L0_xattn_in['ifgate_w'], 'L0_xattn_ifgate_b': _L0_xattn_in['ifgate_b'], 'L0_xattn_outnorm_w': _L0_xattn_in['outnorm_w'], 'L0_ffn_W1': _L0_ffn_in['W1'], 'L0_ffn_b1': _L0_ffn_in['b1'], 'L0_ffn_W2': _L0_ffn_in['W2'], 'L0_ffn_b2': _L0_ffn_in['b2'], 'L0_ffn_scale': _L0_ffn_in['scale'], 'L1_attn_norm_g': _L1_attn_in['norm_g'], 'L1_attn_norm_b': _L1_attn_in['norm_b'], 'L1_attn_qw': _L1_attn_in['qw'], 'L1_attn_kw': _L1_attn_in['kw'], 'L1_attn_vw': _L1_attn_in['vw'], 'L1_attn_ow': _L1_attn_in['ow'], 'L1_attn_ob': _L1_attn_in['ob'], 'L1_attn_ffn_norm_g': _L1_attn_in['ffn_norm_g'], 'L1_attn_ffn_norm_b': _L1_attn_in['ffn_norm_b'], 'L1_attn_w1': _L1_attn_in['w1'], 'L1_attn_b1': _L1_attn_in['b1'], 'L1_attn_w2': _L1_attn_in['w2'], 'L1_attn_b2': _L1_attn_in['b2'], 'L1_xattn_wq': _L1_xattn_in['wq'], 'L1_xattn_bq': _L1_xattn_in['bq'], 'L1_xattn_wk': _L1_xattn_in['wk'], 'L1_xattn_bk': _L1_xattn_in['bk'], 'L1_xattn_wv': _L1_xattn_in['wv'], 'L1_xattn_bv': _L1_xattn_in['bv'], 'L1_xattn_wo': _L1_xattn_in['wo'], 'L1_xattn_bo': _L1_xattn_in['bo'], 'L1_ffn_Wg': _L1_ffn_in['Wg'], 'L1_ffn_bg': _L1_ffn_in['bg'], 'L1_ffn_W1': _L1_ffn_in['W1'], 'L1_ffn_b1': _L1_ffn_in['b1'], 'L1_ffn_W2': _L1_ffn_in['W2'], 'L1_ffn_b2': _L1_ffn_in['b2'], 'L1_ffn_gamma': _L1_ffn_in['gamma'], 'L1_ffn_beta': _L1_ffn_in['beta']}

def reference(x, ctx_1024, L0_attn_W_in, L0_attn_conv_w, L0_attn_conv_b, L0_attn_dt_bias, L0_attn_A_log, L0_attn_D, L0_attn_norm_w, L0_attn_W_out, L0_xattn_ifgate_w, L0_xattn_ifgate_b, L0_xattn_outnorm_w, L0_ffn_W1, L0_ffn_b1, L0_ffn_W2, L0_ffn_b2, L0_ffn_scale, L1_attn_norm_g, L1_attn_norm_b, L1_attn_qw, L1_attn_kw, L1_attn_vw, L1_attn_ow, L1_attn_ob, L1_attn_ffn_norm_g, L1_attn_ffn_norm_b, L1_attn_w1, L1_attn_b1, L1_attn_w2, L1_attn_b2, L1_xattn_wq, L1_xattn_bq, L1_xattn_wk, L1_xattn_bk, L1_xattn_wv, L1_xattn_bv, L1_xattn_wo, L1_xattn_bo, L1_ffn_Wg, L1_ffn_bg, L1_ffn_W1, L1_ffn_b1, L1_ffn_W2, L1_ffn_b2, L1_ffn_gamma, L1_ffn_beta):
    import jax
    import jax.numpy as jnp

    def _L0_attn_ref(x, W_in, conv_w, conv_b, dt_bias, A_log, D, norm_w, W_out):
        import jax, jax.numpy as jnp
        import numpy as np
        D_MODEL = 128
        EXPAND = 2
        HEADDIM = 64
        D_STATE = 128
        D_CONV = 4
        D_INNER = EXPAND * D_MODEL
        NHEADS = D_INNER // HEADDIM
        CONV_DIM = D_INNER + 2 * D_STATE
        EPS = 1e-05

        def _causal_depthwise_conv(u, w, b):
            B, L, C = u.shape
            up = jnp.pad(u, ((0, 0), (D_CONV - 1, 0), (0, 0)))
            y = b
            for k in range(D_CONV):
                y = y + up[:, k:k + L, :] * w[:, k]
            return y

        def _rms(v):
            return v * jax.lax.rsqrt(jnp.mean(v * v, axis=-1, keepdims=True) + EPS)
        b, l, _ = x.shape
        zxbcdt = x @ W_in
        z = zxbcdt[..., :D_INNER]
        xBC = zxbcdt[..., D_INNER:D_INNER + CONV_DIM]
        dt = jax.nn.softplus(zxbcdt[..., -NHEADS:] + dt_bias)
        xBC = jax.nn.silu(_causal_depthwise_conv(xBC, conv_w, conv_b))
        xs = xBC[..., :D_INNER].reshape(b, l, NHEADS, HEADDIM)
        Bm = xBC[..., D_INNER:D_INNER + D_STATE]
        Cm = xBC[..., D_INNER + D_STATE:]
        A = -jnp.exp(A_log)
        decay = jnp.exp(dt * A)

        def step(h, inp):
            dec_t, dt_t, x_t, B_t, C_t = inp
            h = h * dec_t[:, :, None, None] + (dt_t[:, :, None] * x_t)[..., None] * B_t[:, None, None, :]
            y_t = jnp.einsum('bhpn,bn->bhp', h, C_t)
            return (h, y_t)
        h0 = jnp.zeros((b, NHEADS, HEADDIM, D_STATE), x.dtype)
        xs_t = (decay.transpose(1, 0, 2), dt.transpose(1, 0, 2), xs.transpose(1, 0, 2, 3), Bm.transpose(1, 0, 2), Cm.transpose(1, 0, 2))
        _, ys = jax.lax.scan(step, h0, xs_t)
        y = ys.transpose(1, 0, 2, 3) + D[None, None, :, None] * xs
        y = y.reshape(b, l, D_INNER)
        y = _rms(y * jax.nn.silu(z)) * norm_w
        out = y @ W_out
        return _rms(out) + x

    def _L0_xattn_ref(q, k, v, ifgate_w, ifgate_b, outnorm_w):
        import jax, jax.numpy as jnp
        import numpy as np
        B, S, DIM, NH = (2, 256, 128, 8)
        DH = DIM // NH
        GATE_SOFT_CAP = 15.0
        BACKEND_EPS = 5e-05
        NORM_EPS = 1e-06

        def _mlstm_parallel(q, k, v, i_pre, f_pre):
            log_fg = jax.nn.log_sigmoid(f_pre)
            lf_cs = jnp.cumsum(log_fg, axis=-1)
            lf = jnp.concatenate([jnp.zeros_like(lf_cs[..., :1]), lf_cs], axis=-1)
            log_d = lf[..., 1:, None] - lf[..., None, 1:] + i_pre[..., None, :]
            t_idx = jnp.arange(q.shape[2])
            mask = t_idx[:, None] >= t_idx[None, :]
            log_d = jnp.where(mask, log_d, -jnp.inf)
            m = jnp.max(log_d, axis=-1, keepdims=True)
            d_mat = jnp.exp(log_d - m)
            scores = jnp.einsum('bhtd,bhsd->bhts', q, k) * (1.0 / np.sqrt(DH))
            s_mat = scores * d_mat
            denom = jnp.maximum(jnp.abs(jnp.sum(s_mat, axis=-1, keepdims=True)), jnp.exp(-m)) + BACKEND_EPS
            return jnp.einsum('bhts,bhsd->bhtd', s_mat, v) / denom
        b, s, dim = q.shape
        gate_in = jnp.concatenate([q, k, v], axis=-1)
        pre = gate_in @ ifgate_w.T + ifgate_b
        pre = GATE_SOFT_CAP * jnp.tanh(pre / GATE_SOFT_CAP)
        i_pre = pre[..., :NH].transpose(0, 2, 1)
        f_pre = pre[..., NH:].transpose(0, 2, 1)
        qh = q.reshape(b, s, NH, DH).transpose(0, 2, 1, 3)
        kh = k.reshape(b, s, NH, DH).transpose(0, 2, 1, 3)
        vh = v.reshape(b, s, NH, DH).transpose(0, 2, 1, 3)
        h = _mlstm_parallel(qh, kh, vh, i_pre, f_pre)
        rrms = jax.lax.rsqrt(jnp.mean(h * h, axis=-1, keepdims=True) + NORM_EPS)
        gain = (1.0 + outnorm_w).reshape(1, NH, 1, DH)
        h = h * rrms * gain
        return h.transpose(0, 2, 1, 3).reshape(b, s, dim)

    def _L0_ffn_ref(x, W1, b1, W2, b2, scale):
        import jax, jax.numpy as jnp
        import numpy as np
        LORA_DIM = 16
        LORA_TOKEN_INDEX = 1
        B, S, D, H = (4, 256, 128, 512)
        Bx, Sx, Dx = x.shape
        Hx = W1.shape[0]
        lt = jax.lax.dynamic_slice_in_dim(x, LORA_TOKEN_INDEX, LORA_DIM, axis=1)
        even = lt[:, ::2, :]
        odd = lt[:, 1::2, :]
        m1 = (even[:, :4, :, None] * odd[:, :4, None, :]).reshape(Bx, Hx, Dx)
        m2 = (even[:, 4:, :, None] * odd[:, 4:, None, :]).reshape(Bx, Dx, Hx)
        h = jnp.einsum('bsd,hd->bsh', x, W1) + scale * jnp.einsum('bsd,bhd->bsh', x, m1) + b1
        h = jax.nn.gelu(h, approximate=False)
        out = jnp.einsum('bsh,oh->bso', h, W2) + scale * jnp.einsum('bsh,boh->bso', h, m2) + b2
        return out

    def _L1_attn_ref(x, norm_g, norm_b, qw, kw, vw, ow, ob, ffn_norm_g, ffn_norm_b, w1, b1, w2, b2):
        import jax, jax.numpy as jnp
        import numpy as np
        import math
        D_MODEL = 128
        N_HEADS = 16
        EPS_GN = 1e-05

        def channel_group_norm(x, gamma, beta, num_groups, eps=EPS_GN):
            B, T, D = x.shape
            g = num_groups
            xt = x.transpose(0, 2, 1).reshape(B, g, D // g, T)
            mu = xt.mean(axis=(2, 3), keepdims=True)
            var = xt.var(axis=(2, 3), keepdims=True)
            xn = ((xt - mu) / jnp.sqrt(var + eps)).reshape(B, D, T)
            xn = xn * gamma[None, :, None] + beta[None, :, None]
            return xn.transpose(0, 2, 1)

        def l2_normalize(x, eps=1e-12):
            n = jnp.linalg.norm(x, axis=-1, keepdims=True)
            return x / jnp.maximum(n, eps)

        def decay_gammas(num_heads, dtype=jnp.float32):
            return 1.0 - jnp.exp(jnp.linspace(math.log(1.0 / 32.0), math.log(1.0 / 512.0), num_heads)).astype(dtype)
        B, T, D = x.shape
        H = N_HEADS
        dh = D // H
        residual = x
        xn = channel_group_norm(x, norm_g, norm_b, H)
        q = l2_normalize(xn @ qw.T)
        k = l2_normalize(xn @ kw.T)
        v = xn @ vw.T

        def heads(t):
            return t.reshape(B, T, H, dh).transpose(0, 2, 1, 3)
        qh, kh, vh = (heads(q), heads(k), heads(v))
        gammas = decay_gammas(H)
        n = jnp.arange(T)[:, None]
        m = jnp.arange(T)[None, :]
        diff = n - m
        causal = diff >= 0
        exponent = jnp.where(causal, diff, 0).astype(jnp.float32)
        dmask = jnp.where(causal[None], gammas[:, None, None] ** exponent[None], 0.0)
        scale = 1.0 / math.sqrt(dh)
        sim = jnp.einsum('bhnd,bhmd->bhnm', qh, kh) * scale
        sim = sim * dmask[None]
        yh = jnp.einsum('bhnm,bhmd->bhnd', sim, vh)
        y = yh.transpose(0, 2, 1, 3).reshape(B, T, D)
        y = y @ ow.T + ob
        x = residual + y
        residual = x
        xn = channel_group_norm(x, ffn_norm_g, ffn_norm_b, H)
        h = jax.nn.silu(xn @ w1.T + b1)
        x = residual + (h @ w2.T + b2)
        return x

    def _L1_xattn_ref(query, key, value, wq, bq, wk, bk, wv, bv, wo, bo):
        import jax, jax.numpy as jnp
        import numpy as np
        FEATURE_DIM = 128
        NUM_HEADS = 16
        HEAD_DIM = FEATURE_DIM // NUM_HEADS
        B, SQ, D = query.shape
        H, HD = (NUM_HEADS, HEAD_DIM)
        q = (query @ wq.T + bq).reshape(B, SQ, H, HD).transpose(0, 2, 1, 3)
        k = (key @ wk.T + bk).reshape(B, -1, H, HD).transpose(0, 2, 1, 3)
        v = (value @ wv.T + bv).reshape(B, -1, H, HD).transpose(0, 2, 1, 3)
        scores = jnp.einsum('bhqd,bhkd->bhqk', q, k) / jnp.sqrt(jnp.asarray(HD, q.dtype))
        attn = jax.nn.softmax(scores, axis=-1)
        ctx = jnp.einsum('bhqk,bhkd->bhqd', attn, v)
        ctx = ctx.transpose(0, 2, 1, 3).reshape(B, SQ, D)
        return ctx @ wo.T + bo

    def _L1_ffn_ref(x, Wg, bg, W1, b1, W2, b2, gamma, beta):
        import jax, jax.numpy as jnp
        import numpy as np
        D_MODEL = 128
        N_EXPERTS = 8
        TOP_K = 2
        LN_EPS = 1e-05
        logits = jnp.einsum('bsd,de->bse', x, Wg) + bg
        topk_vals, topk_idx = jax.lax.top_k(logits, TOP_K)
        topk_w = jax.nn.softmax(topk_vals, axis=-1)
        h = jax.nn.relu(jnp.einsum('bsd,edf->bsef', x, W1) + b1)
        eo = jnp.einsum('bsef,efd->bsed', h, W2) + b2
        sel = jnp.take_along_axis(eo, topk_idx[..., None], axis=2)
        mixed = jnp.sum(sel * topk_w[..., None], axis=2)
        y = mixed + x
        mu = jnp.mean(y, axis=-1, keepdims=True)
        var = jnp.mean(jnp.square(y - mu), axis=-1, keepdims=True)
        return gamma * (y - mu) * jax.lax.rsqrt(var + LN_EPS) + beta
    x = _layernorm(x + _L0_attn_ref(x, L0_attn_W_in, L0_attn_conv_w, L0_attn_conv_b, L0_attn_dt_bias, L0_attn_A_log, L0_attn_D, L0_attn_norm_w, L0_attn_W_out), axis=-1)
    x = _layernorm(x + _L0_xattn_ref(x, ctx_1024, ctx_1024, L0_xattn_ifgate_w, L0_xattn_ifgate_b, L0_xattn_outnorm_w), axis=-1)
    x = _layernorm(x + _L0_ffn_ref(x, L0_ffn_W1, L0_ffn_b1, L0_ffn_W2, L0_ffn_b2, L0_ffn_scale), axis=-1)
    x = _layernorm(x + _L1_attn_ref(x, L1_attn_norm_g, L1_attn_norm_b, L1_attn_qw, L1_attn_kw, L1_attn_vw, L1_attn_ow, L1_attn_ob, L1_attn_ffn_norm_g, L1_attn_ffn_norm_b, L1_attn_w1, L1_attn_b1, L1_attn_w2, L1_attn_b2), axis=-1)
    x = _layernorm(x + _L1_xattn_ref(x, ctx_1024, ctx_1024, L1_xattn_wq, L1_xattn_bq, L1_xattn_wk, L1_xattn_bk, L1_xattn_wv, L1_xattn_bv, L1_xattn_wo, L1_xattn_bo), axis=-1)
    x = _layernorm(x + _L1_ffn_ref(x, L1_ffn_Wg, L1_ffn_bg, L1_ffn_W1, L1_ffn_b1, L1_ffn_W2, L1_ffn_b2, L1_ffn_gamma, L1_ffn_beta), axis=-1)
    return x

_drawn_inputs = setup_inputs


def setup_inputs(seed=0):
    import zlib

    import numpy as np

    out = dict(_drawn_inputs(seed))
    spreads = {'L0_attn_conv_b': (0.0, 0.1),
     'L0_attn_D': (1.0, 0.2),
     'L0_attn_norm_w': (1.0, 0.2),
     'L0_xattn_outnorm_w': (0.0, 0.1),
     'L0_ffn_b1': (0.0, 0.348),
     'L0_ffn_b2': (0.0, 0.1),
     'L1_attn_norm_g': (1.0, 0.6),
     'L1_attn_norm_b': (0.0, 0.8),
     'L1_attn_ob': (0.0, 0.1),
     'L1_attn_ffn_norm_g': (1.0, 0.2),
     'L1_attn_ffn_norm_b': (0.0, 0.334),
     'L1_attn_b1': (0.0, 0.303),
     'L1_attn_b2': (0.0, 0.1),
     'L1_xattn_bq': (0.0, 0.408),
     'L1_xattn_bk': (0.0, 2.0),
     'L1_xattn_bv': (0.0, 0.1),
     'L1_xattn_bo': (0.0, 0.1),
     'L1_ffn_bg': (0.0, 0.305),
     'L1_ffn_b1': (0.0, 0.8),
     'L1_ffn_b2': (0.0, 0.1),
     'L1_ffn_gamma': (1.0, 0.2),
     'L1_ffn_beta': (0.0, 0.1)}
    factors = {'L0_attn_A_log': 64.0, 'L1_ffn_W1': 3.71, 'L1_ffn_W2': 2.885}
    for name, (base, spread) in spreads.items():
        noise = np.random.default_rng([zlib.crc32(name.encode()), seed]).standard_normal(out[name].shape)
        drawn = base * np.exp(spread * noise) if base else spread * noise
        out[name] = jnp.asarray(drawn.astype(out[name].dtype))
    for name, factor in factors.items():
        out[name] = (out[name] * factor).astype(out[name].dtype)
    return out
```

```python
from contextlib import ExitStack

import concourse.bass as bass
from concourse import mybir

F32 = mybir.dt.float32
BF16 = mybir.dt.bfloat16
U32 = mybir.dt.uint32
ACT = mybir.ActivationFunctionType
ALU = mybir.AluOpType
AX = mybir.AxisListType

P = 128
B = 8
T = 256
NT = T // P
TILES = B * NT
PAIR = 2
LN_EPS = 1e-5

ARENA_WORDS = 79 * 256, 76 * 256
EXP_LN = "natural_log_exp_and_others"


class Env:

    def __init__(self, nc, ctx):
        self.nc, self.ctx = nc, ctx
        self.arena, self.used = None, 0

    def begin(self, arena):
        self.arena, self.used = arena, 0

    def sb(self, name, shape, dt=F32):
        if self.arena is None:
            return self.ctx.enter_context(self.nc.sbuf_tensor(name, shape, dt))
        n = 1
        for s in shape[1:]:
            n *= s
        words = n if dt != BF16 else (n + 1) // 2
        part = self.arena[0:shape[0], self.used:self.used + words]
        self.used += (words + 7) // 8 * 8
        if self.used > self.arena.shape[1]:
            raise ValueError(f"arena is full at {name}")
        if dt != F32:
            part = part.bitcast(dt)[:, 0:n]
        names = "abcde"[:len(shape) - 1]
        if len(names) > 1:
            part = part.rearrange(f"p ({' '.join(names)}) -> p {' '.join(names)}", **dict(zip(names, shape[1:])))
        return part

    def weights(self, name, layout):
        buf = self.sb(name, [P, layout["_size"]])
        return buf, lambda part: buf[:, layout[part][0]:layout[part][1]]

    def x_tile(self, t):
        return self.X[:, bass.ds(t, 1), :].rearrange("p a c -> p (a c)")

    def sem(self, name):
        return self.ctx.enter_context(self.nc.semaphore(name))


class Sublayer:
    def begin(self, eng):
        if self.index >= 2:
            eng.wait_ge(self.env.x_done[self.index - 2], B)
        eng.wait_ge(self.env.w_in[0], 16)
        eng.wait_ge(self.env.w_in[self.index + 1], 16)

    def sp(self, sp):
        pass


def pairs(eng):
    return eng.Fori(0, B // PAIR)


class LayerNormTail:

    def __init__(self, env, tag, eps, index):
        self.env, self.eps = env, env.w0(eps)
        self.stats = env.sb(f"{tag}_stats", [P, PAIR, NT, 6])
        self.mv = env.sb(f"{tag}_mv", [P, PAIR, NT, 2])
        self.lnv = env.sb(f"{tag}_lnv", [P, PAIR, NT])
        self.rstd = env.sb(f"{tag}_rstd", [P, PAIR, NT])
        if index is None:
            self.base = 0
            self.measured = env.sem(f"{tag}_measured")
            self.rooted = env.sem(f"{tag}_rooted")
        else:
            self.base = 2 * B * index
            self.measured, self.rooted = env.ln_measured, env.ln_rooted

    def moments(self, dve, y, b, p):
        both = dve.compute_val(2 * b + self.base + 1)
        for k in range(NT):
            ins = dve.bn_stats(self.stats[:, p, k, :], y[:, k, :])
        ins.then_inc(self.measured, 1)
        dve.wait_ge(self.env.w_in[0], 16)
        dve.wait_ge(self.measured, both)
        for k in range(NT):
            ins = dve.bn_aggr(self.mv[:, p, k, :], self.stats[:, p, k, :])
        ins.then_inc(self.measured, 1)

    def root(self, act, b, p):
        act.wait_ge(self.measured, 2 * b + self.base + 2)
        act.activation(self.lnv[:, p, :], self.mv[:, p, :, 1], ACT.Ln, bias=self.eps).then_inc(self.rooted, 1)
        act.wait_ge(self.rooted, 2 * b + self.base + 1)
        act.activation(self.rstd[:, p, :], self.lnv[:, p, :], ACT.Exp, scale=-0.5).then_inc(self.rooted, 1)

    def apply(self, dve, out, y, b, p, done):
        dve.wait_ge(self.rooted, 2 * b + self.base + 2)
        for k in range(NT):
            ins = dve.tensor_scalar(out(k), y[:, k, :], self.mv[:, p, k, 0:1], self.rstd[:, p, k:k + 1],
                                    ALU.subtract, ALU.mult)
        ins.then_inc(done, 1)


def log1p_half(dve, link, out, e, a, b):
    link(dve.tensor_scalar(a, e, 2.0, None, ALU.add))
    link(dve.reciprocal(b, a))
    link(dve.tensor_tensor(a, e, b, ALU.mult))
    link(dve.tensor_tensor(b, a, a, ALU.mult))
    link(dve.tensor_scalar(out, b, 1.0 / 15, None, ALU.mult))
    for odd in (13, 11, 9, 7, 5, 3):
        link(dve.scalar_tensor_tensor(out=out, in0=out, scalar=1.0 / odd, in1=b, op0=ALU.add, op1=ALU.mult))
    link(dve.scalar_tensor_tensor(out=out, in0=out, scalar=1.0, in1=a, op0=ALU.add, op1=ALU.mult))


def split3(dve, link, parts, x, rest):
    link(dve.tensor_copy(parts[0], x))
    link(dve.tensor_tensor(rest, x, parts[0], ALU.subtract))
    link(dve.tensor_copy(parts[1], rest))
    link(dve.tensor_tensor(parts[2], rest, parts[1], ALU.subtract))


M_INNER, M_STATE, M_HEADS, M_HEAD, M_TAPS = 256, 128, 4, 64, 4
M_CONV = M_INNER + 2 * M_STATE
M_SPLIT = 3
M_EPS = 1e-5


class Mamba(Sublayer):
    DT_ABS, DT_RATE, DT_SPLIT = 3, 19, 23

    def __init__(self, env, w, index):
        self.env, self.w, self.index = env, w, index
        sb, sem = env.sb, env.sem
        self.dt = sb("m_dt", [P, TILES, M_HEADS])
        self.dtv = sb("m_dtv", [P, 10, TILES * M_HEADS])
        self.arate = sb("m_arate", [P, 2, M_HEADS])
        self.dsplit = sb("m_dsplit", [P, TILES, M_SPLIT * M_HEADS], BF16)
        self.drows = sb("m_drows", [M_SPLIT * M_HEADS, TILES * P], BF16)
        self.selb = sb("m_selb", [M_SPLIT * M_HEADS, M_HEADS, P], BF16)
        self.wout = sb("m_wout", [P, 2, P])
        self.zs = sb("m_zs", [P, PAIR, 2, T])
        self.u = sb("m_u", [P, PAIR, 4, T + M_TAPS - 1])
        self.conv = sb("m_conv", [P, PAIR, 4, T])
        self.xbc = sb("m_xbc", [P, PAIR, 4, T])
        self.xdt = sb("m_xdt", [P, PAIR, NT, M_INNER])
        self.L0 = sb("m_L0", [P, PAIR, M_HEADS, T])
        self.L1 = sb("m_L1", [P, PAIR, M_HEADS, P])
        self.g = sb("m_g", [P, PAIR, 2, T])
        self.sq = sb("m_sq", [P, PAIR, 2, T])
        self.sqs = sb("m_sqs", [P, PAIR, T])
        self.junk = sb("m_junk", [P, PAIR, NT, P])
        self.su = sb("m_su", [P, PAIR, NT])
        self.tot = sb("m_tot", [P, PAIR, 2, NT])
        self.r = sb("m_r", [P, PAIR, 2, NT])
        self.y = sb("m_y", [P, PAIR, NT, P])
        self.tail = LayerNormTail(env, "m_ln", "eps_quarter", index)

        self.cast = sem("m_cast")
        self.wscaled = sem("m_wscaled")
        self.dt_raw = sem("m_dt_raw")
        self.dt_step = sem("m_dt_step")
        self.dt_exp = sem("m_dt_exp")
        self.dt_turned = sem("m_dt_turned")
        self.dt_rows = sem("m_dt_rows")
        self.z_up = sem("m_z_up")
        self.u_up = sem("m_u_up")
        self.z_act = sem("m_z_act")
        self.u_copy = sem("m_u_copy")
        self.conv_tap = sem("m_conv_tap")
        self.xbc_act = sem("m_xbc_act")
        self.x_turned = sem("m_x_turned")
        self.g_up = sem("m_g_up")
        self.d_up = sem("m_d_up")
        self.xdt_done = sem("m_xdt_done")
        self.scanned = sem("m_scanned")
        self.masked = sem("m_masked")
        self.y_up = sem("m_y_up")
        self.gated = sem("m_gated")
        self.squared = sem("m_squared")
        self.sq_sum = sem("m_sq_sum")
        self.o_up = sem("m_o_up")
        self.o_sq = sem("m_o_sq")
        self.o_tot = sem("m_o_tot")
        self.o_root = sem("m_o_root")
        self.y_done = sem("m_y_done")

    def pool(self, pool):
        env, w = self.env, self.w
        pool.memset(self.u[:, :, :, 0:M_TAPS - 1], 0.0).then_inc(self.y_done, PAIR)
        pool.tensor_copy(env.identb, env.ident)
        pool.tensor_copy(self.selb[:, :, :], w("sel_decay")[0:M_SPLIT * M_HEADS].rearrange("p (h m) -> p h m", h=M_HEADS)).then_inc(self.cast, 1)
        for hp in range(2):
            ins = pool.tensor_scalar(self.wout[:, hp, :], w("W_out")[:, hp * P:(hp + 1) * P],
                                     w("norm_w")[:, hp:hp + 1], None, ALU.mult)
        ins.then_inc(self.wscaled, 1)
        with pairs(pool) as it:
            for p in range(PAIR):
                b = it * PAIR + p
                pool.wait_ge(self.squared, b + 1)
                pool.tensor_tensor(self.sqs[:, p, :], self.sq[:, p, 0, :], self.sq[:, p, 1, :],
                                   ALU.add).then_inc(self.sq_sum, 1)

    def pe(self, pe):
        env, w, PS = self.env, self.w, self.env.ps
        pe.wait_ge(env.xT_in, 16)
        for t in range(TILES):
            ins = pe.matmul(PS[:, 0, t * M_HEADS:(t + 1) * M_HEADS], env.xT[:, t * P:(t + 1) * P],
                            w("W_in")[:, M_INNER + M_CONV:], start=True, stop=True)
        ins.then_inc(self.dt_raw, 1)
        pe.wait_ge(self.cast, 1)
        pe.wait_ge(self.dt_step, self.DT_SPLIT)
        for t in range(TILES):
            dst = PS[0:M_SPLIT * M_HEADS, 1 + t // 8, :].bitcast(BF16)[:, (t % 8) * P:(t % 8 + 1) * P]
            ins = pe.transpose(dst, self.dsplit[:, t, :], env.identb)
        ins.then_inc(self.dt_turned, 1)
        pe.wait_ge(self.dt_rows, 1)
        with pairs(pe) as it:
            for p in range(PAIR):
                b = it * PAIR + p
                k0 = 4 * p
                rhs = env.xT[:, bass.ds(b * T, T)]
                if True:
                    for j in range(2):
                        ins = pe.matmul(PS[:, k0, j * T:(j + 1) * T], w("W_in")[:, j * P:(j + 1) * P], rhs,
                                        start=True, stop=True)
                    ins.then_inc(self.z_up, 1)
                pe.wait_ge(self.y_done, b + 1)
                for j in range(4):
                    ins = pe.matmul(PS[:, k0 + 1 + j // 2, (j % 2) * T:(j % 2 + 1) * T],
                                    w("W_in")[:, (2 + j) * P:(3 + j) * P], rhs, start=True, stop=True)
                ins.then_inc(self.u_up, 1)
            for p in range(PAIR):
                b = it * PAIR + p
                k0 = 4 * p
                pe.wait_ge(self.xbc_act, b + 1)
                for k in range(NT):
                    for j in range(2):
                        ins = pe.transpose(PS[:, k0 + 3, k * M_INNER + j * P:k * M_INNER + (j + 1) * P],
                                           self.xbc[:, p, j, k * P:(k + 1) * P], env.ident)
                ins.then_inc(self.x_turned, 1)
                for h in range(M_HEADS):
                    ins = pe.matmul(PS[:, k0 + 1 + h // 2, (h % 2) * T:(h % 2 + 1) * T], self.selb[:, h, :],
                                    self.drows[:, bass.ds(b * T, T)], start=True, stop=True)
                ins.then_inc(self.d_up, 1)
                pe.wait_ge(self.z_act, b + 1)
                pe.matmul(PS[:, k0, 0:T], self.xbc[:, p, 2, 0:P], self.xbc[:, p, 3, :], start=True, stop=True)
                pe.matmul(PS[:, k0, T:T + P], self.xbc[:, p, 2, P:T], self.xbc[:, p, 3, P:T],
                          start=True, stop=True).then_inc(self.g_up, 1)
            for p in range(PAIR):
                b = it * PAIR + p
                k0 = 4 * p
                pe.wait_ge(self.xdt_done, b + 1)
                pe.wait_ge(self.masked, b + 1)
                for h in range(M_HEADS):
                    out = PS[(h % 2) * M_HEAD:(h % 2 + 1) * M_HEAD, k0 + 3, (h // 2) * T:(h // 2 + 1) * T]
                    pe.matmul(out, self.xdt[:, p, 0, h * M_HEAD:(h + 1) * M_HEAD], self.L0[:, p, h, :],
                              start=True, stop=False)
                    ins = pe.matmul(out[:, P:T], self.xdt[:, p, 1, h * M_HEAD:(h + 1) * M_HEAD], self.L1[:, p, h, :],
                                    start=False, stop=True)
                ins.then_inc(self.y_up, 1)
            for p in range(PAIR):
                b = it * PAIR + p
                k0 = 4 * p
                if p == 0:
                    pe.wait_ge(self.wscaled, 1)
                pe.wait_ge(self.gated, 3 * b + 3)
                for k in range(NT):
                    for hp in range(2):
                        pe.matmul(PS[:, k0 + 1, k * P:(k + 1) * P], self.g[:, p, hp, k * P:(k + 1) * P],
                                  self.wout[:, hp, :], start=(hp == 0), stop=(hp == 1))
                pe.wait_ge(self.sq_sum, b + 1)
                for k in range(NT):
                    ins = pe.matmul(PS[:, k0 + 1, T + k:T + k + 1], self.sqs[:, p, k * P:(k + 1) * P],
                                    env.ones_row[:, 0:1], start=True, stop=True)
                ins.then_inc(self.o_up, 1)

    def act(self, act):
        env, w, PS = self.env, self.w, self.env.ps
        act.preload_act_table_set(EXP_LN)
        act.wait_ge(self.dt_step, self.DT_ABS)
        act.activation(self.dtv[:, 2, :], self.dtv[:, 1, :], ACT.Exp, scale=-1.0).then_inc(self.dt_exp, 1)
        act.activation(self.arate[:, 1, :], self.arate[:, 0, :], ACT.Exp).then_inc(self.dt_exp, 1)
        act.wait_ge(self.dt_step, self.DT_RATE)
        act.activation(self.dtv[:, 1, :], self.dtv[:, 6, :], ACT.Exp).then_inc(self.dt_exp, 1)
        act.wait_ge(self.dt_turned, 1)
        for n in range(2):
            ins = act.activation(self.drows[:, n * 8 * P:(n + 1) * 8 * P], PS[0:M_SPLIT * M_HEADS, 1 + n, :].bitcast(BF16),
                                 ACT.Copy)
        ins.then_inc(self.dt_rows, 1)
        with pairs(act) as it:
            for p in range(PAIR):
                b = it * PAIR + p
                k0 = 4 * p
                act.wait_ge(self.u_up, b + 1)
                for n in range(2):
                    act.activation(self.u[:, p, 2 * n:2 * n + 2, M_TAPS - 1:],
                                   PS[:, k0 + 1 + n, :].rearrange("p (j t) -> p j t", j=2), ACT.Copy)
                for j in range(4):
                    ins = act.activation(self.conv[:, p, j, :], PS[:, k0 + 1 + j // 2, (j % 2) * T:(j % 2 + 1) * T],
                                         ACT.Identity, scale=w("conv_w")[:, j * M_TAPS + 3:j * M_TAPS + 4],
                                         bias=w("conv_b")[:, j:j + 1])
                ins.then_inc(self.u_copy, 1)
            for p in range(PAIR):
                b = it * PAIR + p
                act.wait_ge(self.z_up, b + 1)
                act.activation(self.zs[:, p, :, :], PS[:, 4 * p, :].rearrange("p (j t) -> p j t", j=2),
                               ACT.Silu).then_inc(self.z_act, 1)
                act.wait_ge(self.conv_tap, 3 * b + 3)
                act.activation(self.xbc[:, p, :, :], self.conv[:, p, :, :], ACT.Silu).then_inc(self.xbc_act, 1)
            for p in range(PAIR):
                b = it * PAIR + p
                act.wait_ge(self.gated, 3 * b + 3)
                act.activation(self.sq[:, p, :, :], self.g[:, p, :, :], ACT.Square).then_inc(self.squared, 1)
            act.preload_act_table_set(EXP_LN)
            for p in range(PAIR):
                b = it * PAIR + p
                act.wait_ge(self.o_up, b + 1)
                for k in range(NT):
                    ins = act.activation(self.junk[:, p, k, :], PS[:, 4 * p + 1, k * P:(k + 1) * P], ACT.Square,
                                         accum_out=self.su[:, p, k:k + 1])
                ins.then_inc(self.o_sq, 1)
                act.wait_ge(self.o_tot, 2 * b + 2)
                act.activation(self.r[:, p, 0, :], self.tot[:, p, 1, :], ACT.Ln, scale=4.0).then_inc(self.o_root, 1)
                act.wait_ge(self.o_root, 2 * b + 1)
                act.activation(self.r[:, p, 1, :], self.r[:, p, 0, :], ACT.Exp, scale=-0.5).then_inc(self.o_root, 1)
            for p in range(PAIR):
                self.tail.root(act, it * PAIR + p, p)

    def dve(self, dve):
        env, w, PS = self.env, self.w, self.env.ps
        n = 0

        def link(ins):
            nonlocal n
            n += 1
            ins.then_inc(self.dt_step, 1)
            dve.wait_ge(self.dt_step, n)

        v = [self.dtv[:, i, :] for i in range(10)]
        dt = self.dt[:, :, :].rearrange("p t h -> p (t h)")
        tiles = lambda a: a.rearrange("p (t h) -> p t h", h=M_HEADS)
        per_head = lambda a: a.unsqueeze(1).broadcast_to([P, TILES, M_HEADS])
        dve.wait_ge(self.dt_raw, 1)
        link(dve.tensor_tensor(tiles(v[0]), tiles(PS[:, 0, 0:TILES * M_HEADS]), per_head(w("dt_bias")), ALU.add))
        link(dve.tensor_scalar(self.arate[:, 0, :], w("A_log"), 88.0, None, ALU.min))
        link(dve.scalar_tensor_tensor(out=v[1], in0=v[0], scalar=-1.0, in1=v[0], op0=ALU.mult, op1=ALU.max))
        assert n == self.DT_ABS
        dve.wait_ge(self.dt_exp, 2)
        log1p_half(dve, link, v[5], v[2], v[3], v[4])
        link(dve.tensor_scalar(v[8], v[0], 0.0, None, ALU.max))
        link(dve.scalar_tensor_tensor(out=dt, in0=v[5], scalar=2.0, in1=v[8], op0=ALU.mult, op1=ALU.add))
        link(dve.tensor_tensor(tiles(v[5]), self.dt[:, :, :], per_head(self.arate[:, 1, :]), ALU.mult))
        link(dve.tensor_scalar(v[6], v[5], -1.0, -200.0, ALU.mult, ALU.max))
        assert n == self.DT_RATE, n
        dve.wait_ge(self.dt_exp, 3)
        parts = [self.dsplit[:, :, i * M_HEADS:(i + 1) * M_HEADS] for i in range(M_SPLIT)]
        split3(dve, link, parts, tiles(v[1]), tiles(v[7]))
        assert n == self.DT_SPLIT
        dve.wait_ge(env.x_in, 16)

        with pairs(dve) as it:
            for p in range(PAIR):
                b = it * PAIR + p
                dve.wait_ge(self.u_copy, b + 1)
                for tap in range(M_TAPS - 1):
                    for j in range(4):
                        ins = dve.scalar_tensor_tensor(
                            out=self.conv[:, p, j, :], in0=self.u[:, p, j, tap:tap + T],
                            scalar=w("conv_w")[:, j * M_TAPS + tap:j * M_TAPS + tap + 1], in1=self.conv[:, p, j, :],
                            op0=ALU.mult, op1=ALU.add)
                    ins.then_inc(self.conv_tap, 1)
                    dve.wait_ge(self.conv_tap, 3 * b + tap + 1)
            for p in range(PAIR):
                b = it * PAIR + p
                k0 = 4 * p
                dve.wait_ge(self.x_turned, b + 1)
                for k in range(NT):
                    ins = dve.tensor_tensor(
                        self.xdt[:, p, k, :].rearrange("p (h c) -> p h c", h=M_HEADS),
                        PS[:, k0 + 3, k * M_INNER:(k + 1) * M_INNER].rearrange("p (h c) -> p h c", h=M_HEADS),
                        self.dt[:, bass.ds(b * NT + k, 1), :].rearrange("p a h -> p (a h)").unsqueeze(2).broadcast_to([P, M_HEADS, M_HEAD]),
                        ALU.mult)
                ins.then_inc(self.xdt_done, 1)
                dve.wait_ge(self.d_up, b + 1)
                for h in range(M_HEADS):
                    row = PS[:, k0 + 1 + h // 2, (h % 2) * T:(h % 2 + 1) * T]
                    dve.tensor_tensor_scan(self.L0[:, p, h, :], row, env.w0("ident"), 0.0, ALU.mult, ALU.add)
                    ins = dve.tensor_tensor_scan(self.L1[:, p, h, :], row[:, P:T], env.ident, 0.0,
                                                 ALU.mult, ALU.add)
                ins.then_inc(self.scanned, 1)
                dve.wait_ge(self.g_up, b + 1)
                dve.wait_ge(self.scanned, b + 1)
                dve.tensor_tensor(self.L0[:, p, :, :], self.L0[:, p, :, :],
                                  PS[:, k0, 0:T].unsqueeze(1).broadcast_to([P, M_HEADS, T]), ALU.mult)
                dve.tensor_tensor(self.L1[:, p, :, :], self.L1[:, p, :, :],
                                  PS[:, k0, T:T + P].unsqueeze(1).broadcast_to([P, M_HEADS, P]),
                                  ALU.mult).then_inc(self.masked, 1)
            for p in range(PAIR):
                b = it * PAIR + p
                dve.wait_ge(self.y_up, b + 1)
                for hp in range(2):
                    ins = dve.scalar_tensor_tensor(
                        out=self.g[:, p, hp, :], in0=self.xbc[:, p, hp, :], scalar=w("D")[:, hp:hp + 1],
                        in1=PS[:, 4 * p + 3, hp * T:(hp + 1) * T], op0=ALU.mult, op1=ALU.add)
                ins.then_inc(self.gated, 2)
                dve.wait_ge(self.gated, 3 * b + 2)
                dve.tensor_tensor(self.g[:, p, :, :], self.g[:, p, :, :], self.zs[:, p, :, :],
                                  ALU.mult).then_inc(self.gated, 1)
            for p in range(PAIR):
                b = it * PAIR + p
                k0 = 4 * p
                dve.wait_ge(self.o_sq, b + 1)
                dve.tensor_scalar(self.tot[:, p, 0, :], PS[:, k0 + 1, T:T + NT], M_EPS / M_INNER, M_EPS * M_EPS,
                                  ALU.mult, ALU.add).then_inc(self.o_tot, 1)
                dve.wait_ge(self.o_tot, 2 * b + 1)
                dve.scalar_tensor_tensor(out=self.tot[:, p, 1, :], in0=self.su[:, p, :], scalar=1.0 / P,
                                         in1=self.tot[:, p, 0, :], op0=ALU.mult, op1=ALU.add).then_inc(self.o_tot, 1)
                dve.wait_ge(self.o_root, 2 * b + 2)
                for k in range(NT):
                    ins = dve.scalar_tensor_tensor(
                        out=self.y[:, p, k, :], in0=PS[:, k0 + 1, k * P:(k + 1) * P], scalar=self.r[:, p, 1, k:k + 1],
                        in1=env.x_tile(b * NT + k), op0=ALU.mult, op1=ALU.add)
                ins.then_inc(self.y_done, 1)
                dve.wait_ge(self.y_done, b + 1 + PAIR)
                self.tail.moments(dve, self.y[:, p, :, :], b, p)
            for p in range(PAIR):
                b = it * PAIR + p
                self.tail.apply(dve, lambda k: env.x_tile(b * NT + k), self.y[:, p, :, :], b, p, env.x_done[0])


class Turned:

    def __init__(self, env, index):
        self.env, self.source = env, index - 1
        self.base = B * (index - 1)
        self.up = env.turned_up
        self.ready = env.turned_ready
        self.all = self.base + B

    def pe(self, pe):
        env = self.env
        pe.wait_ge(env.x_done[self.source], B)
        for b in range(B):
            if b >= 2:
                pe.wait_ge(self.ready, self.base + b - 1)
            for k in range(NT):
                ins = pe.transpose(env.ps[:, 6 + b % 2, k * P:(k + 1) * P], env.X[:, b * NT + k, :], env.ident)
            ins.then_inc(self.up, 1)

    def act(self, act):
        env = self.env
        for b in range(B):
            act.wait_ge(self.up, self.base + b + 1)
            act.activation(env.xT[:, b * T:(b + 1) * T], env.ps[:, 6 + b % 2, 0:T], ACT.Copy).then_inc(self.ready, 1)


X_HEADS, X_DH = 8, 16
X_SLOT = 32
X_UNITS = X_HEADS // 2
X_CAP, X_DEN_EPS, X_NORM_EPS = 15.0, 5e-5, 1e-6


class MLstm(Sublayer):
    CH_CAP, CH_ABS, CH_LF, CH_M, CH_SPLIT = 3, 4, 19, 23, 27

    def __init__(self, env, w, index):
        self.env, self.w, self.index = env, w, index
        sb, sem = env.sb, env.sem
        R = B * X_HEADS
        self.turned = Turned(env, index)
        self.cap = sb("x_cap", [P, T])
        self.rows = sb("x_rows", [R, 12, T])
        self.bcol = sb("x_bcol", [P, 1])
        self.split = sb("x_split", [R, 3, T], BF16)
        self.mrows = sb("x_mrows", [3 * X_HEADS, B, T], BF16)
        self.cols = sb("x_cols", [P, 6, R])
        self.selb = sb("x_selb", [3 * X_HEADS, X_HEADS, P], BF16)
        self.gkv = sb("x_gkv", [P, 2 * (2 * B - 1) * X_HEADS])
        self.maskb = sb("x_maskb", [P, P], BF16)
        self.kT = sb("x_kT", [P, PAIR, T])
        self.ktok = sb("x_ktok", [P, PAIR, P])
        self.xTs = sb("x_xTs", [P, PAIR, P])
        self.abias = sb("x_abias", [P, PAIR, NT, X_HEADS])
        self.V = sb("x_V", [P, PAIR, NT, X_HEADS, X_SLOT])
        self.wV = sb("x_wV", [P, PAIR, X_HEADS, X_SLOT])
        self.q = sb("x_q", [P, PAIR, 2, T])
        self.E = sb("x_E", [P, 2, 4, P])
        self.Pm = sb("x_P", [P, 2, 4, P])
        self.kv = sb("x_kv", [P, PAIR, T])
        self.O = sb("x_O", [P, PAIR, 2, T])
        self.CB = sb("x_CB", [P, PAIR, NT, X_HEADS, X_SLOT])
        self.tmp = sb("x_tmp", [P, PAIR, X_HEADS, X_SLOT])
        self.sq = sb("x_sq", [P, PAIR, NT, P])
        self.den = sb("x_den", [P, PAIR, 6, NT * X_HEADS])
        self.y = sb("x_y", [P, PAIR, NT, P])
        self.tail = LayerNormTail(env, "x_ln", "eps", index)

        self.consts = sem("x_consts")
        self.g_up = sem("x_g_up")
        self.chain = sem("x_chain")
        self.chain_act = sem("x_chain_act")
        self.m_out = sem("x_m_out")
        self.m_in = sem("x_m_in")
        self.c_up = sem("x_c_up")
        self.c_done = sem("x_c_done")
        self.loaded = sem("x_loaded")
        self.v_done = sem("x_v_done")
        self.q_done = sem("x_q_done")
        self.kv_up = sem("x_kv_up")
        self.kv_done = sem("x_kv_done")
        self.inter_up = sem("x_inter_up")
        self.s_up = sem("x_s_up")
        self.e_done = sem("x_e_done")
        self.p_done = sem("x_p_done")
        self.o_up = sem("x_o_up")
        self.o_copy = sem("x_o_copy")
        self.to_up = sem("x_to_up")
        self.to_copy = sem("x_to_copy")
        self.inter_read = sem("x_inter_read")
        self.comb = sem("x_comb")
        self.out = sem("x_out")
        self.rooted = sem("x_rooted")

    def sp(self, sp):
        sp.wait_ge(self.chain, self.CH_SPLIT)
        sp.dma_start(self.env.m_dram.rearrange("s b h t -> (b h) s t"), self.split[:, :, :]).then_inc(self.m_out, 16)
        sp.wait_ge(self.m_out, 16)
        for s in range(3):
            sp.dma_start(self.mrows[s * X_HEADS:(s + 1) * X_HEADS, :, :],
                         self.env.m_dram[s].rearrange("b h t -> h b t")).then_inc(self.m_in, 16)

    def pool(self, pool):
        env, w = self.env, self.w
        flat = self.V[:, :, :, :, :].rearrange("p a k h v -> p (a k h) v")
        pool.memset(flat[:, :, X_DH:X_SLOT], 0.0).then_inc(self.to_up, PAIR)
        pool.wait_ge(self.to_up, PAIR)
        pool.memset(flat[:, :, X_DH:X_DH + 1], 1.0).then_inc(self.inter_read, 1)
        pool.tensor_tensor(self.gkv[:, :], w("gate_k"), w("gate_v"), ALU.add).then_inc(self.to_copy, 1)
        pool.tensor_copy(self.maskb[:, :], w("future"))
        pool.tensor_copy(self.selb[:, :, :],
                         w("sel")[0:3 * X_HEADS].unsqueeze(2).broadcast_to([3 * X_HEADS, X_HEADS, P])).then_inc(self.consts, 1)
        pool.wait_ge(env.ctx_in, 32)
        pool.wait_ge(self.c_done, 1)
        pool.wait_ge(self.turned.ready, self.turned.all)
        with pairs(pool) as it:
            for p in range(PAIR):
                b = it * PAIR + p
                pool.wait_ge(self.to_up, b + 1)
                pool.tensor_copy(self.kT[:, p, :], env.ctxT[:, bass.ds(b * T, T)])
                pool.tensor_copy(self.ktok[:, p, :], env.ctok[:, bass.ds(b * NT, 1), :].rearrange("p a c -> p (a c)"))
                pool.tensor_copy(self.xTs[:, p, :], env.xT[:, bass.ds(b * T + P, P)])
                pool.tensor_copy(self.abias[:, p, :, :],
                                 self.cols[:, 0:2, bass.ds(b * X_HEADS, X_HEADS)]).then_inc(self.loaded, 1)
                for k in range(NT):
                    ins = pool.tensor_copy(
                        self.V[:, p, k, :, 0:X_DH],
                        env.ctok[:, bass.ds(b * NT + k, 1), :].rearrange("p a (h c) -> p (a h) c", h=X_HEADS))
                ins.then_inc(self.v_done, 1)
                pool.wait_ge(self.v_done, 2 * b + 1)
                pool.tensor_tensor(
                    self.wV[:, p, :, :], self.V[:, p, 0, :, :],
                    self.cols[:, 4:5, bass.ds(b * X_HEADS, X_HEADS)].rearrange("p a h -> p (a h)").unsqueeze(2)
                        .broadcast_to([P, X_HEADS, X_SLOT]), ALU.mult).then_inc(self.v_done, 1)

    def pe(self, pe):
        env, w, PS = self.env, self.w, self.env.ps
        pe.wait_ge(env.ctx_in, 32)
        self.turned.pe(pe)
        lo = (B - 1) * X_HEADS
        R = B * X_HEADS
        pe.wait_ge(self.turned.ready, self.turned.all)
        pe.wait_ge(self.to_copy, 1)
        for b in range(B):
            win = slice(lo - b * X_HEADS, lo - b * X_HEADS + R)
            for g in range(2):
                gates = lambda a: a.rearrange("p (g c) -> p g c", g=2)[:, g, win]
                out = PS[g * R:(g + 1) * R, 0, 0:T]
                pe.matmul(out, gates(w("gate_q")), env.xT[:, b * T:(b + 1) * T], start=(b == 0), stop=False)
                ins = pe.matmul(out, gates(self.gkv[:, :]), env.ctxT[:, b * T:(b + 1) * T],
                                start=False, stop=(b == B - 1))
        ins.then_inc(self.g_up, 1)
        pe.wait_ge(self.chain_act, 5)
        for n, (row, k) in enumerate(((5, 0), (5, 1), (8, 0), (8, 1), (9, 0), (10, 1))):
            ins = pe.transpose(PS[:, 1, n * R:(n + 1) * R], self.rows[:, row, k * P:(k + 1) * P],
                               env.ident[0:R, 0:R])
        ins.then_inc(self.c_up, 1)
        pe.wait_ge(self.m_in, 48)
        pe.wait_ge(self.c_done, 1)
        pe.wait_ge(self.consts, 1)

        def scores(b, p, u, n):
            S, D = PS[:, n % 2, :], PS[:, 2 + n % 2, :]
            if u == 0:
                pe.wait_ge(self.loaded, b + 1)
                pe.wait_ge(self.q_done, b + 1)
            for i in range(2):
                r = slice(X_SLOT * u, X_SLOT * u + X_SLOT)
                for c in range(NT):
                    pe.matmul(S[:, (2 * i + c) * P:(2 * i + c + 1) * P], self.kT[r, p, c * P:(c + 1) * P],
                              self.q[r, p, i, c * P:(c + 1) * P], start=True, stop=True)
            for i in range(2):
                pe.matmul(D[:, i * T:(i + 1) * T], self.selb[:, 2 * u + i, :],
                          self.mrows[:, bass.ds(b, 1), :].rearrange("p a t -> p (a t)"),
                          start=(i == 0), stop=False, skip_group_check=True)
            pe.matmul(D, env.identb, self.maskb[:, :].unsqueeze(1).broadcast_to([P, 4, P]),
                      start=False, stop=True, skip_group_check=True).then_inc(self.s_up, 1)

        def mix(b, p, u, n, it):
            pe.wait_ge(self.p_done, (it * PAIR) * X_UNITS + n + 1)
            for i in range(2):
                h = 2 * u + i
                for c in range(NT):
                    q4 = h % 4
                    ins = pe.matmul(PS[X_SLOT * q4:X_SLOT * (q4 + 1), 4 + p, (h // 4) * T + c * P:(h // 4) * T + (c + 1) * P],
                                    self.V[:, p, c, h, :], self.Pm[:, n % 2, 2 * i + c, :], start=True, stop=True)
            if u == X_UNITS - 1:
                ins.then_inc(self.o_up, 1)

        with pairs(pe) as it:
            for p in range(PAIR):
                b = it * PAIR + p
                pe.wait_ge(self.v_done, 2 * b + 2)
                pe.wait_ge(self.inter_read, b + 1)
                pe.matmul(PS[:, 7, 0:T], self.ktok[:, p, :], self.wV[:, p, :, :], start=True, stop=True).then_inc(self.kv_up, 1)
                for u in range(X_UNITS):
                    n = p * X_UNITS + u
                    scores(b, p, u, n)
                    if n > 0:
                        mix(it * PAIR + (n - 1) // X_UNITS, (n - 1) // X_UNITS, (n - 1) % X_UNITS, n - 1, it)
                    if u == 1:
                        pe.wait_ge(self.kv_done, b + 1)
                        pe.matmul(PS[:, 7, T:2 * T], self.xTs[:, p, :], self.kv[:, p, :],
                                  start=True, stop=True).then_inc(self.inter_up, 1)
            mix(it * PAIR + 1, 1, X_UNITS - 1, 2 * X_UNITS - 1, it)
            for p in range(PAIR):
                b = it * PAIR + p
                pe.wait_ge(self.o_copy, b + 1)
                pe.wait_ge(self.to_copy, b + 1)
                for c in range(NT):
                    for g in range(2):
                        ins = pe.transpose(PS[:, 6, (2 * c + g) * P:(2 * c + g + 1) * P],
                                           self.O[:, p, g, c * P:(c + 1) * P], env.ident)
                ins.then_inc(self.to_up, 1)

    def act(self, act):
        env, w, PS = self.env, self.w, self.env.ps
        R = B * X_HEADS
        self.turned.act(act)
        act.wait_ge(self.g_up, 1)
        act.wait_ge(self.chain, 1)
        act.activation(self.cap[:, :], PS[:, 0, 0:T], ACT.Tanh, scale=1.0 / X_CAP, bias=self.bcol[:, 0:1]).then_inc(self.chain_act, 1)
        act.preload_act_table_set(EXP_LN)
        act.wait_ge(self.chain, self.CH_ABS)
        act.activation(self.rows[:, 2, :], self.rows[:, 1, :], ACT.Exp, scale=-1.0).then_inc(self.chain_act, 1)
        act.wait_ge(self.chain, self.CH_M)
        act.activation(self.rows[:, 8, :], self.rows[:, 7, :], ACT.Exp, scale=-1.0).then_inc(self.chain_act, 1)
        act.activation(self.rows[:, 9, 0:P], self.rows[:, 5, 0:P], ACT.Exp, bias=self.rows[:, 11, P - 1:P]).then_inc(self.chain_act, 1)
        act.activation(self.rows[:, 10, P:T], self.rows[:, 11, P:T], ACT.Exp, bias=self.rows[:, 6, P - 1:P]).then_inc(self.chain_act, 1)
        with pairs(act) as it:
            for p in range(PAIR):
                b = it * PAIR + p
                for u in range(X_UNITS):
                    n = p * X_UNITS + u
                    act.wait_ge(self.s_up, (it * PAIR) * X_UNITS + n + 1)
                    for i in range(2):
                        for c in range(NT):
                            ins = act.activation(self.E[:, n % 2, 2 * i + c, :],
                                                 PS[:, 2 + n % 2, (2 * i + c) * P:(2 * i + c + 1) * P], ACT.Exp,
                                                 bias=self.abias[:, p, c, 2 * u + i:2 * u + i + 1])
                    ins.then_inc(self.e_done, 1)
            for p in range(PAIR):
                b = it * PAIR + p
                act.wait_ge(self.o_up, b + 1)
                act.activation(self.O[:, p, :, :], PS[:, 4 + p, :].rearrange("p (g t) -> p g t", g=2),
                               ACT.Copy).then_inc(self.o_copy, 1)
            for p in range(PAIR):
                b = it * PAIR + p
                act.wait_ge(self.to_up, b + 1 + PAIR)
                act.activation(self.CB[:, p, :, :, :].rearrange("p c h v -> p (c h v)"), PS[:, 6, :], ACT.Copy).then_inc(self.to_copy, 1)
            for p in range(PAIR):
                b = it * PAIR + p
                act.wait_ge(self.comb, 8 * b + 8)
                act.activation(self.den[:, p, 4, :], self.den[:, p, 3, :], ACT.Ln, scale=1.0 / X_DH).then_inc(self.rooted, 1)
                act.wait_ge(self.rooted, 2 * b + 1)
                act.activation(self.den[:, p, 5, :], self.den[:, p, 4, :], ACT.Exp, scale=-0.5).then_inc(self.rooted, 1)
            for p in range(PAIR):
                self.tail.root(act, it * PAIR + p, p)

    def dve(self, dve):
        env, w, PS = self.env, self.w, self.env.ps
        R = B * X_HEADS
        row = [self.rows[:, i, :] for i in range(12)]
        n = 0

        def link(ins):
            nonlocal n
            n += 1
            ins.then_inc(self.chain, 1)
            dve.wait_ge(self.chain, n)

        link(dve.tensor_scalar(self.bcol[:, :], w("gate_b"), 1.0 / X_CAP, None, ALU.mult))
        dve.wait_ge(self.chain_act, 1)
        i_, f_ = row[0], row[4]
        link(dve.tensor_scalar(i_, self.cap[0:R, :], X_CAP, None, ALU.mult))
        link(dve.tensor_scalar(f_, self.cap[R:2 * R, :], X_CAP, None, ALU.mult))
        assert n == self.CH_CAP
        link(dve.scalar_tensor_tensor(out=row[1], in0=f_, scalar=-1.0, in1=f_, op0=ALU.mult, op1=ALU.max))
        assert n == self.CH_ABS
        dve.wait_ge(self.chain_act, 2)
        log1p_half(dve, link, row[3], row[2], row[6], row[7])
        link(dve.tensor_scalar(row[6], f_, 0.0, None, ALU.min))
        link(dve.scalar_tensor_tensor(out=row[3], in0=row[3], scalar=-2.0, in1=row[6], op0=ALU.mult, op1=ALU.add))
        link(dve.tensor_tensor_scan(row[4], env.ones_row[0:R, :], row[3], 0.0, ALU.mult, ALU.add))
        assert n == self.CH_LF, n
        link(dve.tensor_tensor(row[5], i_, row[4], ALU.subtract))
        link(dve.tensor_tensor_scan(row[6], row[5], row[5], -3e38, ALU.max, ALU.max))
        link(dve.tensor_tensor(row[7], row[4], row[6], ALU.add))
        link(dve.tensor_scalar(row[11], row[6], -1.0, None, ALU.mult))
        assert n == self.CH_M, n
        split3(dve, link, [self.split[:, i, :] for i in range(3)], row[11], row[2])
        assert n == self.CH_SPLIT, n
        dve.wait_ge(self.c_up, 1)
        dve.tensor_copy(self.cols[:, :, :], PS[:, 1, 0:6 * R].rearrange("p (n r) -> p n r", n=6)).then_inc(self.c_done, 1)

        with pairs(dve) as it:
            for p in range(PAIR):
                b = it * PAIR + p
                for i in range(2):
                    ins = dve.tensor_scalar(self.q[:, p, i, :], env.xT[:, bass.ds(b * T, T)], w("head_par")[:, i:i + 1],
                                            None, ALU.mult)
                ins.then_inc(self.q_done, 1)
            for p in range(PAIR):
                b = it * PAIR + p
                dve.wait_ge(self.kv_up, b + 1)
                dve.tensor_tensor(self.kv[:, p, :], PS[:, 7, 0:T], w("same_head"), ALU.mult).then_inc(self.kv_done, 1)
                for u in range(X_UNITS):
                    m = p * X_UNITS + u
                    dve.wait_ge(self.e_done, (it * PAIR) * X_UNITS + m + 1)
                    dve.tensor_tensor(self.Pm[:, m % 2, :, :].rearrange("p a t -> p (a t)"),
                                      self.E[:, m % 2, :, :].rearrange("p a t -> p (a t)"),
                                      PS[:, m % 2, :], ALU.mult).then_inc(self.p_done, 1)
                dve.wait_ge(self.inter_up, b + 1)
                dve.tensor_tensor(
                    self.tmp[:, p, :, :], PS[:, 7, T:2 * T].rearrange("p (h v) -> p h v", h=X_HEADS),
                    self.cols[:, 5:6, bass.ds(b * X_HEADS, X_HEADS)].rearrange("p a h -> p (a h)").unsqueeze(2)
                        .broadcast_to([P, X_HEADS, X_SLOT]), ALU.mult).then_inc(self.inter_read, 1)
            for p in range(PAIR):
                b = it * PAIR + p
                CB = self.CB[:, p, :, :, :].rearrange("p c h v -> p (c h) v")
                num, wsum = CB[:, :, 0:X_DH], CB[:, :, X_DH:X_DH + 1].rearrange("p h a -> p (h a)")
                sq = self.sq[:, p, :, :].rearrange("p c (h v) -> p (c h) v", h=X_HEADS)
                den = [self.den[:, p, i, :] for i in range(6)]
                em = self.cols[:, 2:4, bass.ds(b * X_HEADS, X_HEADS)]

                def step(ins, k):
                    ins.then_inc(self.comb, 1)
                    dve.wait_ge(self.comb, 8 * b + k)

                dve.wait_ge(self.to_copy, b + 2)
                dve.wait_ge(self.inter_read, b + 2)
                step(dve.tensor_tensor(self.CB[:, p, 1, :, :], self.CB[:, p, 1, :, :], self.tmp[:, p, :, :], ALU.add), 1)
                step(dve.tensor_tensor(sq, num, num, ALU.mult), 2)
                step(dve.scalar_tensor_tensor(out=den[1], in0=wsum, scalar=-1.0, in1=wsum, op0=ALU.mult, op1=ALU.max), 3)
                step(dve.tensor_reduce(den[0], sq, AX.X, ALU.add), 4)
                step(dve.tensor_tensor(den[2].rearrange("p (c h) -> p c h", c=NT), den[1].rearrange("p (c h) -> p c h", c=NT),
                                       em, ALU.max), 5)
                step(dve.tensor_scalar(den[1], den[2], X_DEN_EPS, None, ALU.add), 6)
                step(dve.scalar_tensor_tensor(out=den[2], in0=den[1], scalar=X_DH * X_NORM_EPS, in1=den[1],
                                              op0=ALU.mult, op1=ALU.mult), 7)
                dve.tensor_tensor(den[3], den[0], den[2], ALU.add).then_inc(self.comb, 1)
            for p in range(PAIR):
                b = it * PAIR + p
                CB = self.CB[:, p, :, :, :].rearrange("p c h v -> p (c h) v")
                sq = self.sq[:, p, :, :].rearrange("p c (h v) -> p (c h) v", h=X_HEADS)
                dve.wait_ge(self.rooted, 2 * b + 2)
                dve.tensor_tensor(sq, CB[:, :, 0:X_DH], self.den[:, p, 5, :].unsqueeze(2).broadcast_to([P, NT * X_HEADS, X_DH]),
                                  ALU.mult).then_inc(self.out, 1)
                dve.wait_ge(self.out, 3 * b + 1)
                dve.scalar_tensor_tensor(out=self.sq[:, p, :, :], in0=w("outnorm").unsqueeze(1).broadcast_to([P, NT, P]),
                                         scalar=1.0, in1=self.sq[:, p, :, :], op0=ALU.add, op1=ALU.mult).then_inc(self.out, 1)
                dve.wait_ge(self.out, 3 * b + 2)
                dve.tensor_tensor(self.y[:, p, :, :], self.sq[:, p, :, :], env.X[:, bass.ds(b * NT, NT), :],
                                  ALU.add).then_inc(self.out, 1)
                dve.wait_ge(self.out, 3 * b + 3)
                self.tail.moments(dve, self.y[:, p, :, :], b, p)
            for p in range(PAIR):
                b = it * PAIR + p
                self.tail.apply(dve, lambda k: env.x_tile(b * NT + k), self.y[:, p, :, :], b, p, env.x_done[1])


F_HID, F_PAIRS = 512, 4
F_BLOCKS = F_HID // P


class Ffn(Sublayer):
    def __init__(self, env, w, index):
        self.env, self.w, self.index = env, w, index
        sb, sem = env.sb, env.sem
        self.turned = Turned(env, index)
        self.rows = sb("f_rows", [F_PAIRS, 4, B, P])
        self.odd = sb("f_odd", [F_PAIRS, PAIR, 2, P])
        self.e1 = sb("f_e1", [F_PAIRS, PAIR, F_PAIRS, P])
        self.e2 = sb("f_e2", [F_PAIRS, PAIR, F_BLOCKS, P])
        self.W1 = sb("f_W1b", [P, PAIR, F_HID])
        self.W2 = sb("f_W2b", [P, PAIR, F_HID])
        self.h = sb("f_h", [P, PAIR, F_BLOCKS, T])
        self.xb = sb("f_xb", [P, PAIR, NT, P])
        self.y = sb("f_y", [P, PAIR, NT, P])
        self.tail = LayerNormTail(env, "f_ln", "eps", index)
        self.rows_in = sem("f_rows_in")
        self.rows_set = sem("f_rows_set")
        self.xb_done = sem("f_xb_done")
        self.delta_up = sem("f_delta_up")
        self.w_sum = sem("f_w_sum")
        self.h_up = sem("f_h_up")
        self.h_act = sem("f_h_act")
        self.o_up = sem("f_o_up")
        self.y_done = sem("f_y_done")

    def sp(self, sp):
        env = self.env
        sp.wait_ge(env.x_done[self.index - 1], B)
        for kind, first in enumerate((1, 2, 9, 10)):
            sp.dma_start(self.rows[:, kind, :, :], env.X[first:first + 7:2, 0::NT, :]).then_inc(self.rows_in, 16)

    def pool(self, pool):
        env, w = self.env, self.w
        pool.memset(self.xb[:, :, :, :], 0.0).then_inc(self.y_done, PAIR)
        pool.memset(self.odd[:, :, :, :], 0.0).then_inc(self.delta_up, PAIR)
        pool.wait_ge(self.rows_in, 64)
        pool.wait_ge(self.delta_up, PAIR)
        blk = w("blk")[0:F_PAIRS]
        with pairs(pool) as it:
            for p in range(PAIR):
                b = it * PAIR + p
                row = lambda kind: self.rows[:, kind:kind + 1, bass.ds(b, 1), :].rearrange("p k a c -> p (k a c)")
                pool.wait_ge(self.delta_up, b + 1)
                for n in range(2):
                    pool.tensor_tensor(self.odd[:, p, n, :], row(2 * n + 1),
                                       w("scale")[0:F_PAIRS].broadcast_to([F_PAIRS, P]), ALU.mult)
                pool.tensor_tensor(self.e1[:, p, :, :], row(0).unsqueeze(1).broadcast_to([F_PAIRS, F_PAIRS, P]),
                                   blk.unsqueeze(2).broadcast_to([F_PAIRS, F_PAIRS, P]), ALU.mult)
                ev = row(2).rearrange("p (q r) -> p r q", r=F_BLOCKS)
                for r in range(F_BLOCKS):
                    q = P // F_PAIRS
                    ins = pool.tensor_tensor(
                        self.e2[:, p, r, :].rearrange("p (i q) -> p i q", i=F_PAIRS),
                        ev[:, r, :].unsqueeze(1).broadcast_to([F_PAIRS, F_PAIRS, q]),
                        blk.unsqueeze(2).broadcast_to([F_PAIRS, F_PAIRS, q]), ALU.mult)
                ins.then_inc(self.rows_set, 1)
                pool.wait_ge(self.y_done, b + 1)
                pool.tensor_tensor(self.xb[:, p, :, :], env.X[:, bass.ds(b * NT, NT), :],
                                   w("b2").unsqueeze(1).broadcast_to([P, NT, P]), ALU.add).then_inc(self.xb_done, 1)

    def pe(self, pe):
        env, w, PS = self.env, self.w, self.env.ps
        self.turned.pe(pe)
        pe.wait_ge(self.turned.ready, self.turned.all)
        with pairs(pe) as it:
            for p in range(PAIR):
                b = it * PAIR + p
                pe.wait_ge(self.rows_set, b + 1)
                pe.wait_ge(self.y_done, b + 1)
                pe.matmul(PS[:, 4 * p, :], self.odd[:, p, 0, :], self.e1[:, p, :, :], start=True, stop=True)
                pe.matmul(PS[:, 4 * p + 1, :], self.odd[:, p, 1, :], self.e2[:, p, :, :],
                          start=True, stop=True).then_inc(self.delta_up, 1)
            for p in range(PAIR):
                b = it * PAIR + p
                pe.wait_ge(self.w_sum, 2 * b + 1)
                for j in range(F_BLOCKS):
                    ins = pe.matmul(PS[:, 4 * p + 2 + j // 2, (j % 2) * T:(j % 2 + 1) * T],
                                    self.W1[:, p, j * P:(j + 1) * P], env.xT[:, bass.ds(b * T, T)],
                                    start=True, stop=True)
                ins.then_inc(self.h_up, 1)
            for p in range(PAIR):
                b = it * PAIR + p
                pe.wait_ge(self.w_sum, 2 * b + 2)
                pe.wait_ge(self.h_act, b + 1)
                for k in range(NT):
                    for r in range(F_BLOCKS):
                        ins = pe.matmul(PS[:, 4 * p, k * P:(k + 1) * P], self.h[:, p, r, k * P:(k + 1) * P],
                                        self.W2[:, p, r * P:(r + 1) * P], start=(r == 0), stop=(r == F_BLOCKS - 1))
                ins.then_inc(self.o_up, 1)

    def act(self, act):
        PS, w = self.env.ps, self.w
        self.turned.act(act)
        with pairs(act) as it:
            for p in range(PAIR):
                b = it * PAIR + p
                act.wait_ge(self.h_up, b + 1)
                for j in range(F_BLOCKS):
                    ins = act.activation(self.h[:, p, j, :], PS[:, 4 * p + 2 + j // 2, (j % 2) * T:(j % 2 + 1) * T],
                                         ACT.Gelu, bias=w("b1")[:, j:j + 1])
                ins.then_inc(self.h_act, 1)
            act.preload_act_table_set(EXP_LN)
            for p in range(PAIR):
                self.tail.root(act, it * PAIR + p, p)

    def dve(self, dve):
        env, w, PS = self.env, self.w, self.env.ps
        with pairs(dve) as it:
            for p in range(PAIR):
                b = it * PAIR + p
                dve.wait_ge(self.delta_up, b + 1 + PAIR)
                dve.tensor_tensor(self.W1[:, p, :], w("W1"), PS[:, 4 * p, :], ALU.add).then_inc(self.w_sum, 1)
                dve.tensor_tensor(self.W2[:, p, :], w("W2"), PS[:, 4 * p + 1, :], ALU.add).then_inc(self.w_sum, 1)
            for p in range(PAIR):
                b = it * PAIR + p
                dve.wait_ge(self.o_up, b + 1)
                dve.wait_ge(self.xb_done, b + 1)
                dve.tensor_tensor(self.y[:, p, :, :], self.xb[:, p, :, :],
                                  PS[:, 4 * p, 0:T].rearrange("p (k c) -> p k c", k=NT), ALU.add).then_inc(self.y_done, 1)
                dve.wait_ge(self.y_done, b + 1 + PAIR)
                self.tail.moments(dve, self.y[:, p, :, :], b, p)
            for p in range(PAIR):
                b = it * PAIR + p
                self.tail.apply(dve, lambda k: env.x_tile(b * NT + k), self.y[:, p, :, :], b, p, env.x_done[self.index])


R_HEADS, R_DH, R_HID = 16, 8, 256
R_UNITS = R_HEADS // 2
R_GROUP = 4
R_NORM_SHIFT = 20
R_SLOTS = R_GROUP * (32 + R_DH)


class GroupNorm:

    DVE_STEPS = 9

    def __init__(self, env, tag, w, names, before=None):
        self.env, self.w, self.names = env, w, names
        self.stats = env.sb(f"{tag}_stats", [P, B, 6])
        self.mv = env.sb(f"{tag}_mv", [P, B, 2])
        self.c = env.sb(f"{tag}_c", [P, 6, B])
        self.at = 1 if before else 0
        self.dve_step = before.dve_step if before else env.sem(f"{tag}_dve")
        self.pe_step = before.pe_step if before else env.sem(f"{tag}_pe")
        self.act_step = before.act_step if before else env.sem(f"{tag}_act")
        self.done = (self.at + 1) * self.DVE_STEPS

    def pe(self, pe, bank):
        PS, group = self.env.ps, self.w("group")
        pe.wait_ge(self.dve_step, self.at * self.DVE_STEPS + 2)
        pe.matmul(PS[:, bank, 0:B], group, self.mv[:, :, 0], start=True, stop=True).then_inc(self.pe_step, 1)
        pe.wait_ge(self.dve_step, self.at * self.DVE_STEPS + 5)
        pe.matmul(PS[:, bank, B:2 * B], group, self.c[:, 1, :], start=True, stop=True).then_inc(self.pe_step, 1)

    def act(self, act, bank):
        act.wait_ge(self.pe_step, 2 * self.at + 2)
        act.activation(self.c[:, 2, :], self.env.ps[:, bank, B:2 * B], ACT.Ln, bias=self.env.w0("eps")).then_inc(self.act_step, 1)
        act.wait_ge(self.act_step, 2 * self.at + 1)
        act.activation(self.c[:, 3, :], self.c[:, 2, :], ACT.Exp, scale=-0.5).then_inc(self.act_step, 1)

    def dve(self, dve, bank):
        env, w, (gamma, beta), c = self.env, self.w, self.names, self.c
        mu = env.ps[:, bank, 0:B]

        def step(ins, k):
            ins.then_inc(self.dve_step, 1)
            dve.wait_ge(self.dve_step, self.at * self.DVE_STEPS + k)

        for b in range(B):
            ins = dve.bn_stats(self.stats[:, b, :], env.xT[:, b * T:(b + 1) * T])
        step(ins, 1)
        for b in range(B):
            ins = dve.bn_aggr(self.mv[:, b, :], self.stats[:, b, :])
        step(ins, 2)
        dve.wait_ge(self.pe_step, 2 * self.at + 1)
        step(dve.tensor_tensor(c[:, 0, :], self.mv[:, :, 0], mu, ALU.subtract), 3)
        step(dve.tensor_tensor(c[:, 0, :], c[:, 0, :], c[:, 0, :], ALU.mult), 4)
        step(dve.tensor_tensor(c[:, 1, :], c[:, 0, :], self.mv[:, :, 1], ALU.add), 5)
        dve.wait_ge(self.act_step, 2 * self.at + 2)
        step(dve.tensor_scalar(c[:, 4, :], c[:, 3, :], w(gamma), None, ALU.mult), 6)
        step(dve.tensor_tensor(c[:, 5, :], c[:, 4, :], mu, ALU.mult), 7)
        step(dve.tensor_scalar(c[:, 5, :], c[:, 5, :], -1.0, w(beta), ALU.mult, ALU.add), 8)
        for b in range(B):
            x = env.xT[:, b * T:(b + 1) * T]
            ins = dve.tensor_scalar(x, x, c[:, 4, b:b + 1], c[:, 5, b:b + 1], ALU.mult, ALU.add)
        step(ins, 9)



class Retention(Sublayer):
    def __init__(self, env, w, index):
        self.env, self.w, self.index = env, w, index
        sb, sem = env.sb, env.sem
        self.turned = Turned(env, index)
        self.gn1 = GroupNorm(env, "r_g1", w, ("norm_g", "norm_b"))
        self.gn2 = GroupNorm(env, "r_g2", w, ("fnorm_g", "fnorm_b"), self.gn1)
        self.xn = sb("r_xn", [P, PAIR, T])
        self.qT = sb("r_qT", [P, PAIR, T])
        self.kT = sb("r_kT", [P, PAIR, T])
        self.sq = sb("r_sq", [P, PAIR, 2, T])
        self.ktok = sb("r_ktok", [P, PAIR, P])
        self.qm = sb("r_qm", [P, PAIR, R_GROUP, T])
        self.nn = sb("r_nn", [P, PAIR, 3, 2 * NT])
        self.V = sb("r_V", [P, PAIR, NT, R_GROUP, R_SLOTS])
        self.kv = sb("r_kv", [P, PAIR, P])
        self.Pm = sb("r_P", [P, 2, 4, P])
        self.yT = sb("r_yT", [P, PAIR, T])
        self.xob = sb("r_xob", [P, PAIR, NT, P])
        self.x2 = sb("r_x2", [P, PAIR, NT, P])
        self.h = sb("r_h", [P, PAIR, 2, T])
        self.y = sb("r_y", [P, PAIR, NT, P])
        self.tail = LayerNormTail(env, "r_ln", "eps", index)
        self.loaded = sem("r_loaded")
        self.proj_up = sem("r_proj_up")
        self.squared = sem("r_squared")
        self.nn_up = sem("r_nn_up")
        self.qm_done = sem("r_qm_done")
        self.nn_max = sem("r_nn_max")
        self.rooted = sem("r_rooted")
        self.v_done = sem("r_v_done")
        self.kv_up = sem("r_kv_up")
        self.kv_done = sem("r_kv_done")
        self.s_up = sem("r_s_up")
        self.p_done = sem("r_p_done")
        self.y_up = sem("r_y_up")
        self.yT_done = sem("r_yT_done")
        self.o_up = sem("r_o_up")
        self.xob_done = sem("r_xob_done")
        self.xb2_done = sem("r_xb2_done")
        self.x2_done = sem("r_x2_done")
        self.x2_up = sem("r_x2_up")
        self.x2T = sem("r_x2T")
        self.x2_add = sem("r_x2_add")
        self.h_up = sem("r_h_up")
        self.h_act = sem("r_h_act")
        self.f_up = sem("r_f_up")
        self.y_done = sem("r_y_done")

    def pool(self, pool):
        env, w = self.env, self.w
        pool.memset(self.xn[:, :, :], 0.0).then_inc(self.y_done, PAIR)
        pool.memset(self.V[:, :, :, :, :], 0.0).then_inc(self.x2_done, PAIR)
        pool.memset(self.kv[:, :, :], 0.0).then_inc(self.x2T, PAIR)
        pool.wait_ge(self.gn1.dve_step, self.gn1.done)
        pool.wait_ge(self.y_done, PAIR)
        row = lambda name: w(name).unsqueeze(1).broadcast_to([P, NT, P])
        with pairs(pool) as it:
            for p in range(PAIR):
                b = it * PAIR + p
                pool.wait_ge(self.x2_done, b + 1)
                pool.tensor_copy(self.xn[:, p, :], env.xT[:, bass.ds(b * T, T)]).then_inc(self.loaded, 1)
                pool.tensor_tensor(self.xob[:, p, :, :], env.X[:, bass.ds(b * NT, NT), :], row("ob"), ALU.add).then_inc(self.xob_done, 1)
        pool.wait_ge(self.x2_add, B)
        with pairs(pool) as it:
            for p in range(PAIR):
                b = it * PAIR + p
                pool.wait_ge(self.y_done, b + 1)
                pool.tensor_tensor(self.xob[:, p, :, :], env.X[:, bass.ds(b * NT, NT), :], row("b2"), ALU.add).then_inc(self.xb2_done, 1)

    def pe(self, pe):
        env, w, PS = self.env, self.w, self.env.ps
        self.turned.pe(pe)
        self.gn1.pe(pe, 0)

        def scores(b, p, u, n):
            for i in range(2):
                h = 2 * u + i
                r = slice(32 * (h // R_GROUP), 32 * (h // R_GROUP) + 32)
                for c in range(NT):
                    ins = pe.matmul(PS[:, n % 2, (2 * i + c) * P:(2 * i + c + 1) * P], self.kT[r, p, c * P:(c + 1) * P],
                                    self.qm[r, p, h % R_GROUP, c * P:(c + 1) * P], start=True, stop=True)
            ins.then_inc(self.s_up, 1)

        def mix(p, u, n, base):
            pe.wait_ge(self.p_done, base + n + 1)
            for i in range(2):
                h = 2 * u + i
                g, j = h // R_GROUP, h % R_GROUP
                for c in range(NT):
                    ins = pe.matmul(PS[32 * g:32 * g + 32, 6 + p, c * P:(c + 1) * P],
                                    self.V[:, p, c, g, 32 * j:32 * j + 32], self.Pm[:, n % 2, 2 * i + c, :],
                                    start=False, stop=(j == R_GROUP - 1), skip_group_check=True)
            if u == R_UNITS - 1:
                ins.then_inc(self.y_up, 1)

        with pairs(pe) as it:
            base = it * (PAIR * R_UNITS)
            for p in range(PAIR):
                b = it * PAIR + p
                pe.wait_ge(self.loaded, b + 1)
                for n, name in enumerate(("qw", "kw")):
                    pe.matmul(PS[:, 2 + p, n * T:(n + 1) * T], w(name), self.xn[:, p, :], start=True, stop=True)
                for k in range(NT):
                    pe.matmul(PS[:, 4 + p, k * P:(k + 1) * P], self.xn[:, p, k * P:(k + 1) * P], w("vw"),
                              start=True, stop=True)
                pe.matmul(PS[:, 4 + p, T:T + P], self.xn[:, p, 0:P], w("kw"), start=True, stop=True).then_inc(self.proj_up, 1)
            for p in range(PAIR):
                b = it * PAIR + p
                pe.wait_ge(self.squared, b + 1)
                pe.wait_ge(self.x2T, b + 1)
                for n in range(2 * NT):
                    ins = pe.matmul(PS[:, 6 + p, T + P + n:T + P + n + 1],
                                    self.sq[:, p, n // NT, n % NT * P:(n % NT + 1) * P], env.ones_row[:, 0:1],
                                    start=True, stop=True)
                ins.then_inc(self.nn_up, 1)
            for p in range(PAIR):
                b = it * PAIR + p
                pe.wait_ge(self.v_done, b + 1)
                pe.matmul(PS[:, 6 + p, T:T + P], self.ktok[:, p, :],
                          self.V[:, p, 0, :, :].rearrange("p g (j c) -> p g j c", j=R_GROUP)[:, :, :, 0:R_DH],
                          start=True, stop=True).then_inc(self.kv_up, 1)
                for u in range(R_UNITS):
                    n = p * R_UNITS + u
                    scores(b, p, u, n)
                    if u == 0:
                        if p:
                            mix(0, R_UNITS - 1, n - 1, base)
                        pe.wait_ge(self.kv_done, b + 1)
                        pe.matmul(PS[:, 6 + p, P:T], self.kv[:, p, :], self.qT[:, p, P:T],
                                  start=True, stop=False, skip_group_check=True)
                    else:
                        mix(p, u - 1, n - 1, base)
            mix(1, R_UNITS - 1, 2 * R_UNITS - 1, base)
            for p in range(PAIR):
                b = it * PAIR + p
                pe.wait_ge(self.yT_done, b + 1)
                for k in range(NT):
                    ins = pe.matmul(PS[:, 2 + p, k * P:(k + 1) * P], self.yT[:, p, k * P:(k + 1) * P], w("ow"),
                                    start=True, stop=True)
                ins.then_inc(self.o_up, 1)
            for p in range(PAIR):
                b = it * PAIR + p
                pe.wait_ge(self.x2_done, b + 1 + PAIR)
                for k in range(NT):
                    ins = pe.transpose(PS[:, 6 + p, k * P:(k + 1) * P], self.x2[:, p, k, :], env.ident)
                ins.then_inc(self.x2_up, 1)
        self.gn2.pe(pe, 0)
        pe.wait_ge(self.gn2.dve_step, self.gn2.done)
        with pairs(pe) as it:
            for p in range(PAIR):
                b = it * PAIR + p
                pe.wait_ge(self.y_done, b + 1)
                for j in range(2):
                    ins = pe.matmul(PS[:, p, j * T:(j + 1) * T], w("w1")[:, j * P:(j + 1) * P],
                                    env.xT[:, bass.ds(b * T, T)], start=True, stop=True)
                ins.then_inc(self.h_up, 1)
            for p in range(PAIR):
                b = it * PAIR + p
                pe.wait_ge(self.h_act, b + 1)
                for k in range(NT):
                    for j in range(2):
                        ins = pe.matmul(PS[:, 2 + p, k * P:(k + 1) * P], self.h[:, p, j, k * P:(k + 1) * P],
                                        w("w2")[:, j * P:(j + 1) * P], start=(j == 0), stop=(j == 1))
                ins.then_inc(self.f_up, 1)

    def act(self, act):
        env, w, PS = self.env, self.w, self.env.ps
        self.turned.act(act)
        act.preload_act_table_set(EXP_LN)
        self.gn1.act(act, 0)
        with pairs(act) as it:
            for p in range(PAIR):
                b = it * PAIR + p
                act.wait_ge(self.proj_up, b + 1)
                act.activation(self.sq[:, p, :, :], PS[:, 2 + p, :].rearrange("p (n t) -> p n t", n=2), ACT.Square)
                act.activation(self.kT[:, p, :], PS[:, 2 + p, T:2 * T], ACT.Copy)
                act.activation(self.qT[:, p, :], PS[:, 2 + p, 0:T], ACT.Copy)
                act.activation(self.ktok[:, p, :], PS[:, 4 + p, T:T + P], ACT.Copy).then_inc(self.squared, 1)
            for p in range(PAIR):
                b = it * PAIR + p
                act.wait_ge(self.nn_max, b + 1)
                act.activation(self.nn[:, p, 1, :], self.nn[:, p, 0, :], ACT.Ln, scale=2.0 ** R_NORM_SHIFT).then_inc(self.rooted, 1)
                act.wait_ge(self.rooted, 2 * b + 1)
                act.activation(self.nn[:, p, 2, :], self.nn[:, p, 1, :], ACT.Exp, scale=-0.5).then_inc(self.rooted, 1)
            for p in range(PAIR):
                b = it * PAIR + p
                act.wait_ge(self.x2_up, b + 1)
                act.activation(env.xT[:, bass.ds(b * T, T)], PS[:, 6 + p, 0:T], ACT.Copy).then_inc(self.x2T, 1)
        self.gn2.act(act, 0)
        with pairs(act) as it:
            for p in range(PAIR):
                b = it * PAIR + p
                act.wait_ge(self.h_up, b + 1)
                for j in range(2):
                    ins = act.activation(self.h[:, p, j, :], PS[:, p, j * T:(j + 1) * T], ACT.Silu, bias=w("b1")[:, j:j + 1])
                ins.then_inc(self.h_act, 1)
            act.preload_act_table_set(EXP_LN)
            for p in range(PAIR):
                self.tail.root(act, it * PAIR + p, p)

    def dve(self, dve):
        env, w, PS = self.env, self.w, self.env.ps
        dve.wait_ge(self.turned.ready, self.turned.all)
        self.gn1.dve(dve, 0)
        slots = lambda a: a.rearrange("p g (j c) -> p g j c", j=R_GROUP)[:, :, :, 0:R_DH]
        heads = lambda a: a.rearrange("p (g j c) -> p g j c", g=R_GROUP, j=R_GROUP)
        with pairs(dve) as it:
            base = it * (PAIR * R_UNITS)
            for p in range(PAIR):
                b = it * PAIR + p
                dve.wait_ge(self.squared, b + 1)
                for j in range(R_GROUP):
                    ins = dve.tensor_scalar(self.qm[:, p, j, :], self.qT[:, p, :], w("head_of")[:, j:j + 1], None, ALU.mult)
                ins.then_inc(self.qm_done, 1)
            for p in range(PAIR):
                b = it * PAIR + p
                dve.wait_ge(self.nn_up, b + 1)
                dve.tensor_scalar(self.nn[:, p, 0, :], PS[:, 6 + p, T + P:T + P + 2 * NT], 1e-24, None,
                                  ALU.max).then_inc(self.nn_max, 1)
            for p in range(PAIR):
                b = it * PAIR + p
                dve.wait_ge(self.rooted, 2 * b + 2)
                for c in range(NT):
                    ins = dve.scalar_tensor_tensor(
                        out=slots(self.V[:, p, c, :, :]), in0=heads(PS[:, 4 + p, c * P:(c + 1) * P]),
                        scalar=self.nn[:, p, 2, NT + c:NT + c + 1], in1=heads(w("v_decay")), op0=ALU.mult, op1=ALU.mult)
                ins.then_inc(self.v_done, 1)
            for p in range(PAIR):
                b = it * PAIR + p
                dve.wait_ge(self.kv_up, b + 1)
                dve.tensor_tensor(self.kv[:, p, :], PS[:, 6 + p, T:T + P], w("same_head"), ALU.mult).then_inc(self.kv_done, 1)
                for u in range(R_UNITS):
                    n = p * R_UNITS + u
                    dve.wait_ge(self.s_up, base + n + 1)
                    dve.tensor_tensor(self.Pm[:, n % 2, :, :], PS[:, n % 2, :].rearrange("p (a t) -> p a t", a=4),
                                      w("causal").unsqueeze(1).broadcast_to([P, 4, P]), ALU.mult).then_inc(self.p_done, 1)
                dve.wait_ge(self.y_up, b + 1)
                dve.tensor_tensor(self.yT[:, p, :], PS[:, 6 + p, 0:T], w("y_decay"), ALU.mult).then_inc(self.yT_done, 1)
            for p in range(PAIR):
                b = it * PAIR + p
                dve.wait_ge(self.o_up, b + 1)
                dve.wait_ge(self.xob_done, b + 1)
                for k in range(NT):
                    ins = dve.scalar_tensor_tensor(
                        out=self.x2[:, p, k, :], in0=PS[:, 2 + p, k * P:(k + 1) * P], scalar=self.nn[:, p, 2, k:k + 1],
                        in1=self.xob[:, p, k, :], op0=ALU.mult, op1=ALU.add)
                ins.then_inc(self.x2_done, 1)
                dve.wait_ge(self.x2_done, b + 1 + PAIR)
                X = env.X[:, bass.ds(b * NT, NT), :]
                dve.tensor_tensor(X, X, self.x2[:, p, :, :], ALU.add).then_inc(self.x2_add, 1)
            dve.wait_ge(self.x2_add, it * PAIR + PAIR)
        dve.wait_ge(self.x2T, B + PAIR)
        self.gn2.dve(dve, 0)
        with pairs(dve) as it:
            for p in range(PAIR):
                b = it * PAIR + p
                dve.wait_ge(self.f_up, b + 1)
                dve.wait_ge(self.xb2_done, b + 1)
                dve.tensor_tensor(self.y[:, p, :, :], PS[:, 2 + p, 0:T].rearrange("p (k c) -> p k c", k=NT),
                                  self.xob[:, p, :, :], ALU.add).then_inc(self.y_done, 1)
                dve.wait_ge(self.y_done, b + 1 + PAIR)
                self.tail.moments(dve, self.y[:, p, :, :], b, p)
            for p in range(PAIR):
                b = it * PAIR + p
                self.tail.apply(dve, lambda k: env.x_tile(b * NT + k), self.y[:, p, :, :], b, p, env.x_done[self.index])
            dve.wait_ge(env.x_done[self.index], it * PAIR + PAIR)


A_HEADS, A_DH = 16, 8
A_Q_PARTS, A_K_PARTS = (0, 1, 2, 0, 1, 0), (0, 0, 0, 1, 1, 2)
A_ROWS = len(A_Q_PARTS) * A_DH
A_STACKS = A_HEADS // 2
A_GROUP = 4
A_WINDOW = 64
A_CHUNKS = 4


class CrossAttention(Sublayer):
    def __init__(self, env, w, index):
        self.env, self.w, self.index = env, w, index
        sb, sem = env.sb, env.sem
        C = B * T // A_CHUNKS
        self.turned = Turned(env, index)
        self.proj = sb("a_proj", [P, 2, C])
        self.parts = sb("a_parts", [P, 2, 3, C], BF16)
        self.vtok = sb("a_vtok", [P, TILES, P])
        self.QS = sb("a_QS", [P, PAIR, A_STACKS, T], BF16)
        self.KS = sb("a_KS", [P, PAIR, A_STACKS, T], BF16)
        self.V = sb("a_V", [P, PAIR, NT, A_HEADS // A_GROUP, A_GROUP * (A_WINDOW + A_DH)])
        self.mx = sb("a_mx", [P, PAIR, 3, NT * A_HEADS])
        self.msplit = sb("a_msplit", [P, PAIR, NT, P // A_HEADS, A_HEADS], BF16)
        self.mrow = sb("a_mrow", [P, PAIR, T], BF16)
        self.selb = sb("a_selb", [P, A_HEADS, P], BF16)
        self.E = sb("a_E", [P, 2, NT, T])
        self.O = sb("a_O", [P, PAIR, 2, T])
        self.rec = sb("a_rec", [P, PAIR, 8, A_GROUP])
        self.ct = sb("a_ct", [P, PAIR, NT, P])
        self.cT = sb("a_cT", [P, PAIR, T])
        self.xb = sb("a_xb", [P, PAIR, NT, P])
        self.y = sb("a_y", [P, PAIR, NT, P])
        self.tail = LayerNormTail(env, "a_ln", "eps", index)
        self.proj_up = sem("a_proj_up")
        self.proj_done = sem("a_proj_done")
        self.vtok_up = sem("a_vtok_up")
        self.vtok_done = sem("a_vtok_done")
        self.split = sem("a_split")
        self.st_out = sem("a_st_out")
        self.st_in = [sem(f"a_st_in{p}") for p in range(PAIR)]
        self.v_set = sem("a_v_set")
        self.mx_up = sem("a_mx_up")
        self.mx_done = sem("a_mx_done")
        self.m_step = sem("a_m_step")
        self.mT_up = sem("a_mT_up")
        self.mT_done = sem("a_mT_done")
        self.s_up = sem("a_s_up")
        self.e_done = sem("a_e_done")
        self.pv_up = sem("a_pv_up")
        self.o_copy = sem("a_o_copy")
        self.ot_up = sem("a_ot_up")
        self.c_step = sem("a_c_step")
        self.ct_up = sem("a_ct_up")
        self.cT_done = sem("a_cT_done")
        self.w_up = sem("a_w_up")
        self.xb_done = sem("a_xb_done")
        self.y_done = sem("a_y_done")

    def sp(self, sp):
        env, st = self.env, self.env.st_dram
        elements = B // A_CHUNKS
        for m in range(2 * A_CHUNKS):
            kq, n = m // A_CHUNKS, m % A_CHUNKS
            sp.wait_ge(self.split, 4 * m + 4)
            for c, part in enumerate((A_K_PARTS, A_Q_PARTS)[kq]):
                sp.dma_start(st[kq, :, :, c, :, n * elements:(n + 1) * elements, :].rearrange("i r d b t -> (i r) d (b t)"),
                             self.parts[:, m % 2, part, :]).then_inc(self.st_out, 16)
            sp.wait_ge(self.st_out, 16 * 6 * (m + 1))
        with pairs(sp) as it:
            for p in range(PAIR):
                b = it * PAIR + p
                sp.wait_ge(self.y_done, b + 1)
                for kq, S in enumerate((self.KS, self.QS)):
                    for i in range(2):
                        src = st[kq, i, :, :, :, bass.ds(b, 1), :].rearrange("r c d a t -> (c d) r (a t)")
                        sp.dma_start(S[64 * i:64 * i + A_ROWS, p, :, :], src).then_inc(self.st_in[p], 16)

    def pool(self, pool):
        env, w = self.env, self.w
        flat = self.V[:, :, :, :, :].rearrange("p a c g v -> p (a c g) v")
        pool.memset(flat, 0.0).then_inc(self.y_done, PAIR)
        pool.memset(self.msplit[:, :, :, :, :], 0.0).then_inc(self.m_step, 1)
        pool.wait_ge(self.y_done, PAIR)
        slot = flat.rearrange("p n (j v) -> p n j v", j=A_GROUP)
        for n in range(0, PAIR * NT * (A_HEADS // A_GROUP), 4):
            ins = pool.memset(slot[:, n:n + 4, :, 32:32 + A_DH], 1.0)
        ins.then_inc(self.pv_up, 2)
        pool.tensor_copy(self.selb[:, :, :],
                         w("sel").unsqueeze(2).broadcast_to([P, A_HEADS, P])).then_inc(self.xb_done, 1)
        pool.wait_ge(self.vtok_done, 1)
        with pairs(pool) as it:
            for p in range(PAIR):
                b = it * PAIR + p
                pool.wait_ge(self.y_done, b + 1)
                for c in range(NT):
                    ins = pool.tensor_copy(
                        self.V[:, p, c, :, :].rearrange("p g (j v) -> p g j v", j=A_GROUP)[:, :, :, 0:A_DH],
                        self.vtok[:, bass.ds(b * NT + c, 1), :].rearrange("p a (g j e) -> p (a g) j e", g=A_HEADS // A_GROUP, j=A_GROUP))
                ins.then_inc(self.v_set, 1)
                pool.tensor_tensor(self.xb[:, p, :, :], env.X[:, bass.ds(b * NT, NT), :],
                                   w("bo").unsqueeze(1).broadcast_to([P, NT, P]), ALU.add).then_inc(self.xb_done, 1)

    def pe(self, pe):
        env, w, PS = self.env, self.w, self.env.ps
        C = B * T // A_CHUNKS
        self.turned.pe(pe)
        pe.wait_ge(env.ctx_in, 32)
        pe.wait_ge(self.turned.ready, self.turned.all)
        for m in range(2 * A_CHUNKS):
            kq, n = m // A_CHUNKS, m % A_CHUNKS
            if m >= 4:
                pe.wait_ge(self.proj_done, m - 3)
            pe.matmul(PS[:, m % 4, :], w(("wk", "wq")[kq]), (env.ctxT, env.xT)[kq][:, n * C:(n + 1) * C],
                      start=True, stop=True).then_inc(self.proj_up, 1)
        for t in range(TILES):
            ins = pe.matmul(PS[:, 4 + t // 4, t % 4 * P:(t % 4 + 1) * P], env.ctxT[:, t * P:(t + 1) * P], w("wv"),
                            start=True, stop=True)
        ins.then_inc(self.vtok_up, 1)
        pe.wait_ge(self.proj_done, 2 * A_CHUNKS)
        pe.wait_ge(self.vtok_done, 1)
        pe.wait_ge(self.xb_done, 1)

        def place(h):
            return slice(64 * (h // A_STACKS), 64 * (h // A_STACKS) + A_ROWS), h % A_STACKS

        def max_unit(p, h, base):
            k = p * A_HEADS + h
            rows, r = place(h)
            if k >= 2:
                pe.wait_ge(self.mx_done, base + k - 1)
            for c in range(NT):
                ins = pe.matmul(PS[:, k % 2, c * T:(c + 1) * T], self.QS[rows, p, r, c * P:(c + 1) * P],
                                self.KS[rows, p, r, :], start=True, stop=True)
            ins.then_inc(self.mx_up, 1)

        def turn_max(b, p):
            pe.wait_ge(self.m_step, 6 * b + 7)
            for c in range(NT):
                ins = pe.transpose(PS[:, 6 + p, :].bitcast(BF16)[:, c * P:(c + 1) * P],
                                   self.msplit[:, p, c, :, :].rearrange("p s h -> p (s h)"), env.identb)
            ins.then_inc(self.mT_up, 1)
            pe.wait_ge(self.mT_done, b + 1)

        def exp_unit(p, h):
            n = p * A_HEADS + h
            rows, r = place(h)
            S = PS[:, 2 + n % 2, :]
            for c in range(NT):
                pe.matmul(S[:, c * T:(c + 1) * T], self.KS[rows, p, r, c * P:(c + 1) * P], self.QS[rows, p, r, :],
                          start=(c == 0), stop=False, skip_group_check=True)
            pe.matmul(S, self.selb[rows, h, :], self.mrow[rows, p, :].unsqueeze(1).broadcast_to([A_ROWS, NT, T]),
                      start=False, stop=True, skip_group_check=True).then_inc(self.s_up, 1)

        def value_unit(p, h, base):
            n = p * A_HEADS + h
            g, j = h // A_GROUP, h % A_GROUP
            pe.wait_ge(self.e_done, base + n + 1)
            for c in range(NT):
                ins = pe.matmul(PS[64 * (g % 2):64 * (g % 2) + 64, 4 + p, (g // 2) * T:(g // 2 + 1) * T],
                                self.V[:, p, c, g, j * A_WINDOW:(j + 1) * A_WINDOW], self.E[:, n % 2, c, :],
                                start=(c == 0 and j == 0 and g < 2), stop=(c == 1 and j == A_GROUP - 1),
                                skip_group_check=True)
            ins.then_inc(self.pv_up, 1)

        with pairs(pe) as it:
            base = it * (PAIR * A_HEADS)
            pe.wait_ge(self.st_in[0], it * 64 + 64)
            for h in range(A_HEADS):
                max_unit(0, h, base)
            pe.wait_ge(self.st_in[1], it * 64 + 64)
            for p in range(PAIR):
                b = it * PAIR + p
                turn_max(b, p)
                pe.wait_ge(self.v_set, b + 1)
                exp_unit(p, 0)
                for h in range(A_HEADS):
                    if p == 0:
                        max_unit(1, h, base)
                    if h + 1 < A_HEADS:
                        exp_unit(p, h + 1)
                    value_unit(p, h, base)
            for p in range(PAIR):
                b = it * PAIR + p
                pe.wait_ge(self.o_copy, b + 1)
                for c in range(NT):
                    for g in range(2):
                        ins = pe.transpose(PS[:, 4 + p, (2 * c + g) * P:(2 * c + g + 1) * P],
                                           self.O[:, p, g, c * P:(c + 1) * P], env.ident)
                ins.then_inc(self.ot_up, 1)
            for p in range(PAIR):
                b = it * PAIR + p
                pe.wait_ge(self.c_step, 2 * b + 2)
                for c in range(NT):
                    ins = pe.transpose(PS[:, 6 + p, c * P:(c + 1) * P], self.ct[:, p, c, :], env.ident)
                ins.then_inc(self.ct_up, 1)
            for p in range(PAIR):
                b = it * PAIR + p
                pe.wait_ge(self.cT_done, b + 1)
                for c in range(NT):
                    ins = pe.matmul(PS[:, 6 + p, T + c * P:T + (c + 1) * P], self.cT[:, p, c * P:(c + 1) * P], w("wo"),
                                    start=True, stop=True)
                ins.then_inc(self.w_up, 1)

    def act(self, act):
        env, w, PS = self.env, self.w, self.env.ps
        self.turned.act(act)
        act.preload_act_table_set(EXP_LN)
        for m in range(2 * A_CHUNKS):
            act.wait_ge(self.proj_up, m + 1)
            if m >= 2:
                act.wait_ge(self.split, 4 * (m - 1))
            act.activation(self.proj[:, m % 2, :], PS[:, m % 4, :], ACT.Identity,
                           bias=w(("bk", "bq")[m // A_CHUNKS])).then_inc(self.proj_done, 1)
        with pairs(act) as it:
            base = it * (PAIR * A_HEADS)
            for p in range(PAIR):
                b = it * PAIR + p
                act.wait_ge(self.mT_up, b + 1)
                act.activation(self.mrow[:, p, :], PS[:, 6 + p, :].bitcast(BF16)[:, 0:T], ACT.Copy).then_inc(self.mT_done, 1)
                for h in range(A_HEADS):
                    n = p * A_HEADS + h
                    act.wait_ge(self.s_up, base + n + 1)
                    act.wait_ge(self.pv_up, base + n + 1)
                    act.activation(self.E[:, n % 2, :, :], PS[:, 2 + n % 2, :].rearrange("p (c t) -> p c t", c=NT),
                                   ACT.Exp, scale=A_DH ** -0.5).then_inc(self.e_done, 1)
                act.wait_ge(self.pv_up, base + (p + 1) * A_HEADS + 2)
                act.activation(self.O[:, p, :, :], PS[:, 4 + p, :].rearrange("p (g t) -> p g t", g=2),
                               ACT.Copy).then_inc(self.o_copy, 1)
            for p in range(PAIR):
                b = it * PAIR + p
                act.wait_ge(self.ct_up, b + 1)
                act.activation(self.cT[:, p, :], PS[:, 6 + p, 0:T], ACT.Copy).then_inc(self.cT_done, 1)
            for p in range(PAIR):
                self.tail.root(act, it * PAIR + p, p)

    def dve(self, dve):
        env, w, PS = self.env, self.w, self.env.ps
        n = 0

        def link(ins):
            nonlocal n
            n += 1
            ins.then_inc(self.split, 1)
            dve.wait_ge(self.split, n)

        for m in range(2 * A_CHUNKS):
            dve.wait_ge(self.proj_done, m + 1)
            if m >= 2:
                dve.wait_ge(self.st_out, 16 * 6 * (m - 1))
            x = self.proj[:, m % 2, :]
            parts = [self.parts[:, m % 2, i, :] for i in range(3)]
            split3(dve, link, parts, x, x)
        dve.wait_ge(self.vtok_up, 1)
        for i in range(4):
            ins = dve.tensor_tensor(self.vtok[:, 4 * i:4 * i + 4, :], PS[:, 4 + i, :].rearrange("p (k c) -> p k c", k=4),
                                    w("bv").unsqueeze(1).broadcast_to([P, 4, P]), ALU.add)
        ins.then_inc(self.vtok_done, 1)
        with pairs(dve) as it:
            base = it * (PAIR * A_HEADS)
            for p in range(PAIR):
                b = it * PAIR + p
                mx = self.mx[:, p, 0, :].rearrange("p (c h) -> p c h", c=NT)
                for h in range(A_HEADS):
                    k = p * A_HEADS + h
                    dve.wait_ge(self.mx_up, base + k + 1)
                    dve.tensor_reduce(mx[:, :, h], PS[:, k % 2, :].rearrange("p (c k) -> p c k", c=NT), AX.X,
                                      ALU.max).then_inc(self.mx_done, 1)

                def step(ins, k):
                    ins.then_inc(self.m_step, 1)
                    dve.wait_ge(self.m_step, 6 * b + k + 1)

                dve.wait_ge(self.mx_done, base + (p + 1) * A_HEADS)
                step(dve.tensor_scalar(self.mx[:, p, 1, :], self.mx[:, p, 0, :], -1.0, None, ALU.mult), 1)
                tiles = lambda i: self.mx[:, p, i, :].rearrange("p (c h) -> p c h", c=NT)
                parts = [self.msplit[:, p, :, i, :] for i in range(3)]
                step(dve.tensor_copy(parts[0], tiles(1)), 2)
                step(dve.tensor_tensor(tiles(2), tiles(1), parts[0], ALU.subtract), 3)
                step(dve.tensor_copy(parts[1], tiles(2)), 4)
                step(dve.tensor_tensor(parts[2], tiles(2), parts[1], ALU.subtract), 5)
                step(dve.tensor_copy(self.msplit[:, p, :, 4:7, :], self.msplit[:, p, :, 0:3, :]), 6)
            for p in range(PAIR):
                b = it * PAIR + p
                dve.wait_ge(self.ot_up, b + 1)
                O = PS[:, 4 + p, :].rearrange("p (n v) -> p n v", v=A_WINDOW)
                dve.reciprocal(self.rec[:, p, :, :], O[:, :, 32:64:A_DH]).then_inc(self.c_step, 1)
                dve.wait_ge(self.c_step, 2 * b + 1)
                dve.tensor_tensor(
                    self.ct[:, p, :, :].rearrange("p c (g j e) -> p (c g) j e", j=A_GROUP, e=A_DH),
                    O[:, :, 0:32].rearrange("p n (j e) -> p n j e", j=A_GROUP),
                    self.rec[:, p, :, :].unsqueeze(3).broadcast_to([P, 8, A_GROUP, A_DH]), ALU.mult).then_inc(self.c_step, 1)
            for p in range(PAIR):
                b = it * PAIR + p
                dve.wait_ge(self.w_up, b + 1)
                dve.wait_ge(self.xb_done, b + 2)
                dve.tensor_tensor(self.y[:, p, :, :], self.xb[:, p, :, :],
                                  PS[:, 6 + p, T:2 * T].rearrange("p (k c) -> p k c", k=NT), ALU.add).then_inc(self.y_done, 1)
                dve.wait_ge(self.y_done, b + 1 + PAIR)
                self.tail.moments(dve, self.y[:, p, :, :], b, p)
            for p in range(PAIR):
                b = it * PAIR + p
                self.tail.apply(dve, lambda k: env.x_tile(b * NT + k), self.y[:, p, :, :], b, p, env.x_done[self.index])


E_EXP, E_HID = 8, 256
E_HALVES = E_HID // P


class Experts(Sublayer):
    def __init__(self, env, w, index):
        self.env, self.w, self.index = env, w, index
        sb, sem = env.sb, env.sem
        self.turned = Turned(env, index)
        self.xs = sb("e_xs", [P, PAIR, T])
        self.lg = sb("e_lg", [P, TILES, E_EXP])
        self.top = sb("e_top", [P, TILES, E_EXP])
        self.topi = sb("e_topi", [P, TILES, E_EXP], U32)
        self.topf = sb("e_topf", [P, TILES, 2])
        self.col = sb("e_col", [P, 6, TILES])
        self.oh = sb("e_oh", [P, 2, TILES, E_EXP])
        self.gate = sb("e_gate", [P, TILES, E_EXP])
        self.gT = sb("e_gT", [E_EXP, TILES * P])
        self.h = sb("e_h", [P, 4, E_HALVES, T])
        self.acc = sb("e_acc", [P, TILES, P])
        self.inner = LayerNormTail(env, "e_in", "eps", None)
        self.z = sb("e_z", [P, PAIR, NT, P])
        self.tail = LayerNormTail(env, "e_ln", "eps", index)
        self.loaded = sem("e_loaded")
        self.lg_up = sem("e_lg_up")
        self.g_step = sem("e_g_step")
        self.g_exp = sem("e_g_exp")
        self.g_turned = sem("e_g_turned")
        self.g_rows = sem("e_g_rows")
        self.h_up = sem("e_h_up")
        self.h_act = sem("e_h_act")
        self.o_up = sem("e_o_up")
        self.mixed = sem("e_mixed")
        self.z_done = sem("e_z_done")

    G_STEPS = 11
    MIX_STEPS = E_EXP

    def pool(self, pool):
        env, w = self.env, self.w
        pool.memset(self.xs[:, :, :], 0.0).then_inc(self.o_up, PAIR * E_EXP)
        pool.wait_ge(self.turned.ready, self.turned.all)
        pool.wait_ge(self.o_up, PAIR * E_EXP)
        with pairs(pool) as it:
            for p in range(PAIR):
                b = it * PAIR + p
                pool.wait_ge(self.o_up, E_EXP * b + E_EXP)
                pool.tensor_copy(self.xs[:, p, :], env.xT[:, bass.ds(b * T, T)]).then_inc(self.loaded, 1)

    def pe(self, pe):
        env, w, PS = self.env, self.w, self.env.ps
        self.turned.pe(pe)
        pe.wait_ge(self.turned.ready, self.turned.all)
        for t in range(TILES):
            ins = pe.matmul(PS[:, 4, t * E_EXP:(t + 1) * E_EXP], env.xT[:, t * P:(t + 1) * P], w("Wg"),
                            start=True, stop=True)
        ins.then_inc(self.lg_up, 1)
        pe.wait_ge(self.g_step, self.G_STEPS)
        for t in range(TILES):
            ins = pe.transpose(PS[0:E_EXP, t // 4, t % 4 * P:(t % 4 + 1) * P], self.gate[:, t, :], env.ident)
        ins.then_inc(self.g_turned, 1)
        pe.wait_ge(self.g_rows, 1)
        for t in range(TILES):
            ins = pe.matmul(PS[:, 4 + t // 4, t % 4 * P:(t % 4 + 1) * P], self.gT[:, t * P:(t + 1) * P], w("b2")[0:E_EXP],
                            start=True, stop=True)
        ins.then_inc(self.g_turned, 1)

        def hidden(base, n):
            e, p = n % E_EXP, n // E_EXP
            if n >= 2:
                pe.wait_ge(self.h_act, base + n - 1)
            for j in range(E_HALVES):
                c = (e * E_HALVES + j) * P
                ins = pe.matmul(PS[:, n % 2, j * T:(j + 1) * T], w("W1")[:, c:c + P], self.xs[:, p, :],
                                start=True, stop=True)
            ins.then_inc(self.h_up, 1)

        def result(base, n, b):
            e, p = n % E_EXP, n // E_EXP
            pe.wait_ge(self.h_act, base + n + 1)
            if True:
                q = (n - 2) // E_EXP
                pe.wait_ge(self.mixed, self.MIX_STEPS * (b + q) + PAIR + 1 + (n - 2) % E_EXP)
            for k in range(NT):
                for j in range(E_HALVES):
                    c = (e * E_HALVES + j) * P
                    ins = pe.matmul(PS[:, 2 + n % 2, k * P:(k + 1) * P], self.h[:, n % 4, j, k * P:(k + 1) * P],
                                    w("W2")[:, c:c + P], start=(j == 0), stop=(j == E_HALVES - 1))
            ins.then_inc(self.o_up, 1)

        with pairs(pe) as it:
            b0 = it * PAIR
            base = it * (PAIR * E_EXP)
            for p in range(PAIR):
                b = b0 + p
                pe.wait_ge(self.loaded, b + 1)
            hidden(base, 0)
            hidden(base, 1)
            for n in range(2, PAIR * E_EXP):
                result(base, n - 2, b0)
                hidden(base, n)
            for n in range(PAIR * E_EXP - 2, PAIR * E_EXP):
                result(base, n, b0)

    def act(self, act):
        env, w, PS = self.env, self.w, self.env.ps
        self.turned.act(act)
        act.preload_act_table_set(EXP_LN)
        act.wait_ge(self.g_step, 3)
        act.activation(self.col[:, 1, :], self.col[:, 0, :], ACT.Exp).then_inc(self.g_exp, 1)
        act.wait_ge(self.g_turned, 1)
        for n in range(4):
            ins = act.activation(self.gT[:, n * 4 * P:(n + 1) * 4 * P], PS[0:E_EXP, n, :], ACT.Copy)
        ins.then_inc(self.g_rows, 1)
        with pairs(act) as it:
            base = it * (PAIR * E_EXP)

            def relu(n):
                act.wait_ge(self.h_up, base + n + 1)
                act.wait_ge(self.o_up, base + PAIR * E_EXP + n - 3)
                e = n % E_EXP
                for j in range(E_HALVES):
                    c = e * E_HALVES + j
                    ins = act.activation(self.h[:, n % 4, j, :], PS[:, n % 2, j * T:(j + 1) * T], ACT.Relu,
                                         bias=w("b1")[:, c:c + 1])
                ins.then_inc(self.h_act, 1)

            for n in range(PAIR * E_EXP):
                relu(n)
            for p in range(PAIR):
                self.inner.root(act, it * PAIR + p, p)
            for p in range(PAIR):
                self.tail.root(act, it * PAIR + p, p)

    def dve(self, dve):
        env, w, PS = self.env, self.w, self.env.ps
        def step(ins, k):
            ins.then_inc(self.g_step, 1)
            dve.wait_ge(self.g_step, k)

        bc = lambda a: a.unsqueeze(2).broadcast_to([P, TILES, E_EXP])
        col = lambda i: self.col[:, i, :]
        dve.wait_ge(self.lg_up, 1)
        step(dve.tensor_tensor(self.lg[:, :, :], PS[:, 4, 0:TILES * E_EXP].rearrange("p (t e) -> p t e", t=TILES),
                               w("bg").unsqueeze(1).broadcast_to([P, TILES, E_EXP]), ALU.add), 1)
        for t in range(TILES):
            ins = dve.max(self.top[:, t, :], self.lg[:, t, :])
        step(ins, 2)
        step(dve.tensor_tensor(col(0), self.top[:, :, 1], self.top[:, :, 0], ALU.subtract), 3)
        for t in range(TILES):
            ins = dve.max_index(self.topi[:, t, :], self.top[:, t, :], self.lg[:, t, :])
        step(ins, 4)
        step(dve.tensor_copy(self.topf[:, :, :], self.topi[:, :, 0:2]), 5)
        for i in range(2):
            ins = dve.tensor_tensor(self.oh[:, i, :, :], w("iota").unsqueeze(1).broadcast_to([P, TILES, E_EXP]),
                                    bc(self.topf[:, :, i]), ALU.is_equal)
        step(ins, 6)
        dve.wait_ge(self.g_exp, 1)
        step(dve.tensor_scalar(col(2), col(1), 1.0, None, ALU.add), 7)
        step(dve.reciprocal(col(3), col(2)), 8)
        dve.tensor_tensor(self.oh[:, 0, :, :], self.oh[:, 0, :, :], bc(col(3)), ALU.mult)
        step(dve.tensor_tensor(col(4), col(1), col(3), ALU.mult), 9)
        step(dve.tensor_tensor(self.oh[:, 1, :, :], self.oh[:, 1, :, :], bc(col(4)), ALU.mult), 10)
        step(dve.tensor_tensor(self.gate[:, :, :], self.oh[:, 1, :, :], self.oh[:, 0, :, :], ALU.add), 11)
        dve.wait_ge(self.g_turned, 2)
        for n in range(4):
            ins = dve.tensor_tensor(self.acc[:, 4 * n:4 * n + 4, :], env.X[:, 4 * n:4 * n + 4, :],
                                    PS[:, 4 + n, :].rearrange("p (k c) -> p k c", k=4), ALU.add)
        ins.then_inc(self.mixed, PAIR)
        with pairs(dve) as it:
            base = it * (PAIR * E_EXP)
            for n in range(PAIR * E_EXP):
                e, p = n % E_EXP, n // E_EXP
                b = it * PAIR + p
                acc = self.acc[:, bass.ds(b * NT, NT), :]
                gate = self.gate[:, bass.ds(b * NT, NT), :]
                dve.wait_ge(self.o_up, base + PAIR * E_EXP + n + 1)
                dve.wait_ge(self.mixed, self.MIX_STEPS * b + PAIR + e)
                for k in range(NT):
                    ins = dve.scalar_tensor_tensor(out=acc[:, k, :], in0=PS[:, 2 + n % 2, k * P:(k + 1) * P],
                                                   scalar=gate[:, k, e:e + 1], in1=acc[:, k, :],
                                                   op0=ALU.mult, op1=ALU.add)
                ins.then_inc(self.mixed, 1)
            for p in range(PAIR):
                b = it * PAIR + p
                dve.wait_ge(self.mixed, self.MIX_STEPS * b + self.MIX_STEPS + PAIR)
                self.inner.moments(dve, self.acc[:, bass.ds(b * NT, NT), :], b, p)
            for p in range(PAIR):
                b = it * PAIR + p
                z = self.z[:, p, :, :]
                self.inner.apply(dve, lambda k: z[:, k, :], self.acc[:, bass.ds(b * NT, NT), :], b, p, self.z_done)
                row = lambda name: w(name).unsqueeze(1).broadcast_to([P, NT, P])
                dve.wait_ge(self.z_done, 4 * b + 1)
                dve.tensor_tensor(z, z, row("gamma"), ALU.mult).then_inc(self.z_done, 1)
                dve.wait_ge(self.z_done, 4 * b + 2)
                dve.tensor_tensor(z, z, row("beta"), ALU.add).then_inc(self.z_done, 1)
                dve.wait_ge(self.z_done, 4 * b + 3)
                dve.tensor_tensor(z, z, env.X[:, bass.ds(b * NT, NT), :], ALU.add).then_inc(self.z_done, 1)
                dve.wait_ge(self.z_done, 4 * b + 4)
                self.tail.moments(dve, z, b, p)
            for p in range(PAIR):
                b = it * PAIR + p
                self.tail.apply(dve, lambda k: env.x_tile(b * NT + k), self.z[:, p, :, :], b, p, env.x_done[self.index])


SUBLAYERS = [Mamba, MLstm, Ffn, Retention, CrossAttention, Experts]


def program(nc, d, layouts, out):
    with ExitStack() as ctx:
        env = Env(nc, ctx)
        env.ps = ctx.enter_context(nc.psum_tensor("ps", [P, 8, 512], F32))
        env.X = env.sb("X", [P, TILES, P])
        env.xT = env.sb("xT", [P, B * T])
        env.ctxT = env.sb("ctxT", [P, B * T])
        env.ctok = env.sb("ctok", [P, TILES, P])
        env.m_dram = nc.dram_tensor("m_parts", (3, B, X_HEADS, T), BF16, kind="Internal").ap()
        env.st_dram = nc.dram_tensor("a_stacks", (2, 2, A_STACKS, len(A_Q_PARTS), A_DH, B, T), BF16, kind="Internal").ap()
        env.identb = env.sb("identb", [P, P], BF16)[:, :]
        w0, env.w0 = env.weights("w0", layouts["w0"])
        env.ident = env.w0("ident")[:, 0:P]
        env.ones_row = env.w0("ones")
        env.x_done = [env.sem(f"x_done{n}") for n in range(6)]
        env.w_in = [env.sem(f"w{n}_in") for n in range(7)]
        env.w1_in, env.w2_in = env.w_in[1], env.w_in[2]
        env.xT_in, env.x_in, env.ctx_in, stored = (env.sem(n) for n in ("xT_in", "x_in", "ctx_in", "stored"))
        env.ln_measured, env.ln_rooted = env.sem("ln_measured"), env.sem("ln_rooted")
        env.turned_up, env.turned_ready = env.sem("turned_up"), env.sem("turned_ready")
        arenas = [ctx.enter_context(nc.sbuf_tensor(f"arena{n}", [P, ARENA_WORDS[n]], F32)) for n in range(2)]
        layers, packed = [], []
        for n, kind in enumerate(SUBLAYERS):
            env.begin(arenas[n % 2][:, :])
            buf, w = env.weights(f"w{n + 1}", layouts[f"w{n + 1}"])
            packed.append((n, buf))
            layers.append(kind(env, w, n))
        env.arena = None
        block = ctx.enter_context(nc.Block())

        @block.sync
        def _(sp):
            sp.dma_start(packed[0][1], d[f"w{packed[0][0] + 1}"]).then_inc(env.w_in[packed[0][0] + 1], 16)
            sp.dma_start(w0[:, :], d["w0"]).then_inc(env.w_in[0], 16)
            sp.dma_start(env.xT[:, :], d["xT"]).then_inc(env.xT_in, 16)
            sp.dma_start(env.X[:, :, :], d["x"].rearrange("(t p) c -> p t c", p=P)).then_inc(env.x_in, 16)
            sp.dma_start(env.ctxT[:, :], d["ctxT"]).then_inc(env.ctx_in, 16)
            sp.dma_start(env.ctok[:, :, :], d["ctx"].rearrange("(t p) c -> p t c", p=P)).then_inc(env.ctx_in, 16)
            for m, layer in enumerate(layers):
                if m + 1 < len(layers):
                    n, buf = packed[m + 1]
                    if n >= 2:
                        sp.wait_ge(env.x_done[n - 2], B)
                    sp.dma_start(buf, d[f"w{n + 1}"]).then_inc(env.w_in[n + 1], 16)
                layer.sp(sp)
            sp.wait_ge(env.x_done[layers[-1].index], B)
            sp.dma_start(out.rearrange("(t p) c -> p t c", p=P), env.X[:, :, :]).then_inc(stored, 16)
            sp.wait_ge(stored, 16)

        @block.gpsimd
        def _(pool):
            for layer in layers:
                layer.begin(pool)
                layer.pool(pool)

        @block.tensor
        def _(pe):
            for layer in layers:
                layer.begin(pe)
                layer.pe(pe)

        @block.scalar
        def _(act):
            for layer in layers:
                layer.begin(act)
                layer.act(act)

        @block.vector
        def _(dve):
            for layer in layers:
                layer.begin(dve)
                layer.dve(dve)


def pack(parts):
    import numpy as np
    at, places, cols = 0, {}, []
    for name, a in parts:
        a = np.asarray(a, np.float32)
        a = a.reshape(a.shape[0], -1)
        full = np.zeros((P, a.shape[1]), np.float32)
        full[:a.shape[0]] = a
        places[name] = (at, at + a.shape[1])
        at += a.shape[1]
        cols.append(full)
    places["_size"] = at
    return np.ascontiguousarray(np.concatenate(cols, axis=1)), places


def lay_out(i):
    import numpy as np
    eye = np.eye(P, dtype=np.float32)
    rows = lambda a: np.tile(np.asarray(a).reshape(1, -1), (P, 1))
    cols = lambda a, n=P: np.ascontiguousarray(np.asarray(a).reshape(-1, n).T)
    tiles = lambda a: np.asarray(a).reshape(-1, P, a.shape[-1]).transpose(1, 0, 2)
    sel = np.zeros((M_SPLIT, M_HEADS, M_HEADS, P), np.float32)
    for h in range(M_HEADS):
        sel[:, h, h, :] = 1.0
    w0, l0 = pack([("ident", np.concatenate([eye, 0 * eye], 1)), ("ones", np.ones((P, T))),
                   ("eps", np.full((P, 1), LN_EPS)), ("eps_quarter", np.full((P, 1), LN_EPS / 4))])
    w1, l1 = pack([
        ("W_in", i["L0_attn_W_in"]), 
        ("conv_w", tiles(i["L0_attn_conv_w"])), ("conv_b", cols(i["L0_attn_conv_b"])),
        ("dt_bias", rows(i["L0_attn_dt_bias"])), ("A_log", rows(i["L0_attn_A_log"])),
        ("D", cols(np.repeat(i["L0_attn_D"], M_HEAD))), ("norm_w", cols(i["L0_attn_norm_w"])),
        ("W_out", tiles(i["L0_attn_W_out"])), ("sel_decay", sel.reshape(M_SPLIT * M_HEADS, -1)),
    ])
    head = np.arange(P) // X_DH

    def windowed(a):
        z = np.zeros((P, 2, (B - 1) * X_HEADS), np.float32)
        return np.concatenate([z, a.T.reshape(P, 2, X_HEADS), z], 2)

    gw = i["L0_xattn_ifgate_w"]
    w2, l2 = pack([
        ("gate_q", windowed(gw[:, 0:P])), ("gate_k", windowed(gw[:, P:2 * P])), ("gate_v", windowed(gw[:, 2 * P:])),
        ("gate_b", np.tile(i["L0_xattn_ifgate_b"].reshape(2, 1, X_HEADS), (1, B, 1)).reshape(P, 1)),
        ("sel", np.tile(np.eye(X_HEADS), (3, 1))), ("future", np.tril(np.full((P, P), -30000.0), -1)),
        ("head_par", np.stack([(head % 2 == n) * X_DH ** -0.5 for n in range(2)], 1)),
        ("same_head", np.repeat(head[:, None] == np.arange(X_HEADS)[None, :], X_SLOT, 1) * X_DH ** -0.5),
        ("outnorm", rows(i["L0_xattn_outnorm_w"])),
    ])
    w3, l3 = pack([
        ("W1", i["L0_ffn_W1"].T), ("W2", i["L0_ffn_W2"].reshape(P, F_BLOCKS, P).transpose(2, 1, 0)),
        ("b1", cols(i["L0_ffn_b1"])), ("b2", rows(i["L0_ffn_b2"])), ("scale", rows(i["L0_ffn_scale"])),
        ("blk", np.eye(F_PAIRS)),
    ])
    gam = np.float32(1) - np.exp(np.linspace(np.log(1 / 32), np.log(1 / 512), R_HEADS, dtype=np.float32))
    lg = np.repeat(np.log(gam.astype(np.float64)), R_DH)
    tt = np.arange(P)
    comp = 2.0 ** (R_NORM_SHIFT // 2)
    rhead = np.arange(P) // R_DH
    same = (rhead[:, None] == rhead[None, :])
    w4, l4 = pack([
        ("qw", i["L1_attn_qw"].T), ("kw", i["L1_attn_kw"].T), ("vw", i["L1_attn_vw"].T), ("ow", i["L1_attn_ow"].T),
        ("w1", i["L1_attn_w1"].T), ("w2", i["L1_attn_w2"].T.reshape(2, P, P).transpose(1, 0, 2)),
        ("b1", cols(i["L1_attn_b1"])), ("ob", rows(i["L1_attn_ob"])), ("b2", rows(i["L1_attn_b2"])),
        ("norm_g", cols(i["L1_attn_norm_g"])), ("norm_b", cols(i["L1_attn_norm_b"])),
        ("fnorm_g", cols(i["L1_attn_ffn_norm_g"])), ("fnorm_b", cols(i["L1_attn_ffn_norm_b"])),
        ("group", same / R_DH),
        ("head_of", rhead[:, None] % R_GROUP == np.arange(R_GROUP)[None, :]),
        ("v_decay", comp * np.exp(-lg[None, :] * tt[:, None])),
        ("same_head", same * np.exp(P * lg)[None, :]),
        ("y_decay", np.tile(R_DH ** -0.5 * comp * np.exp(lg[:, None] * tt[None, :]), (1, NT))),
        ("causal", np.triu(np.ones((P, P)))),
    ])
    w5, l5 = pack([
        ("wq", i["L1_xattn_wq"].T), ("wk", i["L1_xattn_wk"].T), ("wv", i["L1_xattn_wv"].T), ("wo", i["L1_xattn_wo"].T),
        ("bq", cols(i["L1_xattn_bq"])), ("bk", cols(i["L1_xattn_bk"])), ("bv", rows(i["L1_xattn_bv"])),
        ("bo", rows(i["L1_xattn_bo"])), ("sel", np.tile(np.eye(A_HEADS), (P // A_HEADS, 1))),
    ])
    w6, l6 = pack([
        ("Wg", i["L1_ffn_Wg"]), ("bg", rows(i["L1_ffn_bg"])), ("W1", i["L1_ffn_W1"].transpose(1, 0, 2)),
        ("b1", cols(i["L1_ffn_b1"])), ("W2", i["L1_ffn_W2"].reshape(E_EXP * E_HALVES, P, P).transpose(1, 0, 2)),
        ("b2", i["L1_ffn_b2"]), ("gamma", rows(i["L1_ffn_gamma"])), ("beta", rows(i["L1_ffn_beta"])),
        ("iota", rows(np.arange(E_EXP))),
    ])
    x, ctx = i["x"].reshape(B * T, P), i["ctx_1024"].reshape(B * T, P)
    return ({"w0": w0, "w1": w1, "w2": w2, "w3": w3, "w4": w4, "w5": w5, "w6": w6, "xT": np.ascontiguousarray(x.T), "x": x, "ctxT": np.ascontiguousarray(ctx.T), "ctx": ctx},
            {"w0": l0, "w1": l1, "w2": l2, "w3": l3, "w4": l4, "w5": l5, "w6": l6})


def kernel(**inputs):
    import numpy as np
    import concourse.bacc as bacc
    from concourse.bass_utils import run_bass_kernel_spmd

    nc = bacc.Bacc("TRN2", target_bir_lowering=False, num_devices=1)
    arrays, layouts = lay_out({k: np.asarray(v) for k, v in inputs.items()})
    arrays = {f"in_{k}": np.ascontiguousarray(a) for k, a in arrays.items()}
    d = {k[3:]: nc.dram_tensor(k, a.shape, mybir.dt.from_np(a.dtype), kind="ExternalInput").ap()
         for k, a in arrays.items()}
    out = nc.dram_tensor("out", (B * T, P), F32, kind="ExternalOutput").ap()
    program(nc, d, layouts, out)
    r = run_bass_kernel_spmd(nc, [arrays], core_ids=[0])
    return r.results[0]["out"].reshape(B, T, P)
```

```python
from contextlib import ExitStack

import concourse.bass as bass
from concourse import mybir

F32 = mybir.dt.float32
BF16 = mybir.dt.bfloat16
U32 = mybir.dt.uint32
ACT = mybir.ActivationFunctionType
ALU = mybir.AluOpType
AX = mybir.AxisListType

P = 128
B = 8
T = 256
NT = T // P
TILES = B * NT
PAIR = 2
LN_EPS = 1e-5

ARENA_WORDS = 79 * 256, 76 * 256
EXP_LN = "natural_log_exp_and_others"


class Env:

    def __init__(self, nc, ctx):
        self.nc, self.ctx = nc, ctx
        self.arena, self.used = None, 0

    def begin(self, arena):
        self.arena, self.used = arena, 0

    def sb(self, name, shape, dt=F32):
        if self.arena is None:
            return self.ctx.enter_context(self.nc.sbuf_tensor(name, shape, dt))
        n = 1
        for s in shape[1:]:
            n *= s
        words = n if dt != BF16 else (n + 1) // 2
        part = self.arena[0:shape[0], self.used:self.used + words]
        self.used += (words + 7) // 8 * 8
        if self.used > self.arena.shape[1]:
            raise ValueError(f"arena is full at {name}")
        if dt != F32:
            part = part.bitcast(dt)[:, 0:n]
        names = "abcde"[:len(shape) - 1]
        if len(names) > 1:
            part = part.rearrange(f"p ({' '.join(names)}) -> p {' '.join(names)}", **dict(zip(names, shape[1:])))
        return part

    def weights(self, name, layout):
        buf = self.sb(name, [P, layout["_size"]])
        return buf, lambda part: buf[:, layout[part][0]:layout[part][1]]

    def x_tile(self, t):
        return self.X[:, bass.ds(t, 1), :].rearrange("p a c -> p (a c)")

    def sem(self, name):
        return self.ctx.enter_context(self.nc.semaphore(name))


class Sublayer:
    def begin(self, eng):
        if self.index >= 2:
            eng.wait_ge(self.env.x_done[self.index - 2], B)
        eng.wait_ge(self.env.w_in[0], 16)
        eng.wait_ge(self.env.w_in[self.index + 1], 16)

    def sp(self, sp):
        pass


def pairs(eng):
    return eng.Fori(0, B // PAIR)


def elements(eng, element):
    for p in range(PAIR):
        element(p, p, p == 0, False)
    with eng.Fori(1, B // PAIR - 1) as it:
        for p in range(PAIR):
            element(it * PAIR + p, p, False, False)
    for p in range(PAIR):
        element(B - PAIR + p, p, False, p == PAIR - 1)


class LayerNormTail:

    def __init__(self, env, tag, index):
        self.env, self.eps = env, env.w0("eps")[:, 0:1]
        self.stats = env.sb(f"{tag}_stats", [P, PAIR, NT, 6])
        self.mv = env.sb(f"{tag}_mv", [P, PAIR, NT, 2])
        self.lnv = env.sb(f"{tag}_lnv", [P, PAIR, NT])
        self.rstd = env.sb(f"{tag}_rstd", [P, PAIR, NT])
        if index is None:
            self.base = 0
            self.measured = env.sem(f"{tag}_measured")
            self.rooted = env.sem(f"{tag}_rooted")
        else:
            self.base = 2 * B * index
            self.measured, self.rooted = env.ln_measured, env.ln_rooted

    def moments(self, dve, y, b, p):
        both = 2 * b + self.base + 1
        if not isinstance(b, int):
            both = dve.compute_val(both)
        for k in range(NT):
            ins = dve.bn_stats(self.stats[:, p, k, :], y[:, k, :])
        ins.then_inc(self.measured, 1)
        dve.wait_ge(self.env.w_in[0], 16)
        dve.wait_ge(self.measured, both)
        for k in range(NT):
            ins = dve.bn_aggr(self.mv[:, p, k, :], self.stats[:, p, k, :])
        ins.then_inc(self.measured, 1)

    def root(self, act, b, p):
        act.wait_ge(self.measured, 2 * b + self.base + 2)
        act.activation(self.lnv[:, p, :], self.mv[:, p, :, 1], ACT.Ln, bias=self.eps).then_inc(self.rooted, 1)
        act.wait_ge(self.rooted, 2 * b + self.base + 1)
        act.activation(self.rstd[:, p, :], self.lnv[:, p, :], ACT.Exp, scale=-0.5).then_inc(self.rooted, 1)

    def root_pool(self, pool, b, p):
        pool.wait_ge(self.measured, 2 * b + self.base + 2)
        pool.tensor_tensor(self.lnv[:, p, :], self.mv[:, p, :, 1], self.env.w0("eps"), ALU.add).then_inc(self.rooted, 1)
        pool.wait_ge(self.rooted, 2 * b + self.base + 1)
        pool.tensor_tensor(self.rstd[:, p, :], self.lnv[:, p, :], self.env.w0("minus_half"), ALU.pow).then_inc(self.rooted, 1)

    def apply(self, dve, out, y, b, p, done):
        dve.wait_ge(self.rooted, 2 * b + self.base + 2)
        for k in range(NT):
            ins = dve.tensor_scalar(out(k), y[:, k, :], self.mv[:, p, k, 0:1], self.rstd[:, p, k:k + 1],
                                    ALU.subtract, ALU.mult)
        ins.then_inc(done, 1)


def log1p_half(dve, link, out, e, a, b):
    link(dve.tensor_scalar(a, e, 2.0, None, ALU.add))
    link(dve.reciprocal(b, a))
    link(dve.tensor_tensor(a, e, b, ALU.mult))
    link(dve.tensor_tensor(b, a, a, ALU.mult))
    link(dve.tensor_scalar(out, b, 1.0 / 15, None, ALU.mult))
    for odd in (13, 11, 9, 7, 5, 3):
        link(dve.scalar_tensor_tensor(out=out, in0=out, scalar=1.0 / odd, in1=b, op0=ALU.add, op1=ALU.mult))
    link(dve.scalar_tensor_tensor(out=out, in0=out, scalar=1.0, in1=a, op0=ALU.add, op1=ALU.mult))


def split3(dve, link, parts, x, rest):
    link(dve.tensor_copy(parts[0], x))
    link(dve.tensor_tensor(rest, x, parts[0], ALU.subtract))
    link(dve.tensor_copy(parts[1], rest))
    link(dve.tensor_tensor(parts[2], rest, parts[1], ALU.subtract))


M_INNER, M_STATE, M_HEADS, M_HEAD, M_TAPS = 256, 128, 4, 64, 4
M_CONV = M_INNER + 2 * M_STATE
M_SPLIT = 3
M_EPS = 1e-5


class Mamba(Sublayer):
    DT_ABS, DT_RATE, DT_SPLIT = 3, 19, 23

    def __init__(self, env, w, index):
        self.env, self.w, self.index = env, w, index
        sb, sem = env.sb, env.sem
        self.dt = sb("m_dt", [P, TILES, M_HEADS])
        self.dtv = sb("m_dtv", [P, 10, TILES * M_HEADS])
        self.arate = sb("m_arate", [P, 2, M_HEADS])
        self.dsplit = sb("m_dsplit", [P, TILES, M_SPLIT * M_HEADS], BF16)
        self.drows = sb("m_drows", [M_SPLIT * M_HEADS, TILES * P], BF16)
        self.selb = sb("m_selb", [M_SPLIT * M_HEADS, M_HEADS, P], BF16)
        self.wout = sb("m_wout", [P, 2, P])
        self.zs = sb("m_zs", [P, PAIR, 2, T])
        self.u = sb("m_u", [P, PAIR, 4, T + M_TAPS - 1])
        self.conv = sb("m_conv", [P, PAIR, 4, T])
        self.xbc = sb("m_xbc", [P, PAIR, 4, T])
        self.xdt = sb("m_xdt", [P, PAIR, NT, M_INNER])
        self.L0 = sb("m_L0", [P, PAIR, M_HEADS, T])
        self.L1 = sb("m_L1", [P, PAIR, M_HEADS, P])
        self.g = sb("m_g", [P, PAIR, 2, T])
        self.sq = sb("m_sq", [P, PAIR, 2, T])
        self.sqs = sb("m_sqs", [P, PAIR, T])
        self.junk = sb("m_junk", [P, PAIR, NT, P])
        self.su = sb("m_su", [P, PAIR, NT])
        self.tot = sb("m_tot", [P, PAIR, 2, NT])
        self.r = sb("m_r", [P, PAIR, NT])
        self.x2 = sb("m_x2", [P, PAIR, NT, P])
        self.y = sb("m_y", [P, PAIR, NT, P])
        self.tail = LayerNormTail(env, "m_ln", index)

        self.cast = sem("m_cast")
        self.wscaled = sem("m_wscaled")
        self.dt_raw = sem("m_dt_raw")
        self.dt_step = sem("m_dt_step")
        self.dt_exp = sem("m_dt_exp")
        self.dt_turned = sem("m_dt_turned")
        self.dt_rows = sem("m_dt_rows")
        self.z_up = sem("m_z_up")
        self.u_up = sem("m_u_up")
        self.z_act = sem("m_z_act")
        self.u_copy = sem("m_u_copy")
        self.conv_tap = sem("m_conv_tap")
        self.xbc_act = sem("m_xbc_act")
        self.x_turned = sem("m_x_turned")
        self.g_up = sem("m_g_up")
        self.d_up = sem("m_d_up")
        self.xdt_done = sem("m_xdt_done")
        self.scanned = sem("m_scanned")
        self.masked = sem("m_masked")
        self.y_up = sem("m_y_up")
        self.gated = sem("m_gated")
        self.squared = sem("m_squared")
        self.sq_sum = sem("m_sq_sum")
        self.x_twice = sem("m_x_twice")
        self.o_up = sem("m_o_up")
        self.o_sq = sem("m_o_sq")
        self.o_tot = sem("m_o_tot")
        self.o_root = sem("m_o_root")
        self.y_done = sem("m_y_done")

    def pool(self, pool):
        env, w = self.env, self.w
        pool.memset(self.u[:, :, :, 0:M_TAPS - 1], 0.0).then_inc(self.y_done, PAIR)
        pool.tensor_copy(env.identb, env.ident)
        pool.tensor_copy(self.selb[:, :, :], w("sel_decay")[0:M_SPLIT * M_HEADS].rearrange("p (h m) -> p h m", h=M_HEADS)).then_inc(self.cast, 1)
        for hp in range(2):
            ins = pool.tensor_scalar(self.wout[:, hp, :], w("W_out")[:, hp * P:(hp + 1) * P],
                                     w("norm_w")[:, hp:hp + 1], None, ALU.mult)
        ins.then_inc(self.wscaled, 1)
        pool.wait_ge(env.x_in, 16)
        with pairs(pool) as it:
            for p in range(PAIR):
                b = it * PAIR + p
                pool.wait_ge(self.y_done, b + 1)
                pool.tensor_tensor(self.x2[:, p, :, :], env.X[:, bass.ds(b * NT, NT), :], env.X[:, bass.ds(b * NT, NT), :],
                                   ALU.add).then_inc(self.x_twice, 1)
            for p in range(PAIR):
                b = it * PAIR + p
                pool.wait_ge(self.squared, b + 1)
                pool.tensor_tensor(self.sqs[:, p, :], self.sq[:, p, 0, :], self.sq[:, p, 1, :],
                                   ALU.add).then_inc(self.sq_sum, 1)
            for p in range(PAIR):
                b = it * PAIR + p
                pool.wait_ge(self.o_tot, 2 * b + 2)
                pool.tensor_tensor(self.r[:, p, :], self.tot[:, p, 1, :], env.w0("minus_half"), ALU.pow).then_inc(self.o_root, 1)
            for p in range(PAIR):
                self.tail.root_pool(pool, it * PAIR + p, p)

    def pe(self, pe):
        env, w, PS = self.env, self.w, self.env.ps
        pe.wait_ge(env.xT_in, 16)
        for t in range(TILES):
            ins = pe.matmul(PS[:, 0, t * M_HEADS:(t + 1) * M_HEADS], env.xT[:, t * P:(t + 1) * P],
                            w("W_in")[:, M_INNER + M_CONV:], start=True, stop=True)
        ins.then_inc(self.dt_raw, 1)
        pe.wait_ge(self.cast, 1)
        pe.wait_ge(self.dt_step, self.DT_SPLIT)
        for t in range(TILES):
            dst = PS[0:M_SPLIT * M_HEADS, 1 + t // 8, :].bitcast(BF16)[:, (t % 8) * P:(t % 8 + 1) * P]
            ins = pe.transpose(dst, self.dsplit[:, t, :], env.identb)
        ins.then_inc(self.dt_turned, 1)
        pe.wait_ge(self.dt_rows, 1)
        def front(b, p):
            rhs = env.xT[:, bass.ds(b * T, T)]
            for j in range(4):
                ins = pe.matmul(PS[:, 4 * p + 1 + j // 2, (j % 2) * T:(j % 2 + 1) * T],
                                w("W_in")[:, (2 + j) * P:(3 + j) * P], rhs, start=True, stop=True)
            ins.then_inc(self.u_up, 1)

        def body(it, last):
            for p in range(PAIR):
                b = it * PAIR + p
                k0 = 4 * p
                rhs = env.xT[:, bass.ds(b * T, T)]
                for j in range(2):
                    ins = pe.matmul(PS[:, k0, j * T:(j + 1) * T], w("W_in")[:, j * P:(j + 1) * P], rhs,
                                    start=True, stop=True)
                ins.then_inc(self.z_up, 1)
            for p in range(PAIR):
                b = it * PAIR + p
                k0 = 4 * p
                pe.wait_ge(self.xbc_act, b + 1)
                pe.wait_ge(self.y_done, b + 1)
                for k in range(NT):
                    for j in range(2):
                        ins = pe.transpose(PS[:, k0 + 3, k * M_INNER + j * P:k * M_INNER + (j + 1) * P],
                                           self.xbc[:, p, j, k * P:(k + 1) * P], env.ident)
                ins.then_inc(self.x_turned, 1)
                for h in range(M_HEADS):
                    ins = pe.matmul(PS[:, k0 + 1 + h // 2, (h % 2) * T:(h % 2 + 1) * T], self.selb[:, h, :],
                                    self.drows[:, bass.ds(b * T, T)], start=True, stop=True)
                ins.then_inc(self.d_up, 1)
                pe.wait_ge(self.z_act, b + 1)
                pe.matmul(PS[:, k0, 0:T], self.xbc[:, p, 2, 0:P], self.xbc[:, p, 3, :], start=True, stop=True)
                pe.matmul(PS[:, k0, T:T + P], self.xbc[:, p, 2, P:T], self.xbc[:, p, 3, P:T],
                          start=True, stop=True).then_inc(self.g_up, 1)
            for p in range(PAIR):
                b = it * PAIR + p
                k0 = 4 * p
                pe.wait_ge(self.xdt_done, b + 1)
                pe.wait_ge(self.masked, b + 1)
                for pair in range(M_HEADS // 2):
                    for k in range(NT):
                        for h in (2 * pair, 2 * pair + 1):
                            out = PS[(h % 2) * M_HEAD:(h % 2 + 1) * M_HEAD, k0 + 3, pair * T + k * P:(pair + 1) * T]
                            L = (self.L0, self.L1)[k]
                            ins = pe.matmul(out, self.xdt[:, p, k, h * M_HEAD:(h + 1) * M_HEAD], L[:, p, h, :],
                                            start=(k == 0), stop=(k == 1))
                ins.then_inc(self.y_up, 1)
                if not last:
                    front(b + PAIR, p)
            for p in range(PAIR):
                b = it * PAIR + p
                k0 = 4 * p
                pe.wait_ge(self.wscaled, 1)
                pe.wait_ge(self.gated, 3 * b + 3)
                for k in range(NT):
                    for hp in range(2):
                        pe.matmul(PS[:, k0 + 3, k * P:(k + 1) * P], self.g[:, p, hp, k * P:(k + 1) * P],
                                  self.wout[:, hp, :], start=(hp == 0), stop=(hp == 1))
                pe.wait_ge(self.sq_sum, b + 1)
                for k in range(NT):
                    ins = pe.matmul(PS[:, k0 + 3, T + k:T + k + 1], self.sqs[:, p, k * P:(k + 1) * P],
                                    env.ones_row[:, 0:1], start=True, stop=True)
                ins.then_inc(self.o_up, 1)

        for p in range(PAIR):
            front(p, p)
        with pe.Fori(0, B // PAIR - 1) as it:
            body(it, False)
        body(B // PAIR - 1, True)

    def act(self, act):
        env, w, PS = self.env, self.w, self.env.ps
        act.preload_act_table_set(EXP_LN)
        act.wait_ge(self.dt_step, self.DT_ABS)
        act.activation(self.dtv[:, 2, :], self.dtv[:, 1, :], ACT.Exp, scale=-1.0).then_inc(self.dt_exp, 1)
        act.activation(self.arate[:, 1, :], self.arate[:, 0, :], ACT.Exp).then_inc(self.dt_exp, 1)
        act.wait_ge(self.dt_step, self.DT_RATE)
        act.activation(self.dtv[:, 1, :], self.dtv[:, 6, :], ACT.Exp).then_inc(self.dt_exp, 1)
        act.wait_ge(self.dt_turned, 1)
        for n in range(2):
            ins = act.activation(self.drows[:, n * 8 * P:(n + 1) * 8 * P], PS[0:M_SPLIT * M_HEADS, 1 + n, :].bitcast(BF16),
                                 ACT.Copy)
        ins.then_inc(self.dt_rows, 1)
        def front(b, p):
            act.wait_ge(self.u_up, b + 1)
            for n in range(2):
                act.activation(self.u[:, p, 2 * n:2 * n + 2, M_TAPS - 1:],
                               PS[:, 4 * p + 1 + n, :].rearrange("p (j t) -> p j t", j=2), ACT.Copy)
            for j in range(4):
                ins = act.activation(self.conv[:, p, j, :], PS[:, 4 * p + 1 + j // 2, (j % 2) * T:(j % 2 + 1) * T],
                                     ACT.Identity, scale=w("conv_w")[:, j * M_TAPS + 3:j * M_TAPS + 4],
                                     bias=w("conv_b")[:, j:j + 1])
            ins.then_inc(self.u_copy, 1)

        def body(it, last):
            for p in range(PAIR):
                b = it * PAIR + p
                act.wait_ge(self.z_up, b + 1)
                act.activation(self.zs[:, p, :, :], PS[:, 4 * p, :].rearrange("p (j t) -> p j t", j=2),
                               ACT.Silu).then_inc(self.z_act, 1)
                act.wait_ge(self.conv_tap, 3 * b + 3)
                act.activation(self.xbc[:, p, :, :], self.conv[:, p, :, :], ACT.Silu).then_inc(self.xbc_act, 1)
            for p in range(PAIR):
                b = it * PAIR + p
                if not last:
                    front(b + PAIR, p)
                act.wait_ge(self.gated, 3 * b + 3)
                act.activation(self.sq[:, p, :, :], self.g[:, p, :, :], ACT.Square).then_inc(self.squared, 1)
            for p in range(PAIR):
                b = it * PAIR + p
                act.wait_ge(self.o_up, b + 1)
                for k in range(NT):
                    ins = act.activation(self.junk[:, p, k, :], PS[:, 4 * p + 3, k * P:(k + 1) * P], ACT.Square,
                                         accum_out=self.su[:, p, k:k + 1])
                ins.then_inc(self.o_sq, 1)

        for p in range(PAIR):
            front(p, p)
        with act.Fori(0, B // PAIR - 1) as it:
            body(it, False)
        body(B // PAIR - 1, True)

    def dve(self, dve):
        env, w, PS = self.env, self.w, self.env.ps
        n = 0

        def link(ins):
            nonlocal n
            n += 1
            ins.then_inc(self.dt_step, 1)
            dve.wait_ge(self.dt_step, n)

        v = [self.dtv[:, i, :] for i in range(10)]
        dt = self.dt[:, :, :].rearrange("p t h -> p (t h)")
        tiles = lambda a: a.rearrange("p (t h) -> p t h", h=M_HEADS)
        per_head = lambda a: a.unsqueeze(1).broadcast_to([P, TILES, M_HEADS])
        dve.wait_ge(self.dt_raw, 1)
        link(dve.tensor_tensor(tiles(v[0]), tiles(PS[:, 0, 0:TILES * M_HEADS]), per_head(w("dt_bias")), ALU.add))
        link(dve.tensor_scalar(self.arate[:, 0, :], w("A_log"), 88.0, None, ALU.min))
        link(dve.scalar_tensor_tensor(out=v[1], in0=v[0], scalar=-1.0, in1=v[0], op0=ALU.mult, op1=ALU.max))
        assert n == self.DT_ABS
        dve.wait_ge(self.dt_exp, 2)
        log1p_half(dve, link, v[5], v[2], v[3], v[4])
        link(dve.tensor_scalar(v[8], v[0], 0.0, None, ALU.max))
        link(dve.scalar_tensor_tensor(out=dt, in0=v[5], scalar=2.0, in1=v[8], op0=ALU.mult, op1=ALU.add))
        link(dve.tensor_tensor(tiles(v[5]), self.dt[:, :, :], per_head(self.arate[:, 1, :]), ALU.mult))
        link(dve.tensor_scalar(v[6], v[5], -1.0, -200.0, ALU.mult, ALU.max))
        assert n == self.DT_RATE, n
        dve.wait_ge(self.dt_exp, 3)
        parts = [self.dsplit[:, :, i * M_HEADS:(i + 1) * M_HEADS] for i in range(M_SPLIT)]
        split3(dve, link, parts, tiles(v[1]), tiles(v[7]))
        assert n == self.DT_SPLIT
        dve.wait_ge(env.x_in, 16)

        def front(b, p):
            dve.wait_ge(self.u_copy, b + 1)
            for tap in range(M_TAPS - 1):
                for j in range(4):
                    ins = dve.scalar_tensor_tensor(
                        out=self.conv[:, p, j, :], in0=self.u[:, p, j, tap:tap + T],
                        scalar=w("conv_w")[:, j * M_TAPS + tap:j * M_TAPS + tap + 1], in1=self.conv[:, p, j, :],
                        op0=ALU.mult, op1=ALU.add)
                ins.then_inc(self.conv_tap, 1)
                dve.wait_ge(self.conv_tap, 3 * b + tap + 1)

        def body(it, last):
            for p in range(PAIR):
                b = it * PAIR + p
                k0 = 4 * p
                dve.wait_ge(self.x_turned, b + 1)
                for k in range(NT):
                    ins = dve.tensor_tensor(
                        self.xdt[:, p, k, :].rearrange("p (h c) -> p h c", h=M_HEADS),
                        PS[:, k0 + 3, k * M_INNER:(k + 1) * M_INNER].rearrange("p (h c) -> p h c", h=M_HEADS),
                        self.dt[:, bass.ds(b * NT + k, 1), :].rearrange("p a h -> p (a h)").unsqueeze(2).broadcast_to([P, M_HEADS, M_HEAD]),
                        ALU.mult)
                ins.then_inc(self.xdt_done, 1)
                dve.wait_ge(self.d_up, b + 1)
                for h in range(M_HEADS):
                    row = PS[:, k0 + 1 + h // 2, (h % 2) * T:(h % 2 + 1) * T]
                    dve.tensor_tensor_scan(self.L0[:, p, h, :], row, env.w0("ident"), 0.0, ALU.mult, ALU.add)
                    ins = dve.tensor_tensor_scan(self.L1[:, p, h, :], row[:, P:T], env.ident, 0.0,
                                                 ALU.mult, ALU.add)
                ins.then_inc(self.scanned, 1)
                dve.wait_ge(self.g_up, b + 1)
                dve.wait_ge(self.scanned, b + 1)
                dve.tensor_tensor(self.L0[:, p, :, :], self.L0[:, p, :, :],
                                  PS[:, k0, 0:T].unsqueeze(1).broadcast_to([P, M_HEADS, T]), ALU.mult)
                dve.tensor_tensor(self.L1[:, p, :, :], self.L1[:, p, :, :],
                                  PS[:, k0, T:T + P].unsqueeze(1).broadcast_to([P, M_HEADS, P]),
                                  ALU.mult).then_inc(self.masked, 1)
            for p in range(PAIR):
                b = it * PAIR + p
                dve.wait_ge(self.y_up, b + 1)
                for hp in range(2):
                    ins = dve.scalar_tensor_tensor(
                        out=self.g[:, p, hp, :], in0=self.xbc[:, p, hp, :], scalar=w("D")[:, hp:hp + 1],
                        in1=PS[:, 4 * p + 3, hp * T:(hp + 1) * T], op0=ALU.mult, op1=ALU.add)
                ins.then_inc(self.gated, 2)
                dve.wait_ge(self.gated, 3 * b + 2)
                dve.tensor_tensor(self.g[:, p, :, :], self.g[:, p, :, :], self.zs[:, p, :, :],
                                  ALU.mult).then_inc(self.gated, 1)
            if not last:
                front(it * PAIR + PAIR, 0)
            for p in range(PAIR):
                b = it * PAIR + p
                dve.wait_ge(self.o_sq, b + 1)
                dve.tensor_scalar(self.tot[:, p, 0, :], PS[:, 4 * p + 3, T:T + NT], M_EPS / M_INNER, M_EPS * M_EPS,
                                  ALU.mult, ALU.add).then_inc(self.o_tot, 1)
                dve.wait_ge(self.o_tot, 2 * b + 1)
                dve.scalar_tensor_tensor(out=self.tot[:, p, 1, :], in0=self.su[:, p, :], scalar=1.0 / P,
                                         in1=self.tot[:, p, 0, :], op0=ALU.mult, op1=ALU.add).then_inc(self.o_tot, 1)
            if not last:
                front(it * PAIR + PAIR + 1, 1)
            for p in range(PAIR):
                b = it * PAIR + p
                dve.wait_ge(self.x_twice, b + 1)
                dve.wait_ge(self.o_root, b + 1)
                for k in range(NT):
                    ins = dve.scalar_tensor_tensor(
                        out=self.y[:, p, k, :], in0=PS[:, 4 * p + 3, k * P:(k + 1) * P], scalar=self.r[:, p, k:k + 1],
                        in1=self.x2[:, p, k, :], op0=ALU.mult, op1=ALU.add)
                ins.then_inc(self.y_done, 1)
                dve.wait_ge(self.y_done, b + 1 + PAIR)
                self.tail.moments(dve, self.y[:, p, :, :], b, p)
            for p in range(PAIR):
                b = it * PAIR + p
                self.tail.apply(dve, lambda k: env.x_tile(b * NT + k), self.y[:, p, :, :], b, p, env.x_done[0])

        for p in range(PAIR):
            front(p, p)
        with dve.Fori(0, B // PAIR - 1) as it:
            body(it, False)
        body(B // PAIR - 1, True)


class Turned:

    def __init__(self, env, index):
        self.env, self.source = env, index - 1
        self.base = B * (index - 1)
        self.up = env.turned_up
        self.ready = env.turned_ready
        self.all = self.base + B

    def pe(self, pe):
        env = self.env
        for b in range(B):
            pe.wait_ge(env.x_done[self.source], b + 1)
            if b >= 2:
                pe.wait_ge(self.ready, self.base + b - 1)
            for k in range(NT):
                ins = pe.transpose(env.ps[:, b % 2, k * P:(k + 1) * P], env.X[:, b * NT + k, :], env.ident)
            ins.then_inc(self.up, 1)

    def act(self, act):
        env = self.env
        for b in range(B):
            act.wait_ge(self.up, self.base + b + 1)
            act.activation(env.xT[:, b * T:(b + 1) * T], env.ps[:, b % 2, 0:T], ACT.Copy).then_inc(self.ready, 1)


X_HEADS, X_DH = 8, 16
X_SLOT = 32
X_UNITS = X_HEADS // 2
X_CAP, X_DEN_EPS, X_NORM_EPS = 15.0, 5e-5, 1e-6


class MLstm(Sublayer):
    CH_CAP, CH_ABS, CH_LF, CH_M, CH_SPLIT = 3, 4, 19, 23, 27

    def __init__(self, env, w, index):
        self.env, self.w, self.index = env, w, index
        sb, sem = env.sb, env.sem
        R = B * X_HEADS
        self.turned = Turned(env, index)
        self.cap = sb("x_cap", [P, T])
        self.rows = sb("x_rows", [R, 12, T])
        self.bcol = sb("x_bcol", [P, 1])
        self.split = sb("x_split", [R, 3, T], BF16)
        self.mrows = sb("x_mrows", [3 * X_HEADS, B, T], BF16)
        self.cols = sb("x_cols", [P, 6, R])
        self.selb = sb("x_selb", [3 * X_HEADS, X_HEADS, P], BF16)
        self.gkv = sb("x_gkv", [P, 2 * (2 * B - 1) * X_HEADS])
        self.maskb = sb("x_maskb", [P, P], BF16)
        self.kT = sb("x_kT", [P, PAIR, T])
        self.ktok = sb("x_ktok", [P, PAIR, P])
        self.xTs = sb("x_xTs", [P, PAIR, P])
        self.abias = sb("x_abias", [P, PAIR, NT, X_HEADS])
        self.V = sb("x_V", [P, PAIR, NT, X_HEADS, X_SLOT])
        self.wV = sb("x_wV", [P, PAIR, X_HEADS, X_SLOT])
        self.q = sb("x_q", [P, PAIR, 2, T])
        self.E = sb("x_E", [P, 2, 4, P])
        self.Pm = sb("x_P", [P, 2, 4, P])
        self.kv = sb("x_kv", [P, PAIR, T])
        self.O = sb("x_O", [P, PAIR, 2, T])
        self.CB = sb("x_CB", [P, PAIR, NT, X_HEADS, X_SLOT])
        self.tmp = sb("x_tmp", [P, PAIR, X_HEADS, X_SLOT])
        self.sq = sb("x_sq", [P, PAIR, NT, P])
        self.den = sb("x_den", [P, PAIR, 6, NT * X_HEADS])
        self.y = sb("x_y", [P, PAIR, NT, P])
        self.tail = LayerNormTail(env, "x_ln", index)

        self.consts = sem("x_consts")
        self.g_up = sem("x_g_up")
        self.chain = sem("x_chain")
        self.chain_act = sem("x_chain_act")
        self.m_out = sem("x_m_out")
        self.m_in = sem("x_m_in")
        self.c_up = sem("x_c_up")
        self.c_done = sem("x_c_done")
        self.loaded = sem("x_loaded")
        self.v_done = sem("x_v_done")
        self.q_done = sem("x_q_done")
        self.kv_up = sem("x_kv_up")
        self.kv_done = sem("x_kv_done")
        self.inter_up = sem("x_inter_up")
        self.s_up = sem("x_s_up")
        self.e_done = sem("x_e_done")
        self.p_done = sem("x_p_done")
        self.o_up = sem("x_o_up")
        self.o_copy = sem("x_o_copy")
        self.to_up = sem("x_to_up")
        self.to_copy = sem("x_to_copy")
        self.inter_read = sem("x_inter_read")
        self.comb = sem("x_comb")
        self.out = sem("x_out")
        self.rooted = sem("x_rooted")

    def sp(self, sp):
        sp.wait_ge(self.chain, self.CH_SPLIT)
        sp.dma_start(self.env.m_dram.rearrange("s b h t -> (b h) s t"), self.split[:, :, :]).then_inc(self.m_out, 16)
        sp.wait_ge(self.m_out, 16)
        for s in range(3):
            sp.dma_start(self.mrows[s * X_HEADS:(s + 1) * X_HEADS, :, :],
                         self.env.m_dram[s].rearrange("b h t -> h b t")).then_inc(self.m_in, 16)

    def pool(self, pool):
        env, w = self.env, self.w
        flat = self.V[:, :, :, :, :].rearrange("p a k h v -> p (a k h) v")
        pool.memset(flat[:, :, X_DH:X_SLOT], 0.0).then_inc(self.o_up, PAIR)
        pool.wait_ge(self.o_up, PAIR)
        pool.memset(flat[:, :, X_DH:X_DH + 1], 1.0).then_inc(self.inter_read, 1)
        pool.tensor_tensor(self.gkv[:, :], w("gate_k"), w("gate_v"), ALU.add).then_inc(self.to_copy, 1)
        pool.tensor_copy(self.maskb[:, :], w("future"))
        pool.tensor_copy(self.selb[:, :, :],
                         w("sel")[0:3 * X_HEADS].unsqueeze(2).broadcast_to([3 * X_HEADS, X_HEADS, P])).then_inc(self.consts, 1)
        pool.wait_ge(env.ctx_in, 32)
        pool.wait_ge(self.c_done, 1)
        pool.wait_ge(self.turned.ready, self.turned.all)

        def load(b, p):
            pool.wait_ge(self.o_up, b + 1)
            pool.tensor_copy(self.kT[:, p, :], env.ctxT[:, bass.ds(b * T, T)])
            pool.tensor_copy(self.ktok[:, p, :], env.ctok[:, bass.ds(b * NT, 1), :].rearrange("p a c -> p (a c)"))
            pool.tensor_copy(self.xTs[:, p, :], env.xT[:, bass.ds(b * T + P, P)])
            pool.tensor_copy(self.abias[:, p, :, :],
                             self.cols[:, 0:2, bass.ds(b * X_HEADS, X_HEADS)]).then_inc(self.loaded, 1)
            for k in range(NT):
                ins = pool.tensor_copy(
                    self.V[:, p, k, :, 0:X_DH],
                    env.ctok[:, bass.ds(b * NT + k, 1), :].rearrange("p a (h c) -> p (a h) c", h=X_HEADS))
            ins.then_inc(self.v_done, 1)
            pool.wait_ge(self.v_done, 2 * b + 1)
            pool.tensor_tensor(
                self.wV[:, p, :, :], self.V[:, p, 0, :, :],
                self.cols[:, 4:5, bass.ds(b * X_HEADS, X_HEADS)].rearrange("p a h -> p (a h)").unsqueeze(2)
                    .broadcast_to([P, X_HEADS, X_SLOT]), ALU.mult).then_inc(self.v_done, 1)

        with pairs(pool) as it:
            for p in range(PAIR):
                load(it * PAIR + p, p)

    def pe(self, pe):
        env, w, PS = self.env, self.w, self.env.ps
        pe.wait_ge(env.ctx_in, 32)
        self.turned.pe(pe)
        lo = (B - 1) * X_HEADS
        R = B * X_HEADS
        pe.wait_ge(self.turned.ready, self.turned.all)
        pe.wait_ge(self.to_copy, 1)
        for b in range(B):
            win = slice(lo - b * X_HEADS, lo - b * X_HEADS + R)
            for g in range(2):
                gates = lambda a: a.rearrange("p (g c) -> p g c", g=2)[:, g, win]
                out = PS[g * R:(g + 1) * R, 0, 0:T]
                pe.matmul(out, gates(w("gate_q")), env.xT[:, b * T:(b + 1) * T], start=(b == 0), stop=False)
                ins = pe.matmul(out, gates(self.gkv[:, :]), env.ctxT[:, b * T:(b + 1) * T],
                                start=False, stop=(b == B - 1))
        ins.then_inc(self.g_up, 1)
        pe.wait_ge(self.chain_act, 5)
        for n, (row, k) in enumerate(((5, 0), (5, 1), (8, 0), (8, 1), (9, 0), (10, 1))):
            ins = pe.transpose(PS[:, 1, n * R:(n + 1) * R], self.rows[:, row, k * P:(k + 1) * P],
                               env.ident[0:R, 0:R])
        ins.then_inc(self.c_up, 1)
        pe.wait_ge(self.m_in, 48)
        pe.wait_ge(self.c_done, 1)
        pe.wait_ge(self.consts, 1)

        def scores(b, p, u):
            S, D = PS[:, u % 2, :], PS[:, 2 + u % 2, :]
            if u == 0:
                pe.wait_ge(self.loaded, b + 1)
                pe.wait_ge(self.q_done, b + 1)
            for i in range(2):
                r = slice(X_SLOT * u, X_SLOT * u + X_SLOT)
                for c in range(NT):
                    pe.matmul(S[:, (2 * i + c) * P:(2 * i + c + 1) * P], self.kT[r, p, c * P:(c + 1) * P],
                              self.q[r, p, i, c * P:(c + 1) * P], start=True, stop=True)
            for i in range(2):
                pe.matmul(D[:, i * T:(i + 1) * T], self.selb[:, 2 * u + i, :],
                          self.mrows[:, bass.ds(b, 1), :].rearrange("p a t -> p (a t)"),
                          start=(i == 0), stop=False, skip_group_check=True)
            pe.matmul(D, env.identb, self.maskb[:, :].unsqueeze(1).broadcast_to([P, 4, P]),
                      start=False, stop=True, skip_group_check=True).then_inc(self.s_up, 1)

        def mix(b, p, u):
            pe.wait_ge(self.p_done, X_UNITS * b + u + 1)
            for c in range(NT):
                for i in range(2):
                    h = 2 * u + i
                    q4 = h % 4
                    ins = pe.matmul(PS[X_SLOT * q4:X_SLOT * (q4 + 1), 4 + p, (h // 4) * T + c * P:(h // 4) * T + (c + 1) * P],
                                    self.V[:, p, c, h, :], self.Pm[:, u % 2, 2 * i + c, :], start=True, stop=True)
            if u == X_UNITS - 1:
                ins.then_inc(self.o_up, 1)

        def turn(b, p):
            pe.wait_ge(self.o_copy, b + 1)
            pe.wait_ge(self.to_copy, b + 1)
            for c in range(NT):
                for g in range(2):
                    ins = pe.transpose(PS[:, 6, (2 * c + g) * P:(2 * c + g + 1) * P],
                                       self.O[:, p, g, c * P:(c + 1) * P], env.ident)
            ins.then_inc(self.to_up, 1)

        def element(b, p, first, last):
            for u in range(X_UNITS):
                scores(b, p, u)
                if u == 0:
                    pe.wait_ge(self.v_done, 2 * b + 2)
                    pe.wait_ge(self.inter_read, b + 1)
                    pe.matmul(PS[:, 7, 0:T], self.ktok[:, p, :], self.wV[:, p, :, :], start=True, stop=True).then_inc(self.kv_up, 1)
                    if not first:
                        mix(b - 1, 1 - p, X_UNITS - 1)
                else:
                    mix(b, p, u - 1)
                if u == 1:
                    pe.wait_ge(self.kv_done, b + 1)
                    pe.matmul(PS[:, 7, T:2 * T], self.xTs[:, p, :], self.kv[:, p, :],
                              start=True, stop=True).then_inc(self.inter_up, 1)
                    if not first:
                        turn(b - 1, 1 - p)

        elements(pe, element)
        mix(B - 1, 1, X_UNITS - 1)
        turn(B - 1, 1)

    def act(self, act):
        env, w, PS = self.env, self.w, self.env.ps
        R = B * X_HEADS
        self.turned.act(act)
        act.wait_ge(self.g_up, 1)
        act.wait_ge(self.chain, 1)
        act.activation(self.cap[:, :], PS[:, 0, 0:T], ACT.Tanh, scale=1.0 / X_CAP, bias=self.bcol[:, 0:1]).then_inc(self.chain_act, 1)
        act.preload_act_table_set(EXP_LN)
        act.wait_ge(self.chain, self.CH_ABS)
        act.activation(self.rows[:, 2, :], self.rows[:, 1, :], ACT.Exp, scale=-1.0).then_inc(self.chain_act, 1)
        act.wait_ge(self.chain, self.CH_M)
        act.activation(self.rows[:, 8, :], self.rows[:, 7, :], ACT.Exp, scale=-1.0).then_inc(self.chain_act, 1)
        act.activation(self.rows[:, 9, 0:P], self.rows[:, 5, 0:P], ACT.Exp, bias=self.rows[:, 11, P - 1:P]).then_inc(self.chain_act, 1)
        act.activation(self.rows[:, 10, P:T], self.rows[:, 11, P:T], ACT.Exp, bias=self.rows[:, 6, P - 1:P]).then_inc(self.chain_act, 1)

        def copy_mixed(b, p):
            act.wait_ge(self.o_up, b + 1 + PAIR)
            act.activation(self.O[:, p, :, :], PS[:, 4 + p, :].rearrange("p (g t) -> p g t", g=2),
                           ACT.Copy).then_inc(self.o_copy, 1)

        def copy_turned(b, p):
            act.wait_ge(self.to_up, b + 1)
            act.activation(self.CB[:, p, :, :, :].rearrange("p c h v -> p (c h v)"), PS[:, 6, :], ACT.Copy).then_inc(self.to_copy, 1)

        def root(b, p):
            act.wait_ge(self.comb, 8 * b + 8)
            act.activation(self.den[:, p, 4, :], self.den[:, p, 3, :], ACT.Ln).then_inc(self.rooted, 1)
            act.wait_ge(self.rooted, 2 * b + 1)
            act.activation(self.den[:, p, 5, :], self.den[:, p, 4, :], ACT.Exp, scale=-0.5).then_inc(self.rooted, 1)

        def element(b, p, first, last):
            for u in range(X_UNITS):
                act.wait_ge(self.s_up, X_UNITS * b + u + 1)
                for i in range(2):
                    for c in range(NT):
                        ins = act.activation(self.E[:, u % 2, 2 * i + c, :],
                                             PS[:, 2 + u % 2, (2 * i + c) * P:(2 * i + c + 1) * P], ACT.Exp,
                                             bias=self.abias[:, p, c, 2 * u + i:2 * u + i + 1])
                ins.then_inc(self.e_done, 1)
                if u == 0 and not first:
                    copy_mixed(b - 1, 1 - p)
                    if not (isinstance(b, int) and b == 1):
                        self.tail.root(act, b - 2, p)
                if u == 2 and not first:
                    copy_turned(b - 1, 1 - p)
            if not first:
                root(b - 1, 1 - p)

        elements(act, element)
        copy_mixed(B - 1, 1)
        self.tail.root(act, B - 2, 0)
        copy_turned(B - 1, 1)
        root(B - 1, 1)
        self.tail.root(act, B - 1, 1)

    def dve(self, dve):
        env, w, PS = self.env, self.w, self.env.ps
        R = B * X_HEADS
        row = [self.rows[:, i, :] for i in range(12)]
        n = 0

        def link(ins):
            nonlocal n
            n += 1
            ins.then_inc(self.chain, 1)
            dve.wait_ge(self.chain, n)

        link(dve.tensor_scalar(self.bcol[:, :], w("gate_b"), 1.0 / X_CAP, None, ALU.mult))
        dve.wait_ge(self.chain_act, 1)
        i_, f_ = row[0], row[4]
        link(dve.tensor_scalar(i_, self.cap[0:R, :], X_CAP, None, ALU.mult))
        link(dve.tensor_scalar(f_, self.cap[R:2 * R, :], X_CAP, None, ALU.mult))
        assert n == self.CH_CAP
        link(dve.scalar_tensor_tensor(out=row[1], in0=f_, scalar=-1.0, in1=f_, op0=ALU.mult, op1=ALU.max))
        assert n == self.CH_ABS
        dve.wait_ge(self.chain_act, 2)
        log1p_half(dve, link, row[3], row[2], row[6], row[7])
        link(dve.tensor_scalar(row[6], f_, 0.0, None, ALU.min))
        link(dve.scalar_tensor_tensor(out=row[3], in0=row[3], scalar=-2.0, in1=row[6], op0=ALU.mult, op1=ALU.add))
        link(dve.tensor_tensor_scan(row[4], env.ones_row[0:R, :], row[3], 0.0, ALU.mult, ALU.add))
        assert n == self.CH_LF, n
        link(dve.tensor_tensor(row[5], i_, row[4], ALU.subtract))
        link(dve.tensor_tensor_scan(row[6], row[5], row[5], -3e38, ALU.max, ALU.max))
        link(dve.tensor_tensor(row[7], row[4], row[6], ALU.add))
        link(dve.tensor_scalar(row[11], row[6], -1.0, None, ALU.mult))
        assert n == self.CH_M, n
        split3(dve, link, [self.split[:, i, :] for i in range(3)], row[11], row[2])
        assert n == self.CH_SPLIT, n
        dve.wait_ge(self.c_up, 1)
        dve.tensor_copy(self.cols[:, :, :], PS[:, 1, 0:6 * R].rearrange("p (n r) -> p n r", n=6)).then_inc(self.c_done, 1)


        def queries(b, p):
            for i in range(2):
                ins = dve.tensor_scalar(self.q[:, p, i, :], env.xT[:, bass.ds(b * T, T)], w("head_par")[:, i:i + 1],
                                        None, ALU.mult)
            ins.then_inc(self.q_done, 1)

        def unit(b, p, u):
            dve.wait_ge(self.e_done, X_UNITS * b + u + 1)
            dve.tensor_tensor(self.Pm[:, u % 2, :, :].rearrange("p a t -> p (a t)"),
                              self.E[:, u % 2, :, :].rearrange("p a t -> p (a t)"),
                              PS[:, u % 2, :], ALU.mult).then_inc(self.p_done, 1)

        def combine(b, p):
            CB = self.CB[:, p, :, :, :].rearrange("p c h v -> p (c h) v")
            num, wsum = CB[:, :, 0:X_DH], CB[:, :, X_DH:X_DH + 1].rearrange("p h a -> p (h a)")
            sq = self.sq[:, p, :, :].rearrange("p c (h v) -> p (c h) v", h=X_HEADS)
            den = [self.den[:, p, i, :] for i in range(6)]
            em = self.cols[:, 2:4, bass.ds(b * X_HEADS, X_HEADS)]

            def step(ins, k):
                ins.then_inc(self.comb, 1)
                dve.wait_ge(self.comb, 8 * b + k)

            dve.wait_ge(self.to_copy, b + 2)
            dve.wait_ge(self.inter_read, b + 2)
            step(dve.tensor_tensor(self.CB[:, p, 1, :, :], self.CB[:, p, 1, :, :], self.tmp[:, p, :, :], ALU.add), 1)
            step(dve.scalar_tensor_tensor(out=sq, in0=num, scalar=1.0 / X_DH, in1=num, op0=ALU.mult, op1=ALU.mult), 2)
            step(dve.scalar_tensor_tensor(out=den[1], in0=wsum, scalar=-1.0, in1=wsum, op0=ALU.mult, op1=ALU.max), 3)
            step(dve.tensor_reduce(den[0], sq, AX.X, ALU.add), 4)
            step(dve.tensor_tensor(den[2].rearrange("p (c h) -> p c h", c=NT), den[1].rearrange("p (c h) -> p c h", c=NT),
                                   em, ALU.max), 5)
            step(dve.tensor_scalar(den[1], den[2], X_DEN_EPS, None, ALU.add), 6)
            step(dve.scalar_tensor_tensor(out=den[2], in0=den[1], scalar=X_NORM_EPS, in1=den[1],
                                          op0=ALU.mult, op1=ALU.mult), 7)
            dve.tensor_tensor(den[3], den[0], den[2], ALU.add).then_inc(self.comb, 1)

        def scale(b, p):
            CB = self.CB[:, p, :, :, :].rearrange("p c h v -> p (c h) v")
            sq = self.sq[:, p, :, :].rearrange("p c (h v) -> p (c h) v", h=X_HEADS)
            dve.wait_ge(self.rooted, 2 * b + 2)
            dve.tensor_tensor(sq, CB[:, :, 0:X_DH], self.den[:, p, 5, :].unsqueeze(2).broadcast_to([P, NT * X_HEADS, X_DH]),
                              ALU.mult).then_inc(self.out, 1)
            dve.wait_ge(self.out, 3 * b + 1)
            dve.scalar_tensor_tensor(out=self.sq[:, p, :, :], in0=w("outnorm").unsqueeze(1).broadcast_to([P, NT, P]),
                                     scalar=1.0, in1=self.sq[:, p, :, :], op0=ALU.add, op1=ALU.mult).then_inc(self.out, 1)
            dve.wait_ge(self.out, 3 * b + 2)
            dve.tensor_tensor(self.y[:, p, :, :], self.sq[:, p, :, :], env.X[:, bass.ds(b * NT, NT), :],
                              ALU.add).then_inc(self.out, 1)
            dve.wait_ge(self.out, 3 * b + 3)
            self.tail.moments(dve, self.y[:, p, :, :], b, p)

        def norm(b, p):
            self.tail.apply(dve, lambda k: env.x_tile(b * NT + k), self.y[:, p, :, :], b, p, env.x_done[1])

        def element(b, p, first, last):
            dve.wait_ge(self.kv_up, b + 1)
            dve.tensor_tensor(self.kv[:, p, :], PS[:, 7, 0:T], w("same_head"), ALU.mult).then_inc(self.kv_done, 1)
            for u in range(X_UNITS):
                unit(b, p, u)
                if u == 0 and not first and not (isinstance(b, int) and b == 1):
                    norm(b - 2, p)
                if u == 1 and not last:
                    queries(b + 1, 1 - p)
                if u == 2 and not first:
                    combine(b - 1, 1 - p)
            dve.wait_ge(self.inter_up, b + 1)
            dve.tensor_tensor(
                self.tmp[:, p, :, :], PS[:, 7, T:2 * T].rearrange("p (h v) -> p h v", h=X_HEADS),
                self.cols[:, 5:6, bass.ds(b * X_HEADS, X_HEADS)].rearrange("p a h -> p (a h)").unsqueeze(2)
                    .broadcast_to([P, X_HEADS, X_SLOT]), ALU.mult).then_inc(self.inter_read, 1)
            if not first:
                scale(b - 1, 1 - p)

        queries(0, 0)
        elements(dve, element)
        norm(B - 2, 0)
        combine(B - 1, 1)
        scale(B - 1, 1)
        norm(B - 1, 1)


F_HID, F_PAIRS = 512, 4
F_BLOCKS = F_HID // P


class Ffn(Sublayer):
    def __init__(self, env, w, index):
        self.env, self.w, self.index = env, w, index
        sb, sem = env.sb, env.sem
        self.turned = Turned(env, index)
        self.rows = sb("f_rows", [F_PAIRS, 4, B, P])
        self.odd = sb("f_odd", [F_PAIRS, PAIR, 2, P])
        self.e1 = sb("f_e1", [F_PAIRS, PAIR, F_PAIRS, P])
        self.e2 = sb("f_e2", [F_PAIRS, PAIR, F_BLOCKS, P])
        self.W1 = sb("f_W1b", [P, PAIR, F_HID])
        self.W2 = sb("f_W2b", [P, PAIR, F_HID])
        self.h = sb("f_h", [P, PAIR, F_BLOCKS, T])
        self.xb = sb("f_xb", [P, PAIR, NT, P])
        self.y = sb("f_y", [P, PAIR, NT, P])
        self.tail = LayerNormTail(env, "f_ln", index)
        self.rows_in = sem("f_rows_in")
        self.rows_set = sem("f_rows_set")
        self.xb_done = sem("f_xb_done")
        self.delta_up = sem("f_delta_up")
        self.w_sum = sem("f_w_sum")
        self.h_up = sem("f_h_up")
        self.h_act = sem("f_h_act")
        self.o_up = sem("f_o_up")
        self.y_done = sem("f_y_done")

    def sp(self, sp):
        env = self.env
        sp.wait_ge(env.x_done[self.index - 1], B)
        for kind, first in enumerate((1, 2, 9, 10)):
            sp.dma_start(self.rows[:, kind, :, :], env.X[first:first + 7:2, 0::NT, :]).then_inc(self.rows_in, 16)

    def pool(self, pool):
        env, w = self.env, self.w
        pool.memset(self.xb[:, :, :, :], 0.0).then_inc(self.y_done, PAIR)
        pool.memset(self.odd[:, :, :, :], 0.0).then_inc(self.delta_up, PAIR)
        pool.memset(self.e1[:, :, :, :], 0.0).then_inc(self.w_sum, 2 * PAIR)
        pool.wait_ge(self.rows_in, 64)
        pool.wait_ge(self.delta_up, PAIR)
        pool.wait_ge(self.w_sum, 2 * PAIR)
        blk = w("blk")[0:F_PAIRS]

        def rows(b, p):
            row = lambda kind: self.rows[:, kind:kind + 1, bass.ds(b, 1), :].rearrange("p k a c -> p (k a c)")
            pool.wait_ge(self.delta_up, b + 1)
            for n in range(2):
                pool.tensor_tensor(self.odd[:, p, n, :], row(2 * n + 1),
                                   w("scale")[0:F_PAIRS].broadcast_to([F_PAIRS, P]), ALU.mult)
            pool.tensor_tensor(self.e1[:, p, :, :], row(0).unsqueeze(1).broadcast_to([F_PAIRS, F_PAIRS, P]),
                               blk.unsqueeze(2).broadcast_to([F_PAIRS, F_PAIRS, P]), ALU.mult)
            ev = row(2).rearrange("p (q r) -> p r q", r=F_BLOCKS)
            shape = [F_PAIRS, F_BLOCKS, F_PAIRS, P // F_PAIRS]
            pool.tensor_tensor(
                self.e2[:, p, :, :].rearrange("p r (i q) -> p r i q", i=F_PAIRS), ev.unsqueeze(2).broadcast_to(shape),
                blk.unsqueeze(1).unsqueeze(3).broadcast_to(shape), ALU.mult).then_inc(self.rows_set, 1)

        def bias(b, p):
            pool.wait_ge(self.y_done, b + 1)
            pool.tensor_tensor(self.xb[:, p, :, :], env.X[:, bass.ds(b * NT, NT), :],
                               w("b2").unsqueeze(1).broadcast_to([P, NT, P]), ALU.add).then_inc(self.xb_done, 1)

        def element(b, p, first, last):
            if not (isinstance(b, int) and b >= B - PAIR):
                rows(b + PAIR, p)
            if not first:
                self.tail.root_pool(pool, b - 1, 1 - p)
            if not last:
                bias(b + 1, 1 - p)

        rows(0, 0)
        rows(1, 1)
        bias(0, 0)
        elements(pool, element)
        self.tail.root_pool(pool, B - 1, 1)

    def pe(self, pe):
        env, w, PS = self.env, self.w, self.env.ps
        self.turned.pe(pe)
        pe.wait_ge(self.turned.ready, self.turned.all)

        def outer(b, p):
            pe.wait_ge(self.rows_set, b + 1)
            pe.wait_ge(self.w_sum, 2 * b + 2)
            pe.matmul(PS[:, 4 * p, :], self.odd[:, p, 0, :], self.e1[:, p, :, :], start=True, stop=True)
            pe.matmul(PS[:, 4 * p + 1, :], self.odd[:, p, 1, :], self.e2[:, p, :, :],
                      start=True, stop=True).then_inc(self.delta_up, 1)

        def hidden(b, p):
            pe.wait_ge(self.y_done, b + 1)
            pe.wait_ge(self.w_sum, 2 * b + 1 + 2 * PAIR)
            for j in range(F_BLOCKS):
                ins = pe.matmul(PS[:, 4 * p + 2 + j // 2, (j % 2) * T:(j % 2 + 1) * T],
                                self.W1[:, p, j * P:(j + 1) * P], env.xT[:, bass.ds(b * T, T)],
                                start=True, stop=True)
            ins.then_inc(self.h_up, 1)

        def result(b, p):
            pe.wait_ge(self.w_sum, 2 * b + 2 + 2 * PAIR)
            pe.wait_ge(self.h_act, b + 1)
            for k in range(NT):
                for r in range(F_BLOCKS):
                    ins = pe.matmul(PS[:, 4 * p + 2, k * P:(k + 1) * P], self.h[:, p, r, k * P:(k + 1) * P],
                                    self.W2[:, p, r * P:(r + 1) * P], start=(r == 0), stop=(r == F_BLOCKS - 1))
            ins.then_inc(self.o_up, 1)

        def element(b, p, first, last):
            hidden(b, p)
            if not last:
                outer(b + 1, 1 - p)
            if not first:
                result(b - 1, 1 - p)

        outer(0, 0)
        elements(pe, element)
        result(B - 1, 1)

    def act(self, act):
        PS, w = self.env.ps, self.w
        self.turned.act(act)
        with pairs(act) as it:
            for p in range(PAIR):
                b = it * PAIR + p
                act.wait_ge(self.h_up, b + 1)
                for j in range(F_BLOCKS):
                    ins = act.activation(self.h[:, p, j, :], PS[:, 4 * p + 2 + j // 2, (j % 2) * T:(j % 2 + 1) * T],
                                         ACT.Gelu, bias=w("b1")[:, j:j + 1])
                ins.then_inc(self.h_act, 1)

    def dve(self, dve):
        env, w, PS = self.env, self.w, self.env.ps

        def add_w1(b, p):
            dve.wait_ge(self.delta_up, b + 1 + PAIR)
            dve.tensor_tensor(self.W1[:, p, :], w("W1"), PS[:, 4 * p, :], ALU.add).then_inc(self.w_sum, 1)

        def add_w2(b, p):
            dve.tensor_tensor(self.W2[:, p, :], w("W2"), PS[:, 4 * p + 1, :], ALU.add).then_inc(self.w_sum, 1)

        def add(b, p):
            dve.wait_ge(self.o_up, b + 1)
            dve.wait_ge(self.xb_done, b + 1)
            dve.tensor_tensor(self.y[:, p, :, :], self.xb[:, p, :, :],
                              PS[:, 4 * p + 2, 0:T].rearrange("p (k c) -> p k c", k=NT), ALU.add).then_inc(self.y_done, 1)
            dve.wait_ge(self.y_done, b + 1 + PAIR)
            self.tail.moments(dve, self.y[:, p, :, :], b, p)

        def norm(b, p):
            self.tail.apply(dve, lambda k: env.x_tile(b * NT + k), self.y[:, p, :, :], b, p, env.x_done[self.index])

        def element(b, p, first, last):
            if not last:
                add_w1(b + 1, 1 - p)
            if not first:
                if not (isinstance(b, int) and b == 1):
                    norm(b - 2, p)
                add(b - 1, 1 - p)
            if not last:
                add_w2(b + 1, 1 - p)

        add_w1(0, 0)
        add_w2(0, 0)
        elements(dve, element)
        norm(B - 2, 0)
        add(B - 1, 1)
        norm(B - 1, 1)


R_HEADS, R_DH, R_HID = 16, 8, 256
R_UNITS = R_HEADS // 2
R_GROUP = 4
R_NORM_SHIFT = 20
R_SLOTS = R_GROUP * (32 + R_DH)


class GroupNorm:

    DVE_STEPS = 9

    def __init__(self, env, tag, w, names, before=None):
        self.env, self.w, self.names = env, w, names
        self.stats = env.sb(f"{tag}_stats", [P, B, 6])
        self.mv = env.sb(f"{tag}_mv", [P, B, 2])
        self.c = env.sb(f"{tag}_c", [P, 6, B])
        self.at = 1 if before else 0
        self.dve_step = before.dve_step if before else env.sem(f"{tag}_dve")
        self.pe_step = before.pe_step if before else env.sem(f"{tag}_pe")
        self.act_step = before.act_step if before else env.sem(f"{tag}_act")
        self.done = (self.at + 1) * self.DVE_STEPS

    def pe(self, pe, bank):
        PS, group = self.env.ps, self.w("group")
        pe.wait_ge(self.dve_step, self.at * self.DVE_STEPS + 2)
        pe.matmul(PS[:, bank, 0:B], group, self.mv[:, :, 0], start=True, stop=True).then_inc(self.pe_step, 1)
        pe.wait_ge(self.dve_step, self.at * self.DVE_STEPS + 5)
        pe.matmul(PS[:, bank, B:2 * B], group, self.c[:, 1, :], start=True, stop=True).then_inc(self.pe_step, 1)

    def act(self, act, bank):
        act.wait_ge(self.pe_step, 2 * self.at + 2)
        act.activation(self.c[:, 2, :], self.env.ps[:, bank, B:2 * B], ACT.Ln, bias=self.env.w0("eps")[:, 0:1]).then_inc(self.act_step, 1)
        act.wait_ge(self.act_step, 2 * self.at + 1)
        act.activation(self.c[:, 3, :], self.c[:, 2, :], ACT.Exp, scale=-0.5).then_inc(self.act_step, 1)

    def dve(self, dve, bank):
        env, w, (gamma, beta), c = self.env, self.w, self.names, self.c
        mu = env.ps[:, bank, 0:B]

        def step(ins, k):
            ins.then_inc(self.dve_step, 1)
            dve.wait_ge(self.dve_step, self.at * self.DVE_STEPS + k)

        for b in range(B):
            ins = dve.bn_stats(self.stats[:, b, :], env.xT[:, b * T:(b + 1) * T])
        step(ins, 1)
        for b in range(B):
            ins = dve.bn_aggr(self.mv[:, b, :], self.stats[:, b, :])
        step(ins, 2)
        dve.wait_ge(self.pe_step, 2 * self.at + 1)
        step(dve.tensor_tensor(c[:, 0, :], self.mv[:, :, 0], mu, ALU.subtract), 3)
        step(dve.tensor_tensor(c[:, 0, :], c[:, 0, :], c[:, 0, :], ALU.mult), 4)
        step(dve.tensor_tensor(c[:, 1, :], c[:, 0, :], self.mv[:, :, 1], ALU.add), 5)
        dve.wait_ge(self.act_step, 2 * self.at + 2)
        step(dve.tensor_scalar(c[:, 4, :], c[:, 3, :], w(gamma), None, ALU.mult), 6)
        step(dve.tensor_tensor(c[:, 5, :], c[:, 4, :], mu, ALU.mult), 7)
        step(dve.tensor_scalar(c[:, 5, :], c[:, 5, :], -1.0, w(beta), ALU.mult, ALU.add), 8)
        for b in range(B):
            x = env.xT[:, b * T:(b + 1) * T]
            ins = dve.tensor_scalar(x, x, c[:, 4, b:b + 1], c[:, 5, b:b + 1], ALU.mult, ALU.add)
        step(ins, 9)



class Retention(Sublayer):
    def __init__(self, env, w, index):
        self.env, self.w, self.index = env, w, index
        sb, sem = env.sb, env.sem
        self.turned = Turned(env, index)
        self.gn1 = GroupNorm(env, "r_g1", w, ("norm_g", "norm_b"))
        self.gn2 = GroupNorm(env, "r_g2", w, ("fnorm_g", "fnorm_b"), self.gn1)
        self.xn = sb("r_xn", [P, PAIR, T])
        self.qT = sb("r_qT", [P, PAIR, T])
        self.kT = sb("r_kT", [P, PAIR, T])
        self.sq = sb("r_sq", [P, PAIR, 2, T])
        self.ktok = sb("r_ktok", [P, PAIR, P])
        self.qm = sb("r_qm", [P, PAIR, R_GROUP, T])
        self.nn = sb("r_nn", [P, PAIR, 3, 2 * NT])
        self.V = sb("r_V", [P, PAIR, NT, R_GROUP, R_SLOTS])
        self.kv = sb("r_kv", [P, PAIR, P])
        self.Pm = sb("r_P", [P, 2, 4, P])
        self.yT = sb("r_yT", [P, PAIR, T])
        self.xob = sb("r_xob", [P, PAIR, NT, P])
        self.x2 = sb("r_x2", [P, PAIR, NT, P])
        self.h = sb("r_h", [P, PAIR, 2, T])
        self.y = sb("r_y", [P, PAIR, NT, P])
        self.tail = LayerNormTail(env, "r_ln", index)
        self.loaded = sem("r_loaded")
        self.proj_up = sem("r_proj_up")
        self.squared = sem("r_squared")
        self.nn_up = sem("r_nn_up")
        self.qm_done = sem("r_qm_done")
        self.nn_max = sem("r_nn_max")
        self.rooted = sem("r_rooted")
        self.v_done = sem("r_v_done")
        self.kv_up = sem("r_kv_up")
        self.kv_done = sem("r_kv_done")
        self.s_up = sem("r_s_up")
        self.p_done = sem("r_p_done")
        self.y_up = sem("r_y_up")
        self.yT_done = sem("r_yT_done")
        self.o_up = sem("r_o_up")
        self.xob_done = sem("r_xob_done")
        self.xb2_done = sem("r_xb2_done")
        self.x2_done = sem("r_x2_done")
        self.x2_up = sem("r_x2_up")
        self.x2T = sem("r_x2T")
        self.x2_add = sem("r_x2_add")
        self.h_up = sem("r_h_up")
        self.h_act = sem("r_h_act")
        self.f_up = sem("r_f_up")
        self.y_done = sem("r_y_done")

    def sp(self, sp):
        self.guest.keys_sp(sp)

    def pool(self, pool):
        env, w = self.env, self.w
        pool.memset(self.xn[:, :, :], 0.0).then_inc(self.y_done, PAIR)
        pool.memset(self.V[:, :, :, :, :], 0.0).then_inc(self.x2_done, PAIR)
        pool.memset(self.kv[:, :, :], 0.0).then_inc(self.x2T, PAIR)
        self.guest.keys_pool_first(pool)
        pool.wait_ge(self.gn1.dve_step, self.gn1.done)
        pool.wait_ge(self.y_done, PAIR)
        row = lambda name: w(name).unsqueeze(1).broadcast_to([P, NT, P])
        with pairs(pool) as it:
            for p in range(PAIR):
                b = it * PAIR + p
                pool.wait_ge(self.x2_done, b + 1)
                pool.tensor_copy(self.xn[:, p, :], env.xT[:, bass.ds(b * T, T)]).then_inc(self.loaded, 1)
                pool.tensor_tensor(self.xob[:, p, :, :], env.X[:, bass.ds(b * NT, NT), :], row("ob"), ALU.add).then_inc(self.xob_done, 1)
                if p == 0:
                    self.guest.keys_pool(pool, it)
        self.guest.windows_pool(pool)
        pool.wait_ge(self.x2_add, B)

        def bias(b, p):
            pool.wait_ge(self.y_done, b + 1)
            pool.tensor_tensor(self.xob[:, p, :, :], env.X[:, bass.ds(b * NT, NT), :], row("b2"), ALU.add).then_inc(self.xb2_done, 1)

        def element(b, p, first, last):
            if not last:
                bias(b + 1, 1 - p)
            self.tail.root_pool(pool, b, p)

        bias(0, 0)
        elements(pool, element)

    def pe(self, pe):
        env, w, PS = self.env, self.w, self.env.ps
        self.turned.pe(pe)
        self.gn1.pe(pe, 0)
        self.guest.keys_pe(pe)

        def prepare(b, p, step):
            if step == 0:
                pe.wait_ge(self.loaded, b + 1)
                for n, name in enumerate(("qw", "kw")):
                    pe.matmul(PS[:, 2 + p, n * T:(n + 1) * T], w(name), self.xn[:, p, :], start=True, stop=True)
                for k in range(NT):
                    pe.matmul(PS[:, 4 + p, k * P:(k + 1) * P], self.xn[:, p, k * P:(k + 1) * P], w("vw"),
                              start=True, stop=True)
                pe.matmul(PS[:, 4 + p, T:T + P], self.xn[:, p, 0:P], w("kw"), start=True, stop=True).then_inc(self.proj_up, 1)
            else:
                pe.wait_ge(self.squared, b + 1)
                pe.wait_ge(self.x2T, b + 1)
                for n in range(2 * NT):
                    ins = pe.matmul(PS[:, 6 + p, T + P + n:T + P + n + 1],
                                    self.sq[:, p, n // NT, n % NT * P:(n % NT + 1) * P], env.ones_row[:, 0:1],
                                    start=True, stop=True)
                ins.then_inc(self.nn_up, 1)

        def scores(p, u):
            for i in range(2):
                h = 2 * u + i
                r = slice(32 * (h // R_GROUP), 32 * (h // R_GROUP) + 32)
                for c in range(NT):
                    ins = pe.matmul(PS[:, u % 2, (2 * i + c) * P:(2 * i + c + 1) * P], self.kT[r, p, c * P:(c + 1) * P],
                                    self.qm[r, p, h % R_GROUP, c * P:(c + 1) * P], start=True, stop=True)
            ins.then_inc(self.s_up, 1)

        def mix(b, p, u):
            pe.wait_ge(self.p_done, R_UNITS * b + u + 1)
            for i in range(2):
                h = 2 * u + i
                g, j = h // R_GROUP, h % R_GROUP
                for c in range(NT):
                    ins = pe.matmul(PS[32 * g:32 * g + 32, 6 + p, c * P:(c + 1) * P],
                                    self.V[:, p, c, g, 32 * j:32 * j + 32], self.Pm[:, u % 2, 2 * i + c, :],
                                    start=False, stop=(j == R_GROUP - 1), skip_group_check=True)
            if u == R_UNITS - 1:
                ins.then_inc(self.y_up, 1)

        def finish(b, p, step):
            if step == 0:
                pe.wait_ge(self.yT_done, b + 1)
                for k in range(NT):
                    ins = pe.matmul(PS[:, 2 + p, k * P:(k + 1) * P], self.yT[:, p, k * P:(k + 1) * P], w("ow"),
                                    start=True, stop=True)
                ins.then_inc(self.o_up, 1)
            else:
                pe.wait_ge(self.x2_done, b + 1 + PAIR)
                for k in range(NT):
                    ins = pe.transpose(PS[:, 6 + p, k * P:(k + 1) * P], self.x2[:, p, k, :], env.ident)
                ins.then_inc(self.x2_up, 1)

        def element(b, p, first, last):
            pe.wait_ge(self.v_done, b + 1)
            for u in range(R_UNITS):
                scores(p, u)
                if u == 0:
                    pe.matmul(PS[:, 6 + p, T:T + P], self.ktok[:, p, :],
                              self.V[:, p, 0, :, :].rearrange("p g (j c) -> p g j c", j=R_GROUP)[:, :, :, 0:R_DH],
                              start=True, stop=True).then_inc(self.kv_up, 1)
                    if not first:
                        mix(b - 1, 1 - p, R_UNITS - 1)
                else:
                    if u == 1:
                        pe.wait_ge(self.kv_done, b + 1)
                        pe.matmul(PS[:, 6 + p, P:T], self.kv[:, p, :], self.qT[:, p, P:T],
                                  start=True, stop=False, skip_group_check=True)
                    mix(b, p, u - 1)
                if not first and u in (1, 2):
                    finish(b - 1, 1 - p, u - 1)
                if not last and u in (3, 5):
                    prepare(b + 1, 1 - p, (u - 3) // 2)

        prepare(0, 0, 0)
        prepare(0, 0, 1)
        elements(pe, element)
        mix(B - 1, 1, R_UNITS - 1)
        finish(B - 1, 1, 0)
        finish(B - 1, 1, 1)
        self.gn2.pe(pe, 0)
        pe.wait_ge(self.gn2.dve_step, self.gn2.done)

        def hidden(b, p):
            for j in range(2):
                ins = pe.matmul(PS[:, p, j * T:(j + 1) * T], w("w1")[:, j * P:(j + 1) * P],
                                env.xT[:, bass.ds(b * T, T)], start=True, stop=True)
            ins.then_inc(self.h_up, 1)

        def forward(b, p, first, last):
            if not last:
                hidden(b + 1, 1 - p)
            pe.wait_ge(self.h_act, b + 1)
            pe.wait_ge(self.y_done, b + 1)
            for k in range(NT):
                for j in range(2):
                    ins = pe.matmul(PS[:, 2 + p, k * P:(k + 1) * P], self.h[:, p, j, k * P:(k + 1) * P],
                                    w("w2")[:, j * P:(j + 1) * P], start=(j == 0), stop=(j == 1))
            ins.then_inc(self.f_up, 1)

        hidden(0, 0)
        elements(pe, forward)

    def act(self, act):
        env, w, PS = self.env, self.w, self.env.ps
        self.turned.act(act)
        act.preload_act_table_set(EXP_LN)
        self.gn1.act(act, 0)
        self.guest.keys_act(act)

        def prepare(b, p):
            act.wait_ge(self.proj_up, b + 1)
            act.activation(self.sq[:, p, :, :], PS[:, 2 + p, :].rearrange("p (n t) -> p n t", n=2), ACT.Square)
            act.activation(self.kT[:, p, :], PS[:, 2 + p, T:2 * T], ACT.Copy)
            act.activation(self.qT[:, p, :], PS[:, 2 + p, 0:T], ACT.Copy)
            act.activation(self.ktok[:, p, :], PS[:, 4 + p, T:T + P], ACT.Copy).then_inc(self.squared, 1)
            act.wait_ge(self.nn_max, b + 1)
            act.activation(self.nn[:, p, 1, :], self.nn[:, p, 0, :], ACT.Ln, scale=2.0 ** R_NORM_SHIFT).then_inc(self.rooted, 1)
            act.wait_ge(self.rooted, 2 * b + 1)
            act.activation(self.nn[:, p, 2, :], self.nn[:, p, 1, :], ACT.Exp, scale=-0.5).then_inc(self.rooted, 1)

        def finish(b, p):
            act.wait_ge(self.x2_up, b + 1)
            act.activation(env.xT[:, bass.ds(b * T, T)], PS[:, 6 + p, 0:T], ACT.Copy).then_inc(self.x2T, 1)

        def element(b, p, first, last):
            if not first:
                finish(b - 1, 1 - p)
            if not last:
                prepare(b + 1, 1 - p)

        prepare(0, 0)
        elements(act, element)
        finish(B - 1, 1)
        self.gn2.act(act, 0)
        with pairs(act) as it:
            for p in range(PAIR):
                b = it * PAIR + p
                act.wait_ge(self.h_up, b + 1)
                for j in range(2):
                    ins = act.activation(self.h[:, p, j, :], PS[:, p, j * T:(j + 1) * T], ACT.Silu, bias=w("b1")[:, j:j + 1])
                ins.then_inc(self.h_act, 1)

    def dve(self, dve):
        env, w, PS = self.env, self.w, self.env.ps
        dve.wait_ge(self.turned.ready, self.turned.all)
        self.gn1.dve(dve, 0)
        self.guest.keys_dve(dve)
        slots = lambda a: a.rearrange("p g (j c) -> p g j c", j=R_GROUP)[:, :, :, 0:R_DH]
        heads = lambda a: a.rearrange("p (g j c) -> p g j c", g=R_GROUP, j=R_GROUP)

        def by_head(b, p):
            dve.wait_ge(self.squared, b + 1)
            for j in range(R_GROUP):
                ins = dve.tensor_scalar(self.qm[:, p, j, :], self.qT[:, p, :], w("head_of")[:, j:j + 1], None, ALU.mult)
            ins.then_inc(self.qm_done, 1)

        def clamp(b, p):
            dve.wait_ge(self.nn_up, b + 1)
            dve.tensor_scalar(self.nn[:, p, 0, :], PS[:, 6 + p, T + P:T + P + 2 * NT], 1e-24, None,
                              ALU.max).then_inc(self.nn_max, 1)

        def values(b, p):
            dve.wait_ge(self.rooted, 2 * b + 2)
            for c in range(NT):
                ins = dve.scalar_tensor_tensor(
                    out=slots(self.V[:, p, c, :, :]), in0=heads(PS[:, 4 + p, c * P:(c + 1) * P]),
                    scalar=self.nn[:, p, 2, NT + c:NT + c + 1], in1=heads(w("v_decay")), op0=ALU.mult, op1=ALU.mult)
            ins.then_inc(self.v_done, 1)

        def decayed(b, p):
            dve.wait_ge(self.y_up, b + 1)
            dve.tensor_tensor(self.yT[:, p, :], PS[:, 6 + p, 0:T], w("y_decay"), ALU.mult).then_inc(self.yT_done, 1)

        def residual(b, p):
            dve.wait_ge(self.o_up, b + 1)
            dve.wait_ge(self.xob_done, b + 1)
            if not isinstance(b, int) or b > 0:
                dve.wait_ge(self.x2_add, b)
            for k in range(NT):
                ins = dve.scalar_tensor_tensor(
                    out=self.x2[:, p, k, :], in0=PS[:, 2 + p, k * P:(k + 1) * P], scalar=self.nn[:, p, 2, k:k + 1],
                    in1=self.xob[:, p, k, :], op0=ALU.mult, op1=ALU.add)
            ins.then_inc(self.x2_done, 1)
            dve.wait_ge(self.x2_done, b + 1 + PAIR)
            X = env.X[:, bass.ds(b * NT, NT), :]
            dve.tensor_tensor(X, X, self.x2[:, p, :, :], ALU.add).then_inc(self.x2_add, 1)

        def element(b, p, first, last):
            dve.wait_ge(self.kv_up, b + 1)
            dve.tensor_tensor(self.kv[:, p, :], PS[:, 6 + p, T:T + P], w("same_head"), ALU.mult).then_inc(self.kv_done, 1)
            for u in range(R_UNITS):
                dve.wait_ge(self.s_up, R_UNITS * b + u + 1)
                dve.tensor_tensor(self.Pm[:, u % 2, :, :], PS[:, u % 2, :].rearrange("p (a t) -> p a t", a=4),
                                  w("causal").unsqueeze(1).broadcast_to([P, 4, P]), ALU.mult).then_inc(self.p_done, 1)
                if not first:
                    if u == 0:
                        decayed(b - 1, 1 - p)
                    if u == 1:
                        residual(b - 1, 1 - p)
                if not last:
                    if u == 4:
                        by_head(b + 1, 1 - p)
                    if u == 5:
                        clamp(b + 1, 1 - p)
                    if u == 6:
                        values(b + 1, 1 - p)

        by_head(0, 0)
        clamp(0, 0)
        values(0, 0)
        elements(dve, element)
        decayed(B - 1, 1)
        residual(B - 1, 1)
        dve.wait_ge(self.x2T, B + PAIR)
        self.gn2.dve(dve, 0)

        def norm(b, p):
            self.tail.apply(dve, lambda k: env.x_tile(b * NT + k), self.y[:, p, :, :], b, p, env.x_done[self.index])

        def forward(b, p, first, last):
            dve.wait_ge(self.f_up, b + 1)
            dve.wait_ge(self.xb2_done, b + 1)
            if not first and not (isinstance(b, int) and b == 1):
                dve.wait_ge(env.x_done[self.index], b - 1)
            dve.tensor_tensor(self.y[:, p, :, :], PS[:, 2 + p, 0:T].rearrange("p (k c) -> p k c", k=NT),
                              self.xob[:, p, :, :], ALU.add).then_inc(self.y_done, 1)
            dve.wait_ge(self.y_done, b + 1 + PAIR)
            self.tail.moments(dve, self.y[:, p, :, :], b, p)
            if not first:
                norm(b - 1, 1 - p)

        elements(dve, forward)
        norm(B - 1, 1)


A_HEADS, A_DH = 16, 8
A_Q_PARTS, A_K_PARTS = (0, 1, 2, 0, 1, 0), (0, 0, 0, 1, 1, 2)
A_RUNS = (((slice(0, 3), 0, 1), (slice(3, 5), 1, 1), (slice(5, 6), 2, 1)),
          ((slice(0, 3), 0, 3), (slice(3, 5), 0, 2), (slice(5, 6), 0, 1)))
A_OUT = 16 * len(A_RUNS[0])
A_ROWS = len(A_Q_PARTS) * A_DH
A_STACKS = A_HEADS // 2
A_GROUP = 4
A_WINDOW = 64
A_CHUNKS = 4


class CrossAttention(Sublayer):
    def __init__(self, env, w, index):
        self.env, self.w, self.index = env, w, index
        sb, sem = env.sb, env.sem
        C = B * T // A_CHUNKS
        self.turned = Turned(env, index)
        self.proj = sb("a_proj", [P, C])
        self.parts = sb("a_parts", [P, 2, 3, C], BF16)
        self.vtok = sb("a_vtok", [P, TILES, P])
        self.QS = sb("a_QS", [P, PAIR, A_STACKS, T], BF16)
        self.KS = sb("a_KS", [P, PAIR, A_STACKS, T], BF16)
        self.V = sb("a_V", [P, PAIR, NT, A_HEADS // A_GROUP, A_GROUP * (A_WINDOW + A_DH)])
        self.keys = self.V[:, :, :, :, :].rearrange("p a c g v -> p (a c g v)")[:, 0:B * T]
        self.mx = sb("a_mx", [P, PAIR, 3, NT * A_HEADS])
        self.msplit = sb("a_msplit", [P, PAIR, NT, P // A_HEADS, A_HEADS], BF16)
        self.mrow = sb("a_mrow", [P, PAIR, T], BF16)
        self.selb = sb("a_selb", [P, A_HEADS, P], BF16)
        self.E = sb("a_E", [P, 2, NT, T])
        self.O = sb("a_O", [P, PAIR, 2, T])
        self.rec = sb("a_rec", [P, PAIR, 8, A_GROUP])
        self.ct = sb("a_ct", [P, PAIR, NT, P])
        self.cT = sb("a_cT", [P, PAIR, T])
        self.xb = sb("a_xb", [P, PAIR, NT, P])
        self.y = sb("a_y", [P, PAIR, NT, P])
        self.tail = LayerNormTail(env, "a_ln", index)
        self.k_up = sem("a_k_up")
        self.k_done = sem("a_k_done")
        self.vtok_up = sem("a_vtok_up")
        self.vtok_done = sem("a_vtok_done")
        self.k_split = sem("a_k_split")
        self.k_out = sem("a_k_out")
        self.proj_up = sem("a_proj_up")
        self.proj_done = sem("a_proj_done")
        self.split = sem("a_split")
        self.q_out = sem("a_q_out")
        self.st_in = [sem(f"a_st_in{p}") for p in range(PAIR)]
        self.v_set = sem("a_v_set")
        self.mx_up = sem("a_mx_up")
        self.mx_done = sem("a_mx_done")
        self.m_step = sem("a_m_step")
        self.mT_up = sem("a_mT_up")
        self.mT_done = sem("a_mT_done")
        self.s_up = sem("a_s_up")
        self.e_done = sem("a_e_done")
        self.pv_up = sem("a_pv_up")
        self.o_copy = sem("a_o_copy")
        self.ot_up = sem("a_ot_up")
        self.c_step = sem("a_c_step")
        self.ct_up = sem("a_ct_up")
        self.cT_done = sem("a_cT_done")
        self.w_up = sem("a_w_up")
        self.xb_done = sem("a_xb_done")
        self.y_done = sem("a_y_done")


    def keys_pe(self, pe):
        env, w, PS = self.env, self.w, self.env.ps
        C = B * T // A_CHUNKS
        pe.wait_ge(env.w_in[self.index + 1], 16)
        pe.wait_ge(env.ctx_in, 32)
        pe.wait_ge(self.m_step, 1)
        for m in range(A_CHUNKS):
            if m == 3:
                pe.wait_ge(self.k_done, 1)
            pe.matmul(PS[:, 1 + m % 3, :], w("wk"), env.ctxT[:, m * C:(m + 1) * C], start=True, stop=True).then_inc(self.k_up, 1)
        for t in range(TILES):
            ins = pe.matmul(PS[:, 4 + t // 4, t % 4 * P:(t % 4 + 1) * P], env.ctxT[:, t * P:(t + 1) * P], w("wv"),
                            start=True, stop=True)
        ins.then_inc(self.vtok_up, 1)
        pe.wait_ge(self.k_done, A_CHUNKS)
        pe.wait_ge(self.vtok_done, 1)

    def keys_act(self, act):
        C = B * T // A_CHUNKS
        for m in range(A_CHUNKS):
            act.wait_ge(self.k_up, m + 1)
            act.activation(self.keys[:, m * C:(m + 1) * C], self.env.ps[:, 1 + m % 3, :], ACT.Identity,
                           bias=self.w("bk")).then_inc(self.k_done, 1)

    def keys_dve(self, dve):
        dve.wait_ge(self.vtok_up, 1)
        for i in range(4):
            ins = dve.tensor_tensor(self.vtok[:, 4 * i:4 * i + 4, :], self.env.ps[:, 4 + i, :].rearrange("p (k c) -> p k c", k=4),
                                    self.w("bv").unsqueeze(1).broadcast_to([P, 4, P]), ALU.add)
        ins.then_inc(self.vtok_done, 1)

    def keys_pool_first(self, pool):
        pool.wait_ge(self.env.x_done[self.index - 2], B)
        pool.memset(self.msplit[:, :, :, :, :], 0.0).then_inc(self.m_step, 1)
        pool.memset(self.mrow[:, 0, 0:8], 0.0).then_inc(self.k_out, 16)

    def keys_pool(self, pool, it):
        C = B * T // A_CHUNKS

        def step(ins, k):
            ins.then_inc(self.k_split, 1)
            pool.wait_ge(self.k_split, 5 * it + k)

        pool.wait_ge(self.k_done, A_CHUNKS)
        pool.wait_ge(self.k_out, A_OUT * it + 16)
        x = self.proj[:, :]
        parts = [self.parts[:, 0, i, :] for i in range(3)]
        step(pool.tensor_copy(x, self.keys[:, bass.ds(it * C, C)]), 1)
        one = self.env.ones_row[:, 0:1].broadcast_to([P, C])
        step(pool.tensor_tensor(parts[0], x, one, ALU.mult), 2)
        step(pool.tensor_tensor(x, x, parts[0], ALU.subtract), 3)
        step(pool.tensor_tensor(parts[1], x, one, ALU.mult), 4)
        step(pool.tensor_tensor(parts[2], x, parts[1], ALU.subtract), 5)

    def parts_out(self, sp, kq, chunk, buf, done):
        elements = B // A_CHUNKS
        C = elements * T
        for rows, first, n in A_RUNS[kq]:
            dst = self.env.st_dram[kq, :, :, :, rows, bass.ds(chunk * elements, elements), :]
            src = self.parts[:, buf, first:first + n, :]
            if n == 1:
                src = src.broadcast_to([P, rows.stop - rows.start, C])
            sp.dma_start(dst.rearrange("i r d c b t -> (i r d) c (b t)"), src).then_inc(done, 16)

    def keys_sp(self, sp):
        with pairs(sp) as it:
            sp.wait_ge(self.k_out, A_OUT * it + 16)
            sp.wait_ge(self.k_split, 5 * it + 5)
            self.parts_out(sp, 0, it, 0, self.k_out)
        sp.wait_ge(self.k_out, A_OUT * A_CHUNKS + 16)


    def stacks_in(self, sp, b, p):
        for kq, S in enumerate((self.KS, self.QS)):
            for i in range(2):
                src = self.env.st_dram[kq, i, :, :, :, bass.ds(b, 1), :].rearrange("r d c a t -> (d c) r (a t)")
                sp.dma_start(S[64 * i:64 * i + A_ROWS, p, :, :], src).then_inc(self.st_in[p], 16)

    def sp(self, sp):
        sp.wait_ge(self.split, 4)
        self.parts_out(sp, 1, 0, 1, self.q_out)
        sp.wait_ge(self.q_out, A_OUT)
        for p in range(PAIR):
            self.stacks_in(sp, p, p)
        with sp.Fori(0, B // PAIR - 1) as it:
            sp.wait_ge(self.split, 4 * it + 8)
            self.parts_out(sp, 1, it + 1, 1, self.q_out)
            sp.wait_ge(self.q_out, A_OUT * it + 2 * A_OUT)
            for p in range(PAIR):
                b = it * PAIR + PAIR + p
                sp.wait_ge(self.s_up, A_HEADS * (b - 1))
                self.stacks_in(sp, b, p)

    def windows_pool(self, pool):
        flat = self.V[:, :, :, :, :].rearrange("p a c g v -> p (a c g) v")
        pool.memset(flat, 0.0).then_inc(self.y_done, PAIR)
        pool.wait_ge(self.y_done, PAIR)
        slot = flat.rearrange("p n (j v) -> p n j v", j=A_GROUP)
        for n in range(0, PAIR * NT * (A_HEADS // A_GROUP), 4):
            ins = pool.memset(slot[:, n:n + 4, :, 32:32 + A_DH], 1.0)
        ins.then_inc(self.pv_up, PAIR * A_HEADS)
        pool.tensor_copy(self.selb[:, :, :],
                         self.w("sel").unsqueeze(2).broadcast_to([P, A_HEADS, P])).then_inc(self.xb_done, 1)

    def pool(self, pool):
        env, w = self.env, self.w
        with pairs(pool) as it:
            for p in range(PAIR):
                b = it * PAIR + p
                pool.wait_ge(self.pv_up, A_HEADS * b + A_HEADS)
                for c in range(NT):
                    ins = pool.tensor_copy(
                        self.V[:, p, c, :, :].rearrange("p g (j v) -> p g j v", j=A_GROUP)[:, :, :, 0:A_DH],
                        self.vtok[:, bass.ds(b * NT + c, 1), :].rearrange("p a (g j e) -> p (a g) j e", g=A_HEADS // A_GROUP, j=A_GROUP))
                ins.then_inc(self.v_set, 1)
                pool.wait_ge(self.y_done, b + 1)
                pool.tensor_tensor(self.xb[:, p, :, :], env.X[:, bass.ds(b * NT, NT), :],
                                   w("bo").unsqueeze(1).broadcast_to([P, NT, P]), ALU.add).then_inc(self.xb_done, 1)

    MAX_FROM, MAX_EACH = 3, 2
    PROJ, TO, CT, WO, TURN = 1, 1, 5, 10, 14

    def pe(self, pe):
        env, w, PS = self.env, self.w, self.env.ps
        C = B * T // A_CHUNKS
        self.turned.pe(pe)
        pe.wait_ge(self.turned.ready, self.turned.all)
        pe.wait_ge(self.xb_done, 1)

        def place(h):
            return slice(64 * (h // A_STACKS), 64 * (h // A_STACKS) + A_ROWS), h % A_STACKS

        def project(chunk):
            pe.matmul(PS[:, 0, :], w("wq"), env.xT[:, bass.ds(chunk * C, C)], start=True, stop=True).then_inc(self.proj_up, 1)

        def max_unit(b, p, n):
            rows, r = place(self.head(n))
            if not (isinstance(b, int) and b == 0 and n < 2):
                pe.wait_ge(self.mx_done, A_HEADS * b + n - 1)
            for c in range(NT):
                ins = pe.matmul(PS[:, n % 2, c * T:(c + 1) * T], self.QS[rows, p, r, c * P:(c + 1) * P],
                                self.KS[rows, p, r, :], start=True, stop=True)
            ins.then_inc(self.mx_up, 1)

        def turn_max(b, p):
            pe.wait_ge(self.m_step, 6 * b + 7)
            pe.wait_ge(self.y_done, b + 1)
            for c in range(NT):
                ins = pe.transpose(PS[:, 6 + p, :].bitcast(BF16)[:, c * P:(c + 1) * P],
                                   self.msplit[:, p, c, :, :].rearrange("p s h -> p (s h)"), env.identb)
            ins.then_inc(self.mT_up, 1)

        def exp_unit(p, n):
            h = self.head(n)
            rows, r = place(h)
            S = PS[:, 2 + n % 2, :]
            for c in range(NT):
                pe.matmul(S[:, c * T:(c + 1) * T], self.KS[rows, p, r, c * P:(c + 1) * P], self.QS[rows, p, r, :],
                          start=(c == 0), stop=False, skip_group_check=True)
            pe.matmul(S, self.selb[rows, h, :], self.mrow[rows, p, :].unsqueeze(1).broadcast_to([A_ROWS, NT, T]),
                      start=False, stop=True, skip_group_check=True).then_inc(self.s_up, 1)

        def value_unit(b, p, n):
            h = self.head(n)
            g, j = h // A_GROUP, h % A_GROUP
            pe.wait_ge(self.e_done, A_HEADS * b + n + 1)
            for c in range(NT):
                ins = pe.matmul(PS[64 * (g % 2):64 * (g % 2) + 64, 4 + p, (g // 2) * T:(g // 2 + 1) * T],
                                self.V[:, p, c, g, j * A_WINDOW:(j + 1) * A_WINDOW], self.E[:, n % 2, c, :],
                                start=(c == 0 and j == 0 and g < 2), stop=(c == 1 and j == A_GROUP - 1),
                                skip_group_check=True)
            ins.then_inc(self.pv_up, 1)

        def finish(b, p, h):
            if h == self.TO:
                pe.wait_ge(self.o_copy, b + 1)
                for c in range(NT):
                    for g in range(2):
                        ins = pe.transpose(PS[:, 4 + p, (2 * c + g) * P:(2 * c + g + 1) * P],
                                           self.O[:, p, g, c * P:(c + 1) * P], env.ident)
                ins.then_inc(self.ot_up, 1)
            if h == self.CT:
                pe.wait_ge(self.c_step, 2 * b + 2)
                for c in range(NT):
                    ins = pe.transpose(PS[:, 6 + p, c * P:(c + 1) * P], self.ct[:, p, c, :], env.ident)
                ins.then_inc(self.ct_up, 1)
            if h == self.WO:
                pe.wait_ge(self.cT_done, b + 1)
                for c in range(NT):
                    ins = pe.matmul(PS[:, 6 + p, T + c * P:T + (c + 1) * P], self.cT[:, p, c * P:(c + 1) * P], w("wo"),
                                    start=True, stop=True)
                ins.then_inc(self.w_up, 1)

        def element(b, p, first, last):
            q = 1 - p
            if not first:
                pe.wait_ge(self.mT_done, b + 1)
            pe.wait_ge(self.v_set, b + 1)
            exp_unit(p, 0)
            for h in range(A_HEADS):
                if p == 0 and not (isinstance(b, int) and b >= B - PAIR) and h == self.PROJ:
                    pe.wait_ge(self.mx_done, A_HEADS * b + A_HEADS)
                    project(b // PAIR + 1 if isinstance(b, int) else self.pe_it + 1)
                if not last and self.MAX_FROM <= h < self.MAX_FROM + A_HEADS // self.MAX_EACH:
                    if h == self.MAX_FROM:
                        pe.wait_ge(self.st_in[q], self.loads(b, p))
                        pe.wait_ge(self.proj_done, self.projected(b, p))
                    for i in range(self.MAX_EACH):
                        max_unit(b + 1, q, (h - self.MAX_FROM) * self.MAX_EACH + i)
                if h + 1 < A_HEADS:
                    exp_unit(p, h + 1)
                value_unit(b, p, h)
                if not first:
                    finish(b - 1, q, h)
                if not last and h == self.TURN:
                    turn_max(b + 1, q)

        project(0)
        pe.wait_ge(self.proj_done, 1)
        pe.wait_ge(self.st_in[0], 64)
        for h in range(A_HEADS):
            max_unit(0, 0, h)
        turn_max(0, 0)
        pe.wait_ge(self.mT_done, 1)
        self.pe_it = None
        for p in range(PAIR):
            element(p, p, p == 0, False)
        with pe.Fori(1, B // PAIR - 1) as it:
            self.pe_it = it
            for p in range(PAIR):
                element(it * PAIR + p, p, False, False)
        for p in range(PAIR):
            element(B - PAIR + p, p, False, p == PAIR - 1)
        for h in (self.TO, self.CT, self.WO):
            finish(B - 1, 1, h)

    @staticmethod
    def head(n):
        return n % 2 * A_STACKS + n // 2

    def loads(self, b, p):
        it = b // PAIR if isinstance(b, int) else self.pe_it
        return 64 * it + 64 * (p + 1)

    def projected(self, b, p):
        it = b // PAIR if isinstance(b, int) else self.pe_it
        return min(it + 2, A_CHUNKS) if isinstance(it, int) else it + 2

    def act(self, act):
        env, w, PS = self.env, self.w, self.env.ps

        def evacuate():
            act.activation(self.proj[:, :], PS[:, 0, :], ACT.Identity, bias=w("bq")).then_inc(self.proj_done, 1)

        def rows_of_max(b, p):
            act.wait_ge(self.mT_up, b + 1)
            act.activation(self.mrow[:, p, :], PS[:, 6 + p, :].bitcast(BF16)[:, 0:T], ACT.Copy).then_inc(self.mT_done, 1)

        def finish(b, p, h):
            if h == self.CT:
                act.wait_ge(self.ct_up, b + 1)
                act.activation(self.cT[:, p, :], PS[:, 6 + p, 0:T], ACT.Copy).then_inc(self.cT_done, 1)
            if h == self.WO + 1:
                self.tail.root(act, b, p)

        def element(b, p, first, last):
            q = 1 - p
            for h in range(A_HEADS):
                act.wait_ge(self.s_up, A_HEADS * b + h + 1)
                act.wait_ge(self.pv_up, A_HEADS * b + h + PAIR * A_HEADS - 1)
                act.activation(self.E[:, h % 2, :, :], PS[:, 2 + h % 2, :].rearrange("p (c t) -> p c t", c=NT),
                               ACT.Exp, scale=A_DH ** -0.5).then_inc(self.e_done, 1)
                if p == 0 and not (isinstance(b, int) and b >= B - PAIR) and h == self.PROJ + 1:
                    act.wait_ge(self.proj_up, self.projected_by(b))
                    act.wait_ge(self.split, self.split_by(b))
                    evacuate()
                if not first:
                    finish(b - 1, q, h - 1)
                if not last and h == self.TURN + 1:
                    rows_of_max(b + 1, q)
            act.wait_ge(self.pv_up, A_HEADS * b + A_HEADS + PAIR * A_HEADS)
            act.activation(self.O[:, p, :, :], PS[:, 4 + p, :].rearrange("p (g t) -> p g t", g=2),
                           ACT.Copy).then_inc(self.o_copy, 1)

        self.turned.act(act)
        act.preload_act_table_set(EXP_LN)
        act.wait_ge(self.proj_up, 1)
        act.wait_ge(self.k_split, 5 * A_CHUNKS)
        evacuate()
        rows_of_max(0, 0)
        self.act_it = None
        for p in range(PAIR):
            element(p, p, p == 0, False)
        with act.Fori(1, B // PAIR - 1) as it:
            self.act_it = it
            for p in range(PAIR):
                element(it * PAIR + p, p, False, False)
        for p in range(PAIR):
            element(B - PAIR + p, p, False, p == PAIR - 1)
        finish(B - 1, 1, self.CT)
        finish(B - 1, 1, self.WO + 1)

    def projected_by(self, b):
        return (b // PAIR if isinstance(b, int) else self.act_it) + 2

    def split_by(self, b):
        return 4 * (b // PAIR if isinstance(b, int) else self.act_it) + 4

    def dve(self, dve):
        env, w, PS = self.env, self.w, self.env.ps

        def split(chunk):
            x = self.proj[:, :]
            parts = [self.parts[:, 1, i, :] for i in range(3)]
            n = 0

            def link(ins):
                nonlocal n
                n += 1
                ins.then_inc(self.split, 1)
                dve.wait_ge(self.split, 4 * chunk + n)

            dve.wait_ge(self.proj_done, chunk + 1)
            if not isinstance(chunk, int) or chunk > 0:
                dve.wait_ge(self.q_out, A_OUT * chunk)
            split3(dve, link, parts, x, x)

        def maxima(b, p, heads):
            mx = self.mx[:, p, 0, :].rearrange("p (c h) -> p c h", c=NT)
            for h in heads:
                dve.wait_ge(self.mx_up, A_HEADS * b + h + 1)
                dve.tensor_reduce(mx[:, :, self.head(h)], PS[:, h % 2, :].rearrange("p (c k) -> p c k", c=NT), AX.X,
                                  ALU.max).then_inc(self.mx_done, 1)

        def split_max(b, p):
            def step(ins, k):
                ins.then_inc(self.m_step, 1)
                dve.wait_ge(self.m_step, 6 * b + k + 1)

            dve.wait_ge(self.mx_done, A_HEADS * b + A_HEADS)
            step(dve.tensor_scalar(self.mx[:, p, 1, :], self.mx[:, p, 0, :], -1.0, None, ALU.mult), 1)
            tiles = lambda i: self.mx[:, p, i, :].rearrange("p (c h) -> p c h", c=NT)
            parts = [self.msplit[:, p, :, i, :] for i in range(3)]
            step(dve.tensor_copy(parts[0], tiles(1)), 2)
            step(dve.tensor_tensor(tiles(2), tiles(1), parts[0], ALU.subtract), 3)
            step(dve.tensor_copy(parts[1], tiles(2)), 4)
            step(dve.tensor_tensor(parts[2], tiles(2), parts[1], ALU.subtract), 5)
            step(dve.tensor_copy(self.msplit[:, p, :, 4:7, :], self.msplit[:, p, :, 0:3, :]), 6)

        def divide(b, p):
            dve.wait_ge(self.ot_up, b + 1)
            O = PS[:, 4 + p, :].rearrange("p (n v) -> p n v", v=A_WINDOW)
            dve.reciprocal(self.rec[:, p, :, :], O[:, :, 32:64:A_DH]).then_inc(self.c_step, 1)
            dve.wait_ge(self.c_step, 2 * b + 1)
            dve.tensor_tensor(
                self.ct[:, p, :, :].rearrange("p c (g j e) -> p (c g) j e", j=A_GROUP, e=A_DH),
                O[:, :, 0:32].rearrange("p n (j e) -> p n j e", j=A_GROUP),
                self.rec[:, p, :, :].unsqueeze(3).broadcast_to([P, 8, A_GROUP, A_DH]), ALU.mult).then_inc(self.c_step, 1)

        def add(b, p):
            dve.wait_ge(self.w_up, b + 1)
            dve.wait_ge(self.xb_done, b + 2)
            dve.tensor_tensor(self.y[:, p, :, :], self.xb[:, p, :, :],
                              PS[:, 6 + p, T:2 * T].rearrange("p (k c) -> p k c", k=NT), ALU.add).then_inc(self.y_done, 1)
            dve.wait_ge(self.y_done, b + 1 + PAIR)
            self.tail.moments(dve, self.y[:, p, :, :], b, p)

        def norm(b, p):
            self.tail.apply(dve, lambda k: env.x_tile(b * NT + k), self.y[:, p, :, :], b, p, env.x_done[self.index])

        def element(b, p, first, last):
            q = 1 - p
            half = A_HEADS // 2
            if not first:
                divide(b - 1, q)
            if not last:
                maxima(b + 1, q, range(A_HEADS))
                split_max(b + 1, q)
            if not first:
                add(b - 1, q)
            if p == 0 and not (isinstance(b, int) and b >= B - PAIR):
                split((b // PAIR if isinstance(b, int) else self.dve_it) + 1)
            if not first:
                norm(b - 1, q)

        split(0)
        maxima(0, 0, range(A_HEADS))
        split_max(0, 0)
        self.dve_it = None
        for p in range(PAIR):
            element(p, p, p == 0, False)
        with dve.Fori(1, B // PAIR - 1) as it:
            self.dve_it = it
            for p in range(PAIR):
                element(it * PAIR + p, p, False, False)
        for p in range(PAIR):
            element(B - PAIR + p, p, False, p == PAIR - 1)
        divide(B - 1, 1)
        add(B - 1, 1)
        norm(B - 1, 1)


E_EXP, E_HID = 8, 256
E_BANKS = 4
E_HALVES = E_HID // P


class Experts(Sublayer):
    def __init__(self, env, w, index):
        self.env, self.w, self.index = env, w, index
        sb, sem = env.sb, env.sem
        self.turned = Turned(env, index)
        self.lg = sb("e_lg", [P, TILES, E_EXP])
        self.top = sb("e_top", [P, TILES, E_EXP])
        self.topi = sb("e_topi", [P, TILES, E_EXP], U32)
        self.topf = sb("e_topf", [P, TILES, 2])
        self.col = sb("e_col", [P, 6, TILES])
        self.oh = sb("e_oh", [P, 2, TILES, E_EXP])
        self.gate = sb("e_gate", [P, TILES, E_EXP])
        self.gT = sb("e_gT", [E_EXP, TILES * P])
        self.h = sb("e_h", [P, 4, E_HALVES, T])
        self.acc = sb("e_acc", [P, TILES, P])
        self.inner = LayerNormTail(env, "e_in", None)
        self.z = sb("e_z", [P, PAIR, NT, P])
        self.tail = LayerNormTail(env, "e_ln", index)
        self.lg_up = sem("e_lg_up")
        self.g_step = sem("e_g_step")
        self.g_exp = sem("e_g_exp")
        self.g_turned = sem("e_g_turned")
        self.g_rows = sem("e_g_rows")
        self.h_up = sem("e_h_up")
        self.h_act = sem("e_h_act")
        self.o_up = sem("e_o_up")
        self.mixed = sem("e_mixed")
        self.z_done = sem("e_z_done")

    G_STEPS = 11

    def pool(self, pool):
        env, w = self.env, self.w
        pool.memset(self.z[:, :, :, :], 0.0).then_inc(self.o_up, PAIR * E_EXP)
        with pairs(pool) as it:
            for p in range(PAIR):
                self.inner.root_pool(pool, it * PAIR + p, p)
                self.tail.root_pool(pool, it * PAIR + p, p)

    def pe(self, pe):
        env, w, PS = self.env, self.w, self.env.ps
        self.turned.pe(pe)
        pe.wait_ge(self.turned.ready, self.turned.all)
        for t in range(TILES):
            ins = pe.matmul(PS[:, 4, t * E_EXP:(t + 1) * E_EXP], env.xT[:, t * P:(t + 1) * P], w("Wg"),
                            start=True, stop=True)
        ins.then_inc(self.lg_up, 1)
        pe.wait_ge(self.g_step, self.G_STEPS)
        for t in range(TILES):
            ins = pe.transpose(PS[0:E_EXP, t // 4, t % 4 * P:(t % 4 + 1) * P], self.gate[:, t, :], env.ident)
        ins.then_inc(self.g_turned, 1)
        pe.wait_ge(self.g_rows, 1)
        for t in range(TILES):
            ins = pe.matmul(PS[:, 4 + t // 4, t % 4 * P:(t % 4 + 1) * P], self.gT[:, t * P:(t + 1) * P], w("b2")[0:E_EXP],
                            start=True, stop=True)
        ins.then_inc(self.g_turned, 1)

        def hidden(b, e):
            b, e = (b, e) if e < E_EXP else (b + 1, e - E_EXP)
            if not (isinstance(b, int) and b == 0 and e < 2):
                pe.wait_ge(self.h_act, E_EXP * b + e - 1)
            x = env.xT[:, bass.ds(b * T, T)]
            for j in range(E_HALVES):
                c = (e * E_HALVES + j) * P
                ins = pe.matmul(PS[:, e % 2, j * T:(j + 1) * T], w("W1")[:, c:c + P], x, start=True, stop=True)
            ins.then_inc(self.h_up, 1)

        def result(b, e):
            pe.wait_ge(self.h_act, E_EXP * b + e + 1)
            pe.wait_ge(self.mixed, E_EXP * b + e + 1)
            for k in range(NT):
                for j in range(E_HALVES):
                    c = (e * E_HALVES + j) * P
                    ins = pe.matmul(PS[:, 2 + e % E_BANKS, k * P:(k + 1) * P], self.h[:, e % 4, j, k * P:(k + 1) * P],
                                    w("W2")[:, c:c + P], start=(j == 0), stop=(j == E_HALVES - 1))
            ins.then_inc(self.o_up, 1)

        def element(b, p, first, last):
            for e in range(E_EXP):
                if not (last and e >= E_EXP - 2):
                    hidden(b, e + 2)
                result(b, e)

        hidden(0, 0)
        hidden(0, 1)
        elements(pe, element)

    def act(self, act):
        env, w, PS = self.env, self.w, self.env.ps
        self.turned.act(act)
        act.preload_act_table_set(EXP_LN)
        act.wait_ge(self.g_step, 3)
        act.activation(self.col[:, 1, :], self.col[:, 0, :], ACT.Exp).then_inc(self.g_exp, 1)
        act.wait_ge(self.g_turned, 1)
        for n in range(4):
            ins = act.activation(self.gT[:, n * 4 * P:(n + 1) * 4 * P], PS[0:E_EXP, n, :], ACT.Copy)
        ins.then_inc(self.g_rows, 1)
        with pairs(act) as it:
            for n in range(PAIR * E_EXP):
                e = n % E_EXP
                act.wait_ge(self.h_up, it * (PAIR * E_EXP) + n + 1)
                act.wait_ge(self.o_up, it * (PAIR * E_EXP) + PAIR * E_EXP + n - 3)
                for j in range(E_HALVES):
                    c = e * E_HALVES + j
                    ins = act.activation(self.h[:, n % 4, j, :], PS[:, n % 2, j * T:(j + 1) * T], ACT.Relu,
                                         bias=w("b1")[:, c:c + 1])
                ins.then_inc(self.h_act, 1)

    def dve(self, dve):
        env, w, PS = self.env, self.w, self.env.ps
        def step(ins, k):
            ins.then_inc(self.g_step, 1)
            dve.wait_ge(self.g_step, k)

        bc = lambda a: a.unsqueeze(2).broadcast_to([P, TILES, E_EXP])
        col = lambda i: self.col[:, i, :]
        dve.wait_ge(self.lg_up, 1)
        step(dve.tensor_tensor(self.lg[:, :, :], PS[:, 4, 0:TILES * E_EXP].rearrange("p (t e) -> p t e", t=TILES),
                               w("bg").unsqueeze(1).broadcast_to([P, TILES, E_EXP]), ALU.add), 1)
        for t in range(TILES):
            ins = dve.max(self.top[:, t, :], self.lg[:, t, :])
        step(ins, 2)
        step(dve.tensor_tensor(col(0), self.top[:, :, 1], self.top[:, :, 0], ALU.subtract), 3)
        for t in range(TILES):
            ins = dve.max_index(self.topi[:, t, :], self.top[:, t, :], self.lg[:, t, :])
        step(ins, 4)
        step(dve.tensor_copy(self.topf[:, :, :], self.topi[:, :, 0:2]), 5)
        for i in range(2):
            ins = dve.tensor_tensor(self.oh[:, i, :, :], w("iota").unsqueeze(1).broadcast_to([P, TILES, E_EXP]),
                                    bc(self.topf[:, :, i]), ALU.is_equal)
        step(ins, 6)
        dve.wait_ge(self.g_exp, 1)
        step(dve.tensor_scalar(col(2), col(1), 1.0, None, ALU.add), 7)
        step(dve.reciprocal(col(3), col(2)), 8)
        dve.tensor_tensor(self.oh[:, 0, :, :], self.oh[:, 0, :, :], bc(col(3)), ALU.mult)
        step(dve.tensor_tensor(col(4), col(1), col(3), ALU.mult), 9)
        step(dve.tensor_tensor(self.oh[:, 1, :, :], self.oh[:, 1, :, :], bc(col(4)), ALU.mult), 10)
        step(dve.tensor_tensor(self.gate[:, :, :], self.oh[:, 1, :, :], self.oh[:, 0, :, :], ALU.add), 11)
        dve.wait_ge(self.g_turned, 2)
        for n in range(4):
            ins = dve.tensor_tensor(self.acc[:, 4 * n:4 * n + 4, :], env.X[:, 4 * n:4 * n + 4, :],
                                    PS[:, 4 + n, :].rearrange("p (k c) -> p k c", k=4), ALU.add)
        ins.then_inc(self.mixed, E_BANKS)

        def finish(b, p, step):
            z = self.z[:, p, :, :]
            row = lambda name: w(name).unsqueeze(1).broadcast_to([P, NT, P])
            acc = lambda: self.acc[:, bass.ds(b * NT, NT), :]
            if step == 0:
                dve.wait_ge(self.mixed, E_EXP * b + E_EXP + E_BANKS)
                self.inner.moments(dve, acc(), b, p)
            elif step == 1:
                self.inner.apply(dve, lambda k: z[:, k, :], acc(), b, p, self.z_done)
                dve.wait_ge(self.z_done, 4 * b + 1)
                dve.tensor_tensor(z, z, row("gamma"), ALU.mult).then_inc(self.z_done, 1)
                dve.wait_ge(self.z_done, 4 * b + 2)
                dve.tensor_tensor(z, z, row("beta"), ALU.add).then_inc(self.z_done, 1)
                dve.wait_ge(self.z_done, 4 * b + 3)
                dve.tensor_tensor(z, z, env.X[:, bass.ds(b * NT, NT), :], ALU.add).then_inc(self.z_done, 1)
                dve.wait_ge(self.z_done, 4 * b + 4)
                self.tail.moments(dve, z, b, p)
            else:
                self.tail.apply(dve, lambda k: env.x_tile(b * NT + k), z, b, p, env.x_done[self.index])

        def element(b, p, first, last):
            for e in range(E_EXP):
                acc = self.acc[:, bass.ds(b * NT, NT), :]
                gate = self.gate[:, bass.ds(b * NT, NT), :]
                dve.wait_ge(self.o_up, E_EXP * b + PAIR * E_EXP + e + 1)
                dve.wait_ge(self.mixed, E_EXP * b + E_BANKS + e)
                for k in range(NT):
                    ins = dve.scalar_tensor_tensor(out=acc[:, k, :], in0=PS[:, 2 + e % E_BANKS, k * P:(k + 1) * P],
                                                   scalar=gate[:, k, e:e + 1], in1=acc[:, k, :],
                                                   op0=ALU.mult, op1=ALU.add)
                ins.then_inc(self.mixed, 1)
                if not first and e in (1, 3, 5):
                    finish(b - 1, 1 - p, e // 2)

        elements(dve, element)
        for step in range(3):
            finish(B - 1, 1, step)


SUBLAYERS = [Mamba, MLstm, Ffn, Retention, CrossAttention, Experts]


def program(nc, d, layouts, out):
    with ExitStack() as ctx:
        env = Env(nc, ctx)
        env.ps = ctx.enter_context(nc.psum_tensor("ps", [P, 8, 512], F32))
        env.X = env.sb("X", [P, TILES, P])
        env.xT = env.sb("xT", [P, B * T])
        env.ctxT = env.sb("ctxT", [P, B * T])
        env.ctok = env.sb("ctok", [P, TILES, P])
        env.m_dram = nc.dram_tensor("m_parts", (3, B, X_HEADS, T), BF16, kind="Internal").ap()
        env.st_dram = nc.dram_tensor("a_stacks", (2, 2, A_STACKS, A_DH, len(A_Q_PARTS), B, T), BF16, kind="Internal").ap()
        env.identb = env.sb("identb", [P, P], BF16)[:, :]
        w0, env.w0 = env.weights("w0", layouts["w0"])
        env.ident = env.w0("ident")[:, 0:P]
        env.ones_row = env.w0("ones")
        env.x_done = [env.sem(f"x_done{n}") for n in range(6)]
        env.w_in = [env.sem(f"w{n}_in") for n in range(7)]
        env.w1_in, env.w2_in = env.w_in[1], env.w_in[2]
        env.xT_in, env.x_in, env.ctx_in, stored = (env.sem(n) for n in ("xT_in", "x_in", "ctx_in", "stored"))
        env.ln_measured, env.ln_rooted = env.sem("ln_measured"), env.sem("ln_rooted")
        env.turned_up, env.turned_ready = env.sem("turned_up"), env.sem("turned_ready")
        arenas = [ctx.enter_context(nc.sbuf_tensor(f"arena{n}", [P, ARENA_WORDS[n]], F32)) for n in range(2)]
        layers, packed = [], []
        for n, kind in enumerate(SUBLAYERS):
            env.begin(arenas[n % 2][:, :])
            buf, w = env.weights(f"w{n + 1}", layouts[f"w{n + 1}"])
            packed.append((n, buf))
            layers.append(kind(env, w, n))
        for layer in layers:
            if isinstance(layer, Retention):
                layer.guest = layers[-1 if len(layers) < 3 else -2]
        env.arena = None
        block = ctx.enter_context(nc.Block())

        @block.sync
        def _(sp):
            sp.dma_start(packed[0][1], d[f"w{packed[0][0] + 1}"]).then_inc(env.w_in[packed[0][0] + 1], 16)
            sp.dma_start(w0[:, :], d["w0"]).then_inc(env.w_in[0], 16)
            sp.dma_start(env.xT[:, :], d["xT"]).then_inc(env.xT_in, 16)
            sp.dma_start(env.X[:, :, :], d["x"].rearrange("(t p) c -> p t c", p=P)).then_inc(env.x_in, 16)
            sp.dma_start(env.ctxT[:, :], d["ctxT"]).then_inc(env.ctx_in, 16)
            sp.dma_start(env.ctok[:, :, :], d["ctx"].rearrange("(t p) c -> p t c", p=P)).then_inc(env.ctx_in, 16)
            for m, layer in enumerate(layers):
                if m + 1 < len(layers):
                    n, buf = packed[m + 1]
                    if n >= 2:
                        sp.wait_ge(env.x_done[n - 2], B)
                    sp.dma_start(buf, d[f"w{n + 1}"]).then_inc(env.w_in[n + 1], 16)
                layer.sp(sp)
            sp.wait_ge(env.x_done[layers[-1].index], B)
            sp.dma_start(out.rearrange("(t p) c -> p t c", p=P), env.X[:, :, :]).then_inc(stored, 16)
            sp.wait_ge(stored, 16)

        @block.gpsimd
        def _(pool):
            for layer in layers:
                layer.begin(pool)
                layer.pool(pool)

        @block.tensor
        def _(pe):
            for layer in layers:
                layer.begin(pe)
                layer.pe(pe)

        @block.scalar
        def _(act):
            for layer in layers:
                layer.begin(act)
                layer.act(act)

        @block.vector
        def _(dve):
            for layer in layers:
                layer.begin(dve)
                layer.dve(dve)


def pack(parts):
    import numpy as np
    at, places, cols = 0, {}, []
    for name, a in parts:
        a = np.asarray(a, np.float32)
        a = a.reshape(a.shape[0], -1)
        full = np.zeros((P, a.shape[1]), np.float32)
        full[:a.shape[0]] = a
        places[name] = (at, at + a.shape[1])
        at += a.shape[1]
        cols.append(full)
    places["_size"] = at
    return np.ascontiguousarray(np.concatenate(cols, axis=1)), places


def lay_out(i):
    import numpy as np
    eye = np.eye(P, dtype=np.float32)
    rows = lambda a: np.tile(np.asarray(a).reshape(1, -1), (P, 1))
    cols = lambda a, n=P: np.ascontiguousarray(np.asarray(a).reshape(-1, n).T)
    tiles = lambda a: np.asarray(a).reshape(-1, P, a.shape[-1]).transpose(1, 0, 2)
    sel = np.zeros((M_SPLIT, M_HEADS, M_HEADS, P), np.float32)
    for h in range(M_HEADS):
        sel[:, h, h, :] = 1.0
    w0, l0 = pack([("ident", np.concatenate([eye, 0 * eye], 1)), ("ones", np.ones((P, T))),
                   ("eps", np.full((P, NT), LN_EPS)), ("minus_half", np.full((P, NT), -0.5))])
    w1, l1 = pack([
        ("W_in", i["L0_attn_W_in"]), 
        ("conv_w", tiles(i["L0_attn_conv_w"])), ("conv_b", cols(i["L0_attn_conv_b"])),
        ("dt_bias", rows(i["L0_attn_dt_bias"])), ("A_log", rows(i["L0_attn_A_log"])),
        ("D", cols(np.repeat(i["L0_attn_D"], M_HEAD))), ("norm_w", cols(i["L0_attn_norm_w"])),
        ("W_out", tiles(i["L0_attn_W_out"])), ("sel_decay", sel.reshape(M_SPLIT * M_HEADS, -1)),
    ])
    head = np.arange(P) // X_DH

    def windowed(a):
        z = np.zeros((P, 2, (B - 1) * X_HEADS), np.float32)
        return np.concatenate([z, a.T.reshape(P, 2, X_HEADS), z], 2)

    gw = i["L0_xattn_ifgate_w"]
    w2, l2 = pack([
        ("gate_q", windowed(gw[:, 0:P])), ("gate_k", windowed(gw[:, P:2 * P])), ("gate_v", windowed(gw[:, 2 * P:])),
        ("gate_b", np.tile(i["L0_xattn_ifgate_b"].reshape(2, 1, X_HEADS), (1, B, 1)).reshape(P, 1)),
        ("sel", np.tile(np.eye(X_HEADS), (3, 1))), ("future", np.tril(np.full((P, P), -30000.0), -1)),
        ("head_par", np.stack([(head % 2 == n) * X_DH ** -0.5 for n in range(2)], 1)),
        ("same_head", np.repeat(head[:, None] == np.arange(X_HEADS)[None, :], X_SLOT, 1) * X_DH ** -0.5),
        ("outnorm", rows(i["L0_xattn_outnorm_w"])),
    ])
    w3, l3 = pack([
        ("W1", i["L0_ffn_W1"].T), ("W2", i["L0_ffn_W2"].reshape(P, F_BLOCKS, P).transpose(2, 1, 0)),
        ("b1", cols(i["L0_ffn_b1"])), ("b2", rows(i["L0_ffn_b2"])), ("scale", rows(i["L0_ffn_scale"])),
        ("blk", np.eye(F_PAIRS)),
    ])
    gam = np.float32(1) - np.exp(np.linspace(np.log(1 / 32), np.log(1 / 512), R_HEADS, dtype=np.float32))
    lg = np.repeat(np.log(gam.astype(np.float64)), R_DH)
    tt = np.arange(P)
    comp = 2.0 ** (R_NORM_SHIFT // 2)
    rhead = np.arange(P) // R_DH
    same = (rhead[:, None] == rhead[None, :])
    w4, l4 = pack([
        ("qw", i["L1_attn_qw"].T), ("kw", i["L1_attn_kw"].T), ("vw", i["L1_attn_vw"].T), ("ow", i["L1_attn_ow"].T),
        ("w1", i["L1_attn_w1"].T), ("w2", i["L1_attn_w2"].T.reshape(2, P, P).transpose(1, 0, 2)),
        ("b1", cols(i["L1_attn_b1"])), ("ob", rows(i["L1_attn_ob"])), ("b2", rows(i["L1_attn_b2"])),
        ("norm_g", cols(i["L1_attn_norm_g"])), ("norm_b", cols(i["L1_attn_norm_b"])),
        ("fnorm_g", cols(i["L1_attn_ffn_norm_g"])), ("fnorm_b", cols(i["L1_attn_ffn_norm_b"])),
        ("group", same / R_DH),
        ("head_of", rhead[:, None] % R_GROUP == np.arange(R_GROUP)[None, :]),
        ("v_decay", comp * np.exp(-lg[None, :] * tt[:, None])),
        ("same_head", same * np.exp(P * lg)[None, :]),
        ("y_decay", np.tile(R_DH ** -0.5 * comp * np.exp(lg[:, None] * tt[None, :]), (1, NT))),
        ("causal", np.triu(np.ones((P, P)))),
    ])
    w5, l5 = pack([
        ("wq", i["L1_xattn_wq"].T), ("wk", i["L1_xattn_wk"].T), ("wv", i["L1_xattn_wv"].T), ("wo", i["L1_xattn_wo"].T),
        ("bq", cols(i["L1_xattn_bq"])), ("bk", cols(i["L1_xattn_bk"])), ("bv", rows(i["L1_xattn_bv"])),
        ("bo", rows(i["L1_xattn_bo"])), ("sel", np.tile(np.eye(A_HEADS), (P // A_HEADS, 1))),
    ])
    w6, l6 = pack([
        ("Wg", i["L1_ffn_Wg"]), ("bg", rows(i["L1_ffn_bg"])), ("W1", i["L1_ffn_W1"].transpose(1, 0, 2)),
        ("b1", cols(i["L1_ffn_b1"])), ("W2", i["L1_ffn_W2"].reshape(E_EXP * E_HALVES, P, P).transpose(1, 0, 2)),
        ("b2", i["L1_ffn_b2"]), ("gamma", rows(i["L1_ffn_gamma"])), ("beta", rows(i["L1_ffn_beta"])),
        ("iota", rows(np.arange(E_EXP))),
    ])
    x, ctx = i["x"].reshape(B * T, P), i["ctx_1024"].reshape(B * T, P)
    return ({"w0": w0, "w1": w1, "w2": w2, "w3": w3, "w4": w4, "w5": w5, "w6": w6, "xT": np.ascontiguousarray(x.T), "x": x, "ctxT": np.ascontiguousarray(ctx.T), "ctx": ctx},
            {"w0": l0, "w1": l1, "w2": l2, "w3": l3, "w4": l4, "w5": l5, "w6": l6})


def kernel(**inputs):
    import numpy as np
    import concourse.bacc as bacc
    from concourse.bass_utils import run_bass_kernel_spmd

    nc = bacc.Bacc("TRN2", target_bir_lowering=False, num_devices=1)
    arrays, layouts = lay_out({k: np.asarray(v) for k, v in inputs.items()})
    arrays = {f"in_{k}": np.ascontiguousarray(a) for k, a in arrays.items()}
    d = {k[3:]: nc.dram_tensor(k, a.shape, mybir.dt.from_np(a.dtype), kind="ExternalInput").ap()
         for k, a in arrays.items()}
    out = nc.dram_tensor("out", (B * T, P), F32, kind="ExternalOutput").ap()
    program(nc, d, layouts, out)
    r = run_bass_kernel_spmd(nc, [arrays], core_ids=[0])
    return r.results[0]["out"].reshape(B, T, P)
```
